# Optimizing a Trainium2 kernel written in Bass

```python
import numpy as np
import jax
import jax.numpy as jnp

def _softmax(x, axis=-1):
    return jax.nn.softmax(x, axis=axis)

def _gelu(x):
    return jax.nn.gelu(x, approximate=True)

def _silu(x):
    return jax.nn.silu(x)

def _sigmoid(x):
    return jax.nn.sigmoid(x)

def _layernorm(x, axis=-1, eps=1e-05):
    m = jnp.mean(x, axis=axis, keepdims=True)
    v = jnp.var(x, axis=axis, keepdims=True)
    return (x - m) / jnp.sqrt(v + eps)

def _scatter_add(tgt, idx, src, axis=0):
    return tgt.at[idx].add(src)

def _segment_sum(src, seg, n):
    return jax.ops.segment_sum(src, seg, n)
kernel_name = 'mk_flamingo_gated_d2_seqx_r8_1baee3'

def setup_inputs(seed: int=0):
    np.random.seed(seed)
    _w = jnp.asarray

    def _rec_inputs():
        import jax
        import jax.numpy as jnp
        _rk = jax.random.key(seed)
        x = -0.0002928 + 1 * jax.random.normal(jax.random.fold_in(_rk, 1), (32, 64, 128), jnp.float32)
        _lenS = 64 - jax.random.randint(jax.random.fold_in(_rk, 7), (32,), 0, max(1, 64 // 4) + 1, jnp.int32)
        _lenS2 = 64 - jax.random.randint(jax.random.fold_in(_rk, 8), (32,), 0, max(1, 64 // 4) + 1, jnp.int32)
        _ctx_1024P = jax.random.normal(jax.random.fold_in(_rk, 11), (32, 16, 128), jnp.float32)
        _ctx_1024c = jax.random.dirichlet(jax.random.fold_in(_rk, 511), 0.3 * jnp.ones((16,), jnp.float32), (32, 64))
        _ctx_1024t = jnp.einsum('bsk,bkd->bsd', _ctx_1024c, _ctx_1024P)
        _ctx_1024t = _ctx_1024t * jax.lax.rsqrt(jnp.mean(jnp.square(_ctx_1024t)) + 1e-12) * 0.953939
        ctx_1024 = -1.39393e-06 + 0.999914 * (_ctx_1024t + 0.3 * jax.random.normal(jax.random.fold_in(_rk, 611), (32, 64, 128), jnp.float32))
        _g = jax.random.normal(jax.random.fold_in(_rk, 9001), (2, 2), jnp.float32)
        _g = jnp.sign(_g) * jnp.maximum(jnp.abs(_g), 1.0) + (_g == 0) * 1.0
        g_xattn = _g[0]
        g_ffn = _g[1]
        return (x, ctx_1024, g_xattn, g_ffn)
    x, ctx_1024, g_xattn, g_ffn = _rec_inputs()

    def _L0_xattn_setup():
        import jax, jax.numpy as jnp
        import numpy as np
        D_MODEL = 128
        NUM_HEADS = 16
        key = jax.random.key(seed)
        ks = jax.random.split(key, 12)
        B, S, D = (2, 256, D_MODEL)
        s = 1.0 / np.sqrt(D)
        return {'q': jax.random.normal(ks[0], (B, S, D), jnp.float32), 'k': jax.random.normal(ks[1], (B, S, D), jnp.float32), 'v': jax.random.normal(ks[2], (B, S, D), jnp.float32), 'wq': jax.random.normal(ks[3], (D, D), jnp.float32) * s, 'bq': jnp.zeros((D,), jnp.float32), 'wk': jax.random.normal(ks[4], (D, D), jnp.float32) * s, 'bk': jnp.zeros((D,), jnp.float32), 'wv': jax.random.normal(ks[5], (D, D), jnp.float32) * s, 'bv': jnp.zeros((D,), jnp.float32), 'wo': jax.random.normal(ks[6], (D, D), jnp.float32) * s, 'bo': jnp.zeros((D,), jnp.float32)}
    _L0_xattn_all = _L0_xattn_setup()
    _L0_xattn_in = {k: v for k, v in _L0_xattn_all.items() if k in ('wq', 'bq', 'wk', 'bk', 'wv', 'bv', 'wo', 'bo')}
    del _L0_xattn_all

    def _L0_ffn_setup():
        import jax, jax.numpy as jnp
        import numpy as np
        D_MODEL = 128
        H_SHARED = 256
        H_ROUTED = 128
        N_EXPERTS = 8
        TOP_K = 2
        key = jax.random.key(seed)
        ks = jax.random.split(key, 8)
        B, T = (2, 256)
        sc_d = 1.0 / np.sqrt(D_MODEL)
        sc_hs = 1.0 / np.sqrt(H_SHARED)
        sc_hr = 1.0 / np.sqrt(H_ROUTED)
        return {'x': jax.random.normal(ks[0], (B, T, D_MODEL), dtype=jnp.float32), 'router_w': jax.random.normal(ks[1], (N_EXPERTS, D_MODEL), dtype=jnp.float32) * sc_d, 'router_bias': jnp.zeros((N_EXPERTS,), dtype=jnp.float32), 'sw1': jax.random.normal(ks[2], (D_MODEL, H_SHARED), dtype=jnp.float32) * sc_d, 'sw3': jax.random.normal(ks[3], (D_MODEL, H_SHARED), dtype=jnp.float32) * sc_d, 'sw2': jax.random.normal(ks[4], (H_SHARED, D_MODEL), dtype=jnp.float32) * sc_hs, 'ew1': jax.random.normal(ks[5], (N_EXPERTS, D_MODEL, H_ROUTED), dtype=jnp.float32) * sc_d, 'ew2': jax.random.normal(ks[6], (N_EXPERTS, H_ROUTED, D_MODEL), dtype=jnp.float32) * sc_hr}
    _L0_ffn_all = _L0_ffn_setup()
    _L0_ffn_in = {k: v for k, v in _L0_ffn_all.items() if k in ('router_w', 'router_bias', 'sw1', 'sw3', 'sw2', 'ew1', 'ew2')}
    del _L0_ffn_all

    def _L1_xattn_setup():
        import jax, jax.numpy as jnp
        import numpy as np
        B, S, E, NH = (1, 256, 128, 8)
        DH = E // NH
        EPS_BACKEND = 1e-06
        EPS_NORM = 1e-05
        key = jax.random.key(seed)
        ks = jax.random.split(key, 8)
        q = jax.random.normal(ks[0], (B, S, E), jnp.float32)
        k = jax.random.normal(ks[1], (B, S, E), jnp.float32)
        v = jax.random.normal(ks[2], (B, S, E), jnp.float32)
        igate_w = jax.random.normal(ks[3], (NH, 3 * E), jnp.float32) * 0.02
        igate_b = jax.random.normal(ks[4], (NH,), jnp.float32) * 0.1
        fgate_w = jax.random.normal(ks[5], (NH, 3 * E), jnp.float32) * 0.02
        fgate_b = jnp.linspace(3.0, 6.0, NH).astype(jnp.float32)
        norm_w = 1.0 + 0.1 * jax.random.normal(ks[6], (E,), jnp.float32)
        return dict(q=q, k=k, v=v, igate_w=igate_w, igate_b=igate_b, fgate_w=fgate_w, fgate_b=fgate_b, norm_w=norm_w)
    _L1_xattn_all = _L1_xattn_setup()
    _L1_xattn_in = {k: v for k, v in _L1_xattn_all.items() if k in ('igate_w', 'igate_b', 'fgate_w', 'fgate_b', 'norm_w')}
    del _L1_xattn_all

    def _L1_ffn_setup():
        import jax, jax.numpy as jnp
        import numpy as np
        from jax import lax
        T, B, I, M, O = (32, 64, 128, 128, 128)

        def _xavier(key, shape):
            fan_out, fan_in = shape
            limit = float(np.sqrt(6.0 / (fan_in + fan_out)))
            return jax.random.uniform(key, shape, jnp.float32, -limit, limit)
        key = jax.random.key(seed)
        ks = jax.random.split(key, 9)
        x = jax.random.normal(ks[0], (T, B, I), jnp.float32)
        return {'x': x, 'wf': _xavier(ks[1], (M, I)), 'uf': _xavier(ks[2], (M, M)), 'bf': jnp.zeros((M,), jnp.float32), 'wi': _xavier(ks[3], (M, I)), 'ui': _xavier(ks[4], (M, M)), 'bi': jnp.zeros((M,), jnp.float32), 'wc': _xavier(ks[5], (M, I)), 'uc': _xavier(ks[6], (M, M)), 'bc': jnp.zeros((M,), jnp.float32), 'wo': _xavier(ks[7], (O, I)), 'uo': _xavier(ks[8], (O, M)), 'bo': jnp.zeros((O,), jnp.float32), 'in_c': jnp.zeros((M,), jnp.float32)}
    _L1_ffn_all = _L1_ffn_setup()
    _L1_ffn_in = {k: v for k, v in _L1_ffn_all.items() if k in ('wf', 'uf', 'bf', 'wi', 'ui', 'bi', 'wc', 'uc', 'bc', 'wo', 'uo', 'bo', 'in_c')}
    del _L1_ffn_all
    return {'x': x, 'ctx_1024': ctx_1024, 'g_xattn': g_xattn, 'g_ffn': g_ffn, 'L0_xattn_wq': _L0_xattn_in['wq'], 'L0_xattn_bq': _L0_xattn_in['bq'], 'L0_xattn_wk': _L0_xattn_in['wk'], 'L0_xattn_bk': _L0_xattn_in['bk'], 'L0_xattn_wv': _L0_xattn_in['wv'], 'L0_xattn_bv': _L0_xattn_in['bv'], 'L0_xattn_wo': _L0_xattn_in['wo'], 'L0_xattn_bo': _L0_xattn_in['bo'], 'L0_ffn_router_w': _L0_ffn_in['router_w'], 'L0_ffn_router_bias': _L0_ffn_in['router_bias'], 'L0_ffn_sw1': _L0_ffn_in['sw1'], 'L0_ffn_sw3': _L0_ffn_in['sw3'], 'L0_ffn_sw2': _L0_ffn_in['sw2'], 'L0_ffn_ew1': _L0_ffn_in['ew1'], 'L0_ffn_ew2': _L0_ffn_in['ew2'], 'L1_xattn_igate_w': _L1_xattn_in['igate_w'], 'L1_xattn_igate_b': _L1_xattn_in['igate_b'], 'L1_xattn_fgate_w': _L1_xattn_in['fgate_w'], 'L1_xattn_fgate_b': _L1_xattn_in['fgate_b'], 'L1_xattn_norm_w': _L1_xattn_in['norm_w'], 'L1_ffn_wf': _L1_ffn_in['wf'], 'L1_ffn_uf': _L1_ffn_in['uf'], 'L1_ffn_bf': _L1_ffn_in['bf'], 'L1_ffn_wi': _L1_ffn_in['wi'], 'L1_ffn_ui': _L1_ffn_in['ui'], 'L1_ffn_bi': _L1_ffn_in['bi'], 'L1_ffn_wc': _L1_ffn_in['wc'], 'L1_ffn_uc': _L1_ffn_in['uc'], 'L1_ffn_bc': _L1_ffn_in['bc'], 'L1_ffn_wo': _L1_ffn_in['wo'], 'L1_ffn_uo': _L1_ffn_in['uo'], 'L1_ffn_bo': _L1_ffn_in['bo'], 'L1_ffn_in_c': _L1_ffn_in['in_c']}

def reference(x, ctx_1024, g_xattn, g_ffn, L0_xattn_wq, L0_xattn_bq, L0_xattn_wk, L0_xattn_bk, L0_xattn_wv, L0_xattn_bv, L0_xattn_wo, L0_xattn_bo, L0_ffn_router_w, L0_ffn_router_bias, L0_ffn_sw1, L0_ffn_sw3, L0_ffn_sw2, L0_ffn_ew1, L0_ffn_ew2, L1_xattn_igate_w, L1_xattn_igate_b, L1_xattn_fgate_w, L1_xattn_fgate_b, L1_xattn_norm_w, L1_ffn_wf, L1_ffn_uf, L1_ffn_bf, L1_ffn_wi, L1_ffn_ui, L1_ffn_bi, L1_ffn_wc, L1_ffn_uc, L1_ffn_bc, L1_ffn_wo, L1_ffn_uo, L1_ffn_bo, L1_ffn_in_c):
    import jax
    import jax.numpy as jnp

    def _L0_xattn_ref(q, k, v, wq, bq, wk, bk, wv, bv, wo, bo):
        import jax, jax.numpy as jnp
        import numpy as np
        D_MODEL = 128
        NUM_HEADS = 16
        B, S, D = q.shape
        H = NUM_HEADS
        dk = D // H
        Q = (q @ wq.T + bq).reshape(B, S, H, dk).transpose(0, 2, 1, 3)
        K = (k @ wk.T + bk).reshape(B, S, H, dk).transpose(0, 2, 1, 3)
        V = (v @ wv.T + bv).reshape(B, S, H, dk).transpose(0, 2, 1, 3)
        scores = jnp.einsum('bhqd,bhkd->bhqk', Q, K) / jnp.sqrt(jnp.float32(dk))
        attn = jax.nn.softmax(scores, axis=-1)
        out = jnp.einsum('bhqk,bhkd->bhqd', attn, V)
        out = out.transpose(0, 2, 1, 3).reshape(B, S, D)
        return out @ wo.T + bo

    def _L0_ffn_ref(x, router_w, router_bias, sw1, sw3, sw2, ew1, ew2):
        import jax, jax.numpy as jnp
        import numpy as np
        D_MODEL = 128
        H_SHARED = 256
        H_ROUTED = 128
        N_EXPERTS = 8
        TOP_K = 2
        B, T, C = x.shape
        xf = x.reshape(-1, C)
        shared_out = jax.nn.silu(xf @ sw1) * (xf @ sw3) @ sw2
        s = jax.nn.sigmoid((xf @ router_w.T).astype(jnp.float32))
        sel_scores = s + router_bias.astype(jnp.float32)
        _, topk_idx = jax.lax.top_k(sel_scores, TOP_K)
        s_sel = jnp.take_along_axis(s, topk_idx, axis=1)
        denom = s_sel.sum(axis=1, keepdims=True)
        gates = jnp.where(denom > 1e-09, s_sel / (denom + 1e-09), 1.0 / TOP_K).astype(x.dtype)
        one_hot = jax.nn.one_hot(topk_idx, N_EXPERTS, dtype=x.dtype)
        comb = jnp.einsum('nke,nk->ne', one_hot, gates)
        h = jax.nn.gelu(jnp.einsum('nd,edh->neh', xf, ew1), approximate=False)
        y = jnp.einsum('neh,ehd->ned', h, ew2)
        routed_out = jnp.einsum('ned,ne->nd', y, comb)
        return (shared_out + routed_out).reshape(B, T, C)

    def _L1_xattn_ref(q, k, v, igate_w, igate_b, fgate_w, fgate_b, norm_w):
        import jax, jax.numpy as jnp
        import numpy as np
        B, S, E, NH = (1, 256, 128, 8)
        DH = E // NH
        EPS_BACKEND = 1e-06
        EPS_NORM = 1e-05
        Bq, Sq, Eq = q.shape
        nh = igate_w.shape[0]
        dh = Eq // nh
        gate_in = jnp.concatenate([q, k, v], axis=-1)
        ig = jnp.transpose(gate_in @ igate_w.T + igate_b, (0, 2, 1))
        fg = jnp.transpose(gate_in @ fgate_w.T + fgate_b, (0, 2, 1))
        qh = q.reshape(Bq, Sq, nh, dh).transpose(0, 2, 1, 3)
        kh = k.reshape(Bq, Sq, nh, dh).transpose(0, 2, 1, 3)
        vh = v.reshape(Bq, Sq, nh, dh).transpose(0, 2, 1, 3)
        log_f_cum = jnp.cumsum(jax.nn.log_sigmoid(fg), axis=-1)
        log_fg_mat = log_f_cum[:, :, :, None] - log_f_cum[:, :, None, :]
        ltr = jnp.tril(jnp.ones((Sq, Sq), dtype=bool))
        log_D = jnp.where(ltr, log_fg_mat + ig[:, :, None, :], -jnp.inf)
        max_log_D = jnp.max(log_D, axis=-1, keepdims=True)
        D = jnp.exp(log_D - max_log_D)
        qk = jnp.einsum('bhsd,bhtd->bhst', qh, kh) / jnp.sqrt(jnp.float32(dh))
        C = qk * D
        normalizer = jnp.maximum(jnp.abs(jnp.sum(C, axis=-1, keepdims=True)), jnp.exp(-max_log_D))
        h = jnp.einsum('bhst,bhtd->bhsd', C / (normalizer + EPS_BACKEND), vh)
        mean = jnp.mean(h, axis=-1, keepdims=True)
        var = jnp.var(h, axis=-1, keepdims=True)
        h_norm = (h - mean) / jnp.sqrt(var + EPS_NORM)
        h_norm = h_norm * norm_w.reshape(nh, dh)[None, :, None, :]
        return h_norm.transpose(0, 2, 1, 3).reshape(Bq, Sq, Eq)

    def _L1_ffn_ref(x, wf, uf, bf, wi, ui, bi, wc, uc, bc, wo, uo, bo, in_c):
        import jax, jax.numpy as jnp
        import numpy as np
        from jax import lax
        T, B, I, M, O = (32, 64, 128, 128, 128)

        def _xavier(key, shape):
            fan_out, fan_in = shape
            limit = float(np.sqrt(6.0 / (fan_in + fan_out)))
            return jax.random.uniform(key, shape, jnp.float32, -limit, limit)
        batch = x.shape[1]
        c0 = jnp.broadcast_to(in_c, (batch, in_c.shape[0]))

        def step(c, xt):
            ft = jax.nn.sigmoid(xt @ wf.T + c @ uf.T + bf)
            it = jax.nn.sigmoid(xt @ wi.T + c @ ui.T + bi)
            gt = jnp.tanh(xt @ wc.T + c @ uc.T + bc)
            c = ft * c + it * gt
            return (c, None)
        c_final, _ = lax.scan(step, c0, x)
        h = jnp.tanh(jnp.einsum('tbi,oi->tbo', x, wo) + c_final @ uo.T + bo)
        return h
    x = x + jnp.tanh(g_xattn[0]) * _L0_xattn_ref(_layernorm(x, axis=-1), ctx_1024, ctx_1024, L0_xattn_wq, L0_xattn_bq, L0_xattn_wk, L0_xattn_bk, L0_xattn_wv, L0_xattn_bv, L0_xattn_wo, L0_xattn_bo)
    x = x + jnp.tanh(g_ffn[0]) * _L0_ffn_ref(_layernorm(x, axis=-1), L0_ffn_router_w, L0_ffn_router_bias, L0_ffn_sw1, L0_ffn_sw3, L0_ffn_sw2, L0_ffn_ew1, L0_ffn_ew2)
    x = x + jnp.tanh(g_xattn[1]) * _L1_xattn_ref(_layernorm(x, axis=-1), ctx_1024, ctx_1024, L1_xattn_igate_w, L1_xattn_igate_b, L1_xattn_fgate_w, L1_xattn_fgate_b, L1_xattn_norm_w)
    x = x + jnp.tanh(g_ffn[1]) * _L1_ffn_ref(_layernorm(x, axis=-1), L1_ffn_wf, L1_ffn_uf, L1_ffn_bf, L1_ffn_wi, L1_ffn_ui, L1_ffn_bi, L1_ffn_wc, L1_ffn_uc, L1_ffn_bc, L1_ffn_wo, L1_ffn_uo, L1_ffn_bo, L1_ffn_in_c)
    return x

_drawn_inputs = setup_inputs


def setup_inputs(seed=0):
    import zlib

    import numpy as np

    out = dict(_drawn_inputs(seed))
    spreads = {'g_ffn': (-1.0, 0.2),
     'L0_xattn_bq': (0.0, 0.1),
     'L0_xattn_bk': (0.0, 2.0),
     'L0_xattn_bv': (0.0, 0.1),
     'L0_xattn_bo': (0.0, 0.1),
     'L0_ffn_router_bias': (0.0, 0.1),
     'L1_ffn_bf': (0.0, 0.8),
     'L1_ffn_bi': (0.0, 0.8),
     'L1_ffn_bc': (0.0, 0.1),
     'L1_ffn_bo': (0.0, 0.1),
     'L1_ffn_in_c': (0.0, 2.0)}
    factors = {'L1_xattn_igate_b': 64.0, 'L1_xattn_fgate_w': 3.505}
    for name, (base, spread) in spreads.items():
        noise = np.random.default_rng([zlib.crc32(name.encode()), seed]).standard_normal(out[name].shape)
        drawn = base * np.exp(spread * noise) if base else spread * noise
        out[name] = jnp.asarray(drawn.astype(out[name].dtype))
    for name, factor in factors.items():
        out[name] = (out[name] * factor).astype(out[name].dtype)
    return out
```

```python
from contextlib import ExitStack

import numpy as np

import concourse.bass as bass
from concourse import mybir

P = 128
SEQ = 64
NB = 32
NP = NB // 2
EXPERTS = 8
BIG = -1.0e30
LOWEST = -3.0e38
W0 = 17
W1 = 33
WIN = 48
V0W = 7 * W0 + WIN
V1W = 3 * W1 + WIN
EPS_LN = 1e-5
EPS_MLSTM = 1e-6

F32 = mybir.dt.float32
ALU = mybir.AluOpType
ACT = mybir.ActivationFunctionType
AX = mybir.AxisListType.X

WEIGHTS_A = [("wq", P), ("wk", P), ("wv", P), ("wo", P)]
WEIGHTS_F = [("router", 96), ("sw1", 2 * P), ("sw3", 2 * P), ("sw2", 2 * P), ("ew1", EXPERTS * P), ("ew2", EXPERTS * P)]
WEIGHTS_M = [("gx", 40), ("gk", 40), ("gv", 40)]
WEIGHTS_R = [("wf", P), ("wi", P), ("wc", P), ("wy", P), ("uf", P), ("ui", P), ("uc", P), ("uy", P)]
COLUMNS = [("bq", 1), ("bk", 1), ("bv", 1), ("bf", 1), ("bi", 1), ("bc", 1), ("c0", 1), ("igb", 1), ("fgb", 1),
           ("one", 1), ("gates", 4), ("mhalf", 8), ("head0", 8), ("head1", 4), ("rb", 8), ("earlier", 64),
           ("bo", P), ("nw", P), ("by", P), ("ident", P), ("keep", P), ("floor", P), ("ldl", P), ("ldr", 4 * P)]


def offsets(names):
    at, out = 0, {}
    for name, width in names:
        out[name] = (at, at + width)
        at += width
    return out, at


WA, WA_N = offsets(WEIGHTS_A)
WF, WF_N = offsets(WEIGHTS_F)
WM, WM_N = offsets(WEIGHTS_M)
WR, WR_N = offsets(WEIGHTS_R)
CO, CO_N = offsets(COLUMNS)

EVENTS = """
xn0_aggr xn0_eps xn0_rstd xn0 xn1_aggr xn1_eps xn1_rstd xn1
xn2_aggr xn2_eps xn2_rstd xn2 xn3_aggr xn3_eps xn3_rstd xn3
a_xT_mm a_xT a_qkv_mm a_qs a_kv a_qm0 a_qm1 a_s0_mm a_s1_mm a_max0 a_max1 a_sub0 a_sub1 a_exp0 a_exp1
a_pT0_mm a_pT1_mm a_pT0 a_pT1 a_pv_mm a_o9 a_rden a_on a_oT_mm a_oT a_proj_mm a_xb a_x1
f_xT_mm f_xT f_logit_mm f_logit f_hs_mm f_tanh f_silu_half f_hs f_ys_mm f_acc0 f_he0_mm f_he1_mm f_ge0 f_ge1
f_y0_mm f_y1_mm f_acc1 f_acc2 f_acc3 f_acc4 f_acc5 f_acc6 f_acc7 f_acc8 f_x2
r_plus r_sig r_sel r_cmp r_tie r_beat r_rank r_top r_best r_sum r_guard r_inv r_share f_comb
m_xT_mm m_xT m_qs m_qm m_gate_mm m_abs m_exp m_ln m_min m_logf m_cum m_a m_run m_neg
m_s_mm m_ld_mm m_d m_c m_cv_mm m_h17 m_nT_mm m_clamp m_ex m_norm0 m_norm1 m_norm2 m_norm3 m_h
m_sum m_cent m_sq m_var m_veps m_rstd m_hn m_hw m_x3 m_kept
l_xT_mm l_xT l_xw_mm l_po l_u0_mm l_u1_mm l_g0 l_g1 l_q0 l_q1 l_c0 l_c1
""".split()


def build(nc, x_d, ctxT_d, ctx_d, wa_d, wf_d, wm_d, wr_d, co_d, out_d):
    with ExitStack() as ctx:
        def sb(name, shape):
            return ctx.enter_context(nc.sbuf_tensor(name, shape, F32))

        S = {name: ctx.enter_context(nc.semaphore(name)) for name in EVENTS}
        for name in ("ld_a ld_w ld_x0 ld_x1 ld_m0 ld_m1 rows0 rows1 "
                     "su_zero su_dve su_act su_pe t_rr_mm t_rr t_dup t_pre t_tanh t_out stored0 stored1").split():
            S[name] = ctx.enter_context(nc.semaphore(name))

        wa, wf, wm, wr, co = (sb(n, [P, w]) for n, w in
                              (("wa", WA_N), ("wf", WF_N), ("wm", WM_N), ("wr", WR_N), ("co", CO_N)))

        def A_(n):
            return wa[:, WA[n][0]:WA[n][1]]

        def F_(n, i=0, w=None):
            a = WF[n][0]
            return wf[:, a + i * P:a + (i + 1) * P] if w is None else wf[:, a:a + w]

        def R_(n):
            return wr[:, WR[n][0]:WR[n][1]]

        def C_(n, rows=slice(0, P)):
            return co[rows, CO[n][0]:CO[n][1]]

        gkv = sb("gkv", [P, 40])
        tg = sb("tg", [P, 4])
        bo_g = sb("bo_g", [P, P])
        nw_g = sb("nw_g", [P, P])
        u_half = sb("u_half", [P, 4 * P])
        b_half = sb("b_half", [P, 2])
        ident = C_("ident")

        def two(name, shape):
            return [sb(f"{name}{k}", shape) for k in range(2)]

        x_in, ctxT_a, ctxT_m = two("x_in", [P, P]), two("ctxT_a", [P, P]), two("ctxT_m", [P, P])
        kb1, v1 = two("kb1", [P, 2, P]), two("v1", [P, 2, V1W])
        xn = [two(f"xn{k}", [P, P]) for k in range(4)]
        st = [two(f"st{k}", [P, 6]) for k in range(4)]
        mv = [two(f"mv{k}", [P, 2]) for k in range(4)]
        ve = [two(f"ve{k}", [P, 1]) for k in range(4)]
        rs = [two(f"rs{k}", [P, 1]) for k in range(4)]
        xT = [two(f"xT{k}", [P, P]) for k in range(4)]
        qs, qm = two("qs", [P, 2, SEQ]), two("qm", [P, 2, 8, SEQ])
        kb, v0 = two("kb", [P, 2, P]), two("v0", [P, 2, V0W])
        mx, ex = two("mx", [P, 2, 8]), two("ex", [P, 2, 4 * P])
        pT, o9 = two("pT", [P, 2, 4 * P]), two("o9", [P, 8, 18])
        rden, on_buf, oT, xb, x1 = two("rden", [P, 16]), two("on", [P, P]), two("oT", [P, P]), two("xb", [P, P]), two("x1", [P, P])
        th, uh, hs = two("th", [P, 2 * P]), two("uh", [P, 2 * P]), two("hs", [P, 2 * P])
        he, acc, x2 = two("he", [P, 8 * P]), two("acc", [P, 9, P]), two("x2", [P, P])
        rt = two("rt", [P, 12, 8])
        rc = two("rc", [P, 3, 64])
        r1c = two("r1c", [P, 4])
        qs1, qm1 = two("qs1", [P, 2, SEQ]), two("qm1", [P, 2, 4, SEQ])
        ga, nsum = two("ga", [8, 8, P]), two("nsum", [P, P])
        ldl, ldr = two("ldl", [P, P]), two("ldr", [P, 4 * P])
        dd, cc, h17 = two("dd", [P, 4 * P]), two("cc", [P, 4 * P]), two("h17", [P, 4, 34])
        n8 = two("n8", [P, 5, 8])
        hm = two("hm", [P, 5, P])
        s8 = two("s8", [P, 5, 8])
        tgate, pp = two("tgate", [P, 3, SEQ]), two("pp", [P, 2, SEQ])
        cst = two("cst", [P, 96])
        x3 = two("x3", [P, P])
        x3_all, po_all = sb("x3_all", [P, NP, P]), sb("po_all", [P, NP, P])
        rr, cdup = sb("rr", [P, P]), sb("cdup", [P, P])
        pre, tt, res = two("pre", [P, 4, P]), two("tt", [P, 4, P]), two("res", [P, 4, P])

        def bank(name, n=1):
            return ctx.enter_context(nc.psum_tensor(name, [P, n, 512], F32))

        TA, SS, FB, MB, RB = bank("TA"), bank("SS", 2), bank("FB", 2), bank("MB", 2), bank("RB")
        block = ctx.enter_context(nc.Block())

        def wait(eng, name, count):
            if not isinstance(count, int) or count > 0:
                eng.wait_ge(S[name], count)

        def steps(eng, step):
            for i in range(-1, 5):
                step(i, i)
            with eng.Fori(5, 14, 2) as r:
                for k in range(2):
                    step(r if k == 0 else eng.snap(r + 1), 5 + k)
            for i in range(15, NP + 3):
                step(i, i)

        def on(i, pair):
            return not isinstance(i, int) or 0 <= pair < NP

        def counter(eng, i):
            known = {}

            def count(d):
                if d not in known:
                    known[d] = i + d if isinstance(i, int) else eng.snap(i + d)
                return known[d]
            return count

        @block.sync
        def _(sp):
            sp.dma_start(co[:, :], co_d).then_inc(S["ld_a"], 16)
            sp.dma_start(wa[:, :], wa_d).then_inc(S["ld_a"], 16)

            def load(i, par):
                count = counter(sp, i)
                fixed = isinstance(i, int)
                has = lambda d: not fixed or 0 <= i + d < NP
                for d in range(-3, 1):
                    count(d)

                def tokens(d, b=None):
                    n = P if b is None else SEQ
                    at = (i + d) * P + (b or 0) * SEQ
                    return slice(at, at + n) if fixed else bass.ds(sp.snap(at), n)

                near = tokens(1) if has(1) else None
                far = (tokens(-1), tokens(-1, 0), tokens(-1, 1)) if has(-1) else None
                if has(1):
                    k = (par + 1) % 2
                    wait(sp, "a_xb", count(0))
                    wait(sp, "xn0", count(0))
                    wait(sp, "a_qkv_mm", count(0))
                    sp.dma_start(x_in[k][:, :], x_d[near, :]).then_inc(S[f"ld_x{k}"], 16)
                    sp.dma_start(ctxT_a[k][:, :], ctxT_d[:, near]).then_inc(S[f"ld_x{k}"], 16)
                if has(-1):
                    k = (par + 1) % 2
                    wait(sp, "m_gate_mm", count(-2))
                    sp.dma_start(ctxT_m[k][:, :], ctxT_d[:, far[0]]).then_inc(S[f"ld_m{k}"], 16)
                    wait(sp, "m_s_mm", count(-2))
                    wait(sp, "m_cv_mm", count(-2))
                    for b in range(2):
                        q = slice(b * SEQ, (b + 1) * SEQ)
                        sp.dma_start(kb1[k][q, :, q], ctxT_d[:, far[1 + b]].rearrange("(u d) t -> d u t", u=2)).then_inc(S[f"ld_m{k}"], 16)
                        for h in range(2):
                            sp.dma_start(v1[k][q, b, 0:4 * W1].rearrange("t (h w) -> t h w", w=W1)[:, :, 17 * h:17 * h + 16],
                                         ctx_d[far[1 + b], :].rearrange("t (h w) -> t h w", w=32)[:, :, 16 * h:16 * h + 16])\
                              .then_inc(S[f"ld_m{k}"], 16)
                if fixed and i == -1:
                    sp.dma_start(wf[:, :], wf_d).then_inc(S["ld_w"], 16)
                    sp.dma_start(wm[:, :], wm_d).then_inc(S["ld_w"], 16)
                    sp.dma_start(wr[:, :], wr_d).then_inc(S["ld_w"], 16)
                    wait(sp, "su_zero", 4)
                if has(-2):
                    k = par % 2
                    wait(sp, "m_ld_mm", count(-3))
                    wait(sp, "m_neg", count(-1))
                    for b in range(2):
                        sp.dma_start(ldr[k][96 + b:97 + b, :].rearrange("o (h s) -> o h s", h=8),
                                     ga[k][:, 6, b * SEQ:(b + 1) * SEQ]).then_inc(S[f"rows{k}"], 16)
            steps(sp, load)
            sp.wait_ge(S["stored0"], 2 * 16)
            sp.wait_ge(S["stored1"], 2 * 16)

        @block.gpsimd
        def _(pool):
            for k in range(2):
                nc.gpsimd.memset(kb[k][:, :, :], 0.0)
                nc.gpsimd.memset(v0[k][:, :, :], 0.0)
                nc.gpsimd.memset(kb1[k][:, :, :], 0.0)
                nc.gpsimd.memset(cst[k][:, :], 0.0)
                nc.gpsimd.memset(nsum[k][:, :], 0.0)
                nc.gpsimd.memset(v1[k][:, :, :], 0.0).then_inc(S["su_zero"], 1)
            pool.wait_ge(S["su_zero"], 2)
            for k in range(2):
                for b in range(2):
                    q = slice(b * SEQ, (b + 1) * SEQ)
                    nc.gpsimd.memset(v0[k][q, b, 0:8 * W0].rearrange("t (h w) -> t h w", w=W0)[:, :, 8:9], 1.0)
                    last = nc.gpsimd.memset(v1[k][q, b, 0:4 * W1].rearrange("t (h w) -> t h w", w=W1)[:, :, 16:17], 1.0)
                last.then_inc(S["su_zero"], 1)
            pool.wait_ge(S["su_dve"], 3)

            def norm(n, par, count):
                wait(pool, f"xn{n}_eps", count)
                nc.gpsimd.tensor_tensor(rs[n][par][:, :], ve[n][par][:, :], C_("mhalf")[:, 0:1], ALU.pow).then_inc(S[f"xn{n}_rstd"], 1)

            def step(i, j):
                a = j % 2
                f, m, r = (a + 1) % 2, a, (a + 1) % 2
                count = counter(pool, i)
                has = lambda d: not isinstance(i, int) or 0 <= i + d < NP
                if has(0):
                    for u in range(2):
                        if u == 0:
                            wait(pool, "a_qs", count(1))
                            wait(pool, "a_s1_mm", count(-1))
                        nc.gpsimd.tensor_tensor(qm[a][:, u, :, :], qs[a][:, u, :].unsqueeze(1).to_broadcast([P, 8, SEQ]),
                                                C_("head0").unsqueeze(2).to_broadcast([P, 8, SEQ]), ALU.mult).then_inc(S[f"a_qm{u}"], 1)
                if has(-2):
                    wait(pool, "m_qs", count(-1))
                    wait(pool, "m_s_mm", count(-3))
                    nc.gpsimd.tensor_tensor(qm1[m][:, :, :, :], qs1[m][:, :, :].unsqueeze(2).to_broadcast([P, 2, 4, SEQ]),
                                            C_("head1").unsqueeze(1).unsqueeze(3).to_broadcast([P, 2, 4, SEQ]), ALU.mult).then_inc(S["m_qm"], 1)
                if has(0):
                    wait(pool, "xn0", count(1))
                    wait(pool, "a_x1", count(-1))
                    nc.gpsimd.tensor_tensor(xb[a][:, :], x_in[a][:, :], bo_g[:, :], ALU.add).then_inc(S["a_xb"], 1)
                if has(-2):
                    wait(pool, "m_cent", count(-1))
                    nc.gpsimd.tensor_tensor(hm[m][:, 2, :], hm[m][:, 1, :], hm[m][:, 1, :], ALU.mult).then_inc(S["m_sq"], 1)
                    wait(pool, "m_veps", count(-1))
                    nc.gpsimd.tensor_tensor(s8[m][:, 4, :], s8[m][:, 3, :], C_("mhalf"), ALU.pow).then_inc(S["m_rstd"], 1)
                    norm(3, m, count(-1))
                if has(0):
                    norm(1, a, count(1))
                if has(-1):
                    norm(2, f, count(0))
                if has(1):
                    norm(0, f, count(2))
            steps(pool, step)

        @block.scalar
        def _(act):
            act.wait_ge(S["ld_a"], 32)
            nc.scalar.activation(tg[:, :], C_("gates"), ACT.Tanh).then_inc(S["su_act"], 1)

            def scan(k, r, count):
                wait(act, f"l_u{k}_mm", count(-2))
                wait(act, f"l_c{k}", count(-3))
                for g in range(3):
                    last = nc.scalar.activation(tgate[k][:, g, :], RB[:, 0, g * P + k * SEQ:g * P + (k + 1) * SEQ], ACT.Tanh,
                                                bias=b_half[:, g:g + 1] if g < 2 else C_("bc"), scale=0.5 if g < 2 else 1.0)
                last.then_inc(S[f"l_g{k}"], 1)

            def step(i, j):
                a = j % 2
                f, m, r = (a + 1) % 2, a, (a + 1) % 2
                count = counter(act, i)
                has = lambda d: not isinstance(i, int) or 0 <= i + d < NP
                act.preload_act_table_set("natural_log_exp_and_others")
                if has(0):
                    wait(act, "a_xT_mm", count(1))
                    wait(act, "a_qkv_mm", count(0))
                    nc.scalar.copy(xT[0][a][:, :], TA[:, 0, 0:P]).then_inc(S["a_xT"], 1)
                if has(-2):
                    wait(act, "m_xT_mm", count(-1))
                    nc.scalar.copy(xT[2][m][:, :], MB[:, 0, 0:P]).then_inc(S["m_xT"], 1)
                    for u in range(2):
                        for b in range(2):
                            last = nc.scalar.copy(qs1[m][b * SEQ:(b + 1) * SEQ, u, :],
                                                  MB[u * SEQ:(u + 1) * SEQ, 0, b * SEQ:(b + 1) * SEQ])
                    last.then_inc(S["m_qs"], 1)
                if has(0):
                    wait(act, "a_qkv_mm", count(1))
                    wait(act, "a_s1_mm", count(-1))
                    for u in range(2):
                        for b in range(2):
                            q, w = slice(b * SEQ, (b + 1) * SEQ), slice(u * SEQ, (u + 1) * SEQ)
                            last = nc.scalar.activation(kb[a][q, u, q], TA[w, 0, 2 * P + b * SEQ:2 * P + (b + 1) * SEQ],
                                                        ACT.Identity, bias=C_("bk", w))
                    wait(act, "a_pv_mm", count(-1))
                    for b in range(2):
                        q = slice(b * SEQ, (b + 1) * SEQ)
                        v = v0[a][q, b, 0:8 * W0].rearrange("t (h w) -> t h w", w=W0)
                        s = TA[q, 0, 3 * P:4 * P].rearrange("t (h w) -> t h w", w=16)
                        nc.scalar.copy(v[:, :, 0:8], s[:, :, 0:8])
                        last = nc.scalar.copy(v[:, :, 9:17], s[:, :, 8:16])
                    last.then_inc(S["a_kv"], 1)
                if has(-2):
                    wait(act, "m_gate_mm", count(-1))
                    wait(act, "m_logf", count(-3))
                    nc.scalar.activation(ga[m][:, 0, :], MB[32:40, 0, P:2 * P], ACT.Abs, bias=C_("fgb", slice(32, 40))).then_inc(S["m_abs"], 1)
                    wait(act, "m_abs", count(-1))
                    nc.scalar.activation(ga[m][:, 1, :], ga[m][:, 0, :], ACT.Exp, scale=-1.0).then_inc(S["m_exp"], 1)
                    wait(act, "m_exp", count(-1))
                    nc.scalar.activation(ga[m][:, 2, :], ga[m][:, 1, :], ACT.Ln, bias=C_("one", slice(0, 8))).then_inc(S["m_ln"], 1)
                if has(0):
                    for u in range(2):
                        wait(act, f"a_sub{u}", count(1))
                        nc.scalar.activation(ex[a][:, u, :], ex[a][:, u, :], ACT.Exp, scale=8.0 ** -0.5).then_inc(S[f"a_exp{u}"], 1)
                if has(-1):
                    wait(act, "f_xT_mm", count(0))
                    wait(act, "f_he1_mm", count(-2))
                    nc.scalar.copy(xT[1][f][:, :], FB[:, 0, 0:P]).then_inc(S["f_xT"], 1)
                    wait(act, "f_logit_mm", count(0))
                    nc.scalar.activation(rt[f][:, 0, :], FB[:, 1, 0:EXPERTS], ACT.Exp, scale=-1.0).then_inc(S["f_logit"], 1)
                if has(0):
                    wait(act, "a_pv_mm", count(-1))
                    for u in range(2):
                        wait(act, f"a_pT{u}_mm", count(1))
                        nc.scalar.copy(pT[a][:, u, :], SS[:, u, :]).then_inc(S[f"a_pT{u}"], 1)
                if has(-2):
                    wait(act, "m_ld_mm", count(-1))
                    nc.scalar.activation(dd[m][:, :], MB[:, 0, :], ACT.Exp).then_inc(S["m_d"], 1)
                if has(0):
                    wait(act, "a_pv_mm", count(1))
                    wait(act, "a_on", count(-1))
                    pv = SS[:, :, 0:4 * 96].rearrange("p u (k b w) -> p u k b w", k=4, b=2)
                    o = o9[a][:, :, :].rearrange("p (u k) w -> p u k w", u=2)
                    for h in range(2):
                        for b in range(2):
                            last = nc.scalar.copy(o[b * SEQ:(b + 1) * SEQ, :, :, 9 * h:9 * h + 9],
                                                  pv[h * SEQ:(h + 1) * SEQ, :, :, b, 8 * h:8 * h + 9])
                    last.then_inc(S["a_o9"], 1)
                if has(-3):
                    wait(act, "l_xT_mm", count(-2))
                    wait(act, "l_xw_mm", count(-3))
                    nc.scalar.copy(xT[3][r][:, :], RB[:, 0, 3 * P:4 * P]).then_inc(S["l_xT"], 1)
                    wait(act, "l_xw_mm", count(-2))
                    dst = po_all[:, i - 3, :] if isinstance(i, int) else po_all[:, bass.ds(count(-3), 1), :].rearrange("p o d -> p (o d)")
                    nc.scalar.copy(dst, RB[:, 0, 3 * P:4 * P]).then_inc(S["l_po"], 1)
                if has(-2):
                    wait(act, "m_cv_mm", count(-1))
                    wait(act, "m_h", count(-3))
                    cv = MB[:, 1, 0:4 * 96].rearrange("p (k b w) -> p k b w", k=4, b=2)
                    for h in range(2):
                        for b in range(2):
                            last = nc.scalar.copy(h17[m][b * SEQ:(b + 1) * SEQ, :, 17 * h:17 * h + 17],
                                                  cv[h * SEQ:(h + 1) * SEQ, :, b, 16 * h:16 * h + 17])
                    last.then_inc(S["m_h17"], 1)
                    wait(act, "m_clamp", count(-1))
                    nc.scalar.activation(n8[m][:, 1, :], n8[m][:, 0, :], ACT.Exp).then_inc(S["m_ex"], 1)
                if has(-1) or has(-3):
                    act.preload_act_table(ACT.Gelu)
                if has(-1):
                    wait(act, "f_hs_mm", count(0))
                    nc.scalar.activation(th[f][:, :], FB[:, 0, 0:2 * P], ACT.Tanh, scale=0.5).then_inc(S["f_tanh"], 1)
                if has(-3):
                    scan(0, r, count)
                if has(-1):
                    wait(act, "f_he0_mm", count(0))
                    nc.scalar.activation(he[f][:, 0:4 * P], FB[:, 1, :], ACT.Gelu).then_inc(S["f_ge0"], 1)
                    wait(act, "f_he1_mm", count(0))
                    nc.scalar.activation(he[f][:, 4 * P:8 * P], FB[:, 0, :], ACT.Gelu).then_inc(S["f_ge1"], 1)
                if has(0):
                    wait(act, "a_oT_mm", count(1))
                    nc.scalar.copy(oT[a][:, :], TA[:, 0, 0:P]).then_inc(S["a_oT"], 1)
                if has(-3):
                    scan(1, r, count)
                if has(-2):
                    wait(act, "m_x3", count(-1))
                    dst = x3_all[:, i - 2, :] if isinstance(i, int) else x3_all[:, bass.ds(count(-2), 1), :].rearrange("p o d -> p (o d)")
                    nc.scalar.copy(dst, x3[m][:, :]).then_inc(S["m_kept"], 1)
            steps(act, step)

            for g in range(4):
                wait(act, "t_pre", g + 1)
                if g >= 2:
                    wait(act, "t_out", g - 1)
                nc.scalar.activation(tt[g % 2][:, :, :], pre[g % 2][:, :, :], ACT.Tanh).then_inc(S["t_tanh"], 1)
                wait(act, "t_out", g + 1)
                act.dma_start(out_d.rearrange("(n p) d -> p n d", p=P)[:, 4 * g:4 * g + 4, :], res[g % 2][:, :, :]).then_inc(S[f"stored{g % 2}"], 16)

        @block.vector
        def _(dve):
            dve.wait_ge(S["ld_a"], 32)
            dve.wait_ge(S["ld_w"], 48)
            dve.wait_ge(S["su_act"], 1)
            dve.wait_ge(S["su_zero"], 4)
            v = nc.vector
            v.tensor_tensor(gkv[:, :], wm[:, WM["gk"][0]:WM["gk"][1]], wm[:, WM["gv"][0]:WM["gv"][1]], ALU.add)
            v.tensor_scalar(nw_g[:, :], C_("nw"), tg[:, 1:2], None, ALU.mult)
            v.tensor_scalar(u_half[:, :], wr[:, WR["uf"][0]:WR["uy"][1]], 0.5, None, ALU.mult)
            v.tensor_scalar(b_half[:, :], co[:, CO["bf"][0]:CO["bi"][1]], 0.5, None, ALU.mult)
            v.tensor_scalar(cst[0][:, 0:SEQ], C_("c0").to_broadcast([P, SEQ]), 2.0, None, ALU.mult)
            for k in range(2):
                v.tensor_copy(ldl[k][:, :], C_("ldl"))
                last = v.tensor_copy(ldr[k][:, :], C_("ldr"))
            last.then_inc(S["su_dve"], 1)
            dve.wait_ge(S["su_pe"], 1)
            v.tensor_tensor(pre[0][:, 0, :], TA[:, 0, 0:P], C_("bo"), ALU.add).then_inc(S["su_dve"], 1)
            dve.wait_ge(S["su_dve"], 2)
            v.tensor_scalar(bo_g[:, :], pre[0][:, 0, :], tg[:, 0:1], None, ALU.mult).then_inc(S["su_dve"], 1)

            def norm(n, par, count, src):
                v.bn_stats(st[n][par][:, :], src)
                dve.drain()
                v.bn_aggr(mv[n][par][:, :], st[n][par][:, :]).then_inc(S[f"xn{n}_aggr"], 1)
                wait(dve, f"xn{n}_aggr", count)
                v.tensor_scalar(ve[n][par][:, :], mv[n][par][:, 1:2], EPS_LN, None, ALU.add).then_inc(S[f"xn{n}_eps"], 1)

            def normed(n, par, count, src):
                wait(dve, f"xn{n}_rstd", count)
                v.tensor_scalar(xn[n][par][:, :], src, mv[n][par][:, 0:1], rs[n][par][:, 0:1], ALU.subtract, ALU.mult).then_inc(S[f"xn{n}"], 1)

            def state(k, count):
                now, new = cst[k], cst[1 - k]
                wait(dve, f"l_g{k}", count(-2))
                v.scalar_tensor_tensor(pp[k][:, 0, :], tgate[k][:, 0, :], 1.0, now[:, 0:SEQ], ALU.add, ALU.mult)
                v.scalar_tensor_tensor(pp[k][:, 1, :], tgate[k][:, 1, :], 1.0, tgate[k][:, 2, :], ALU.add, ALU.mult).then_inc(S[f"l_q{k}"], 1)
                wait(dve, f"l_q{k}", count(-2))
                v.scalar_tensor_tensor(new[:, 0:SEQ], pp[k][:, 0, :], 0.5, pp[k][:, 1, :], ALU.mult, ALU.add).then_inc(S[f"l_c{k}"], 1)

            def step(i, j):
                a = j % 2
                f, m, r = (a + 1) % 2, a, (a + 1) % 2
                count = counter(dve, i)
                has = lambda d: not isinstance(i, int) or 0 <= i + d < NP
                if has(0):
                    wait(dve, "a_qkv_mm", count(1))
                    for u in range(2):
                        for b in range(2):
                            w = slice(u * SEQ, (u + 1) * SEQ)
                            last = v.tensor_scalar(qs[a][b * SEQ:(b + 1) * SEQ, u, :], SS[w, 0, b * SEQ:(b + 1) * SEQ],
                                                   C_("bq", w), None, ALU.add)
                    last.then_inc(S["a_qs"], 1)
                if has(-2):
                    G = ga[m]
                    wait(dve, "m_abs", count(-1))
                    v.tensor_scalar(G[:, 3, :], MB[32:40, 0, P:2 * P], C_("fgb", slice(32, 40)), 0.0, ALU.add, ALU.min).then_inc(S["m_min"], 1)
                    wait(dve, "m_min", count(-1))
                    wait(dve, "m_ln", count(-1))
                    v.tensor_tensor(G[:, 3, :], G[:, 3, :], G[:, 2, :], ALU.subtract).then_inc(S["m_logf"], 1)
                    wait(dve, "m_logf", count(-1))
                    v.tensor_tensor_scan(G[:, 4, :], C_("keep", slice(0, 8)), G[:, 3, :], 0.0, ALU.mult, ALU.add).then_inc(S["m_cum"], 1)
                    wait(dve, "m_cum", count(-1))
                    wait(dve, "m_ld_mm", count(-3))
                    v.scalar_tensor_tensor(ldl[m][64:72, :], MB[0:8, 0, P:2 * P], C_("igb", slice(0, 8)), G[:, 4, :], ALU.add, ALU.subtract)
                    v.scalar_tensor_tensor(G[:, 5, :], MB[0:8, 0, P:2 * P], C_("igb", slice(0, 8)), G[:, 4, :], ALU.add, ALU.subtract).then_inc(S["m_a"], 1)
                    wait(dve, "m_a", count(-1))
                    v.tensor_tensor_scan(G[:, 7, :], C_("floor", slice(0, 8)), G[:, 5, :], LOWEST, ALU.add, ALU.max).then_inc(S["m_run"], 1)
                    wait(dve, "m_run", count(-1))
                    if isinstance(i, int):
                        if i - 2 >= 2:
                            dve.wait_ge(S[f"rows{m}"], 32 * ((i - 2) // 2))
                    else:
                        dve.wait_ge(S[f"rows{m}"], dve.snap((i - 5 + 5 - 2 - m) * 16))
                    v.scalar_tensor_tensor(nsum[m][0:8, :], G[:, 4, :], -1.0, G[:, 7, :], ALU.mult, ALU.subtract)
                    v.tensor_scalar(G[:, 6, :], G[:, 7, :], -1.0, None, ALU.mult).then_inc(S["m_neg"], 1)
                if has(0):
                    for u in range(2):
                        sc = SS[:, u, :].rearrange("p (g t) -> p g t", t=SEQ)
                        wait(dve, f"a_s{u}_mm", count(1))
                        v.tensor_reduce(mx[a][:, u, :], sc, AX, ALU.max).then_inc(S[f"a_max{u}"], 1)
                        wait(dve, f"a_max{u}", count(1))
                        if u == 0:
                            wait(dve, "a_pT1_mm", count(-1))
                        v.tensor_tensor(ex[a][:, u, :].rearrange("p (g t) -> p g t", t=SEQ), sc,
                                        mx[a][:, u, :].unsqueeze(2).to_broadcast([P, 8, SEQ]), ALU.subtract).then_inc(S[f"a_sub{u}"], 1)
                if has(-1):
                    T, K, c1 = rt[f], rc[f], r1c[f]
                    now = count(0)
                    wait(dve, "f_logit", now)
                    v.tensor_scalar(T[:, 1, :], T[:, 0, :], 1.0, None, ALU.add).then_inc(S["r_plus"], 1)
                    wait(dve, "r_plus", now)
                    v.reciprocal(T[:, 2, :], T[:, 1, :]).then_inc(S["r_sig"], 1)
                    wait(dve, "r_sig", now)
                    v.tensor_tensor(T[:, 3, :], T[:, 2, :], C_("rb"), ALU.add).then_inc(S["r_sel"], 1)
                    wait(dve, "r_sel", now)
                    mine = T[:, 3, :].unsqueeze(2).to_broadcast([P, 8, 8])
                    other = T[:, 3, :].unsqueeze(1).to_broadcast([P, 8, 8])
                    sq = lambda n: K[:, n, :].rearrange("p (e o) -> p e o", o=8)
                    v.tensor_tensor(sq(0), other, mine, ALU.is_gt)
                    v.tensor_tensor(sq(1), other, mine, ALU.is_ge).then_inc(S["r_cmp"], 1)
                    wait(dve, "r_cmp", now)
                    v.tensor_tensor(K[:, 2, :], K[:, 1, :], C_("earlier"), ALU.mult).then_inc(S["r_tie"], 1)
                    wait(dve, "r_tie", now)
                    v.tensor_tensor(K[:, 1, :], K[:, 0, :], K[:, 2, :], ALU.max).then_inc(S["r_beat"], 1)
                    wait(dve, "r_beat", now)
                    v.reduce_sum(T[:, 4, :], sq(1), AX).then_inc(S["r_rank"], 1)
                    wait(dve, "r_rank", now)
                    v.tensor_scalar(T[:, 5, :], T[:, 4, :], 2.0, None, ALU.is_lt).then_inc(S["r_top"], 1)
                    wait(dve, "r_top", now)
                    v.tensor_tensor(T[:, 6, :], T[:, 5, :], T[:, 2, :], ALU.mult).then_inc(S["r_best"], 1)
                    wait(dve, "r_best", now)
                    v.reduce_sum(c1[:, 0:1], T[:, 6, :], AX).then_inc(S["r_sum"], 1)
                    wait(dve, "r_sum", now)
                    v.tensor_scalar(c1[:, 2:3], c1[:, 0:1], 1e-9, 0.5, ALU.is_le, ALU.mult)
                    v.tensor_scalar(c1[:, 1:2], c1[:, 0:1], 1e-9, None, ALU.add).then_inc(S["r_guard"], 1)
                    wait(dve, "r_guard", now)
                    v.reciprocal(c1[:, 3:4], c1[:, 1:2]).then_inc(S["r_inv"], 1)
                    wait(dve, "r_inv", now)
                    v.tensor_scalar(T[:, 7, :], T[:, 6, :], c1[:, 3:4], c1[:, 2:3], ALU.mult, ALU.max).then_inc(S["r_share"], 1)
                    wait(dve, "r_share", now)
                    v.scalar_tensor_tensor(T[:, 9, :], T[:, 7, :], tg[:, 2:3], T[:, 5, :], ALU.mult, ALU.mult).then_inc(S["f_comb"], 1)
                if has(-2):
                    wait(dve, "m_d", count(-1))
                    wait(dve, "m_s_mm", count(-1))
                    v.scalar_tensor_tensor(cc[m][:, :], MB[:, 1, :], 0.25, dd[m][:, :], ALU.mult, ALU.mult).then_inc(S["m_c"], 1)
                    wait(dve, "m_nT_mm", count(-1))
                    v.tensor_scalar(n8[m][:, 0, :], MB[:, 0, 0:8], 88.0, None, ALU.min).then_inc(S["m_clamp"], 1)
                if has(-1):
                    wait(dve, "f_tanh", count(0))
                    v.scalar_tensor_tensor(uh[f][:, :], th[f][:, :], 1.0, FB[:, 0, 0:2 * P], ALU.add, ALU.mult).then_inc(S["f_silu_half"], 1)
                    wait(dve, "f_silu_half", count(0))
                    v.scalar_tensor_tensor(hs[f][:, :], uh[f][:, :], 0.5, FB[:, 0, 2 * P:4 * P], ALU.mult, ALU.mult).then_inc(S["f_hs"], 1)
                if has(-3):
                    state(0, count)
                if has(-1):
                    wait(dve, "f_ys_mm", count(0))
                    v.scalar_tensor_tensor(acc[f][:, 0, :], FB[:, 0, 0:P], tg[:, 2:3], x1[f][:, :], ALU.mult, ALU.add).then_inc(S["f_acc0"], 1)
                if has(-2):
                    dn = h17[m][:, :, 16:18]
                    n = count(-1)
                    wait(dve, "m_h17", n)
                    wait(dve, "m_ex", n)
                    q8 = lambda k: n8[m][:, k, :].rearrange("p (k h) -> p k h", h=2)
                    v.scalar_tensor_tensor(q8(2), dn, -1.0, dn, ALU.mult, ALU.max).then_inc(S["m_norm0"], 1)
                    wait(dve, "m_norm0", n)
                    v.tensor_tensor(q8(3), q8(2), q8(1), ALU.max).then_inc(S["m_norm1"], 1)
                    wait(dve, "m_norm1", n)
                    v.tensor_scalar(n8[m][:, 2, :], n8[m][:, 3, :], EPS_MLSTM, None, ALU.add).then_inc(S["m_norm2"], 1)
                    wait(dve, "m_norm2", n)
                    v.reciprocal(n8[m][:, 4, :], n8[m][:, 2, :]).then_inc(S["m_norm3"], 1)
                    wait(dve, "m_norm3", n)
                    H = hm[m]
                    by8 = lambda t: t.rearrange("p (h w) -> p h w", w=16)
                    wide = lambda t: t.unsqueeze(2).to_broadcast([P, 8, 16])
                    for h in range(2):
                        last = v.tensor_tensor(H[:, 0, :].rearrange("p (k h w) -> p k h w", h=2, w=16)[:, :, h, :], h17[m][:, :, 18 * h:18 * h + 16],
                                               q8(4)[:, :, h:h + 1].to_broadcast([P, 4, 16]), ALU.mult)
                    last.then_inc(S["m_h"], 1)
                    wait(dve, "m_h", n)
                    v.reduce_sum(s8[m][:, 0, :], by8(H[:, 0, :]), AX).then_inc(S["m_sum"], 1)
                    wait(dve, "m_sum", n)
                    v.scalar_tensor_tensor(by8(H[:, 1, :]), wide(s8[m][:, 0, :]), -1.0 / 16, by8(H[:, 0, :]), ALU.mult, ALU.add).then_inc(S["m_cent"], 1)
                if has(0):
                    wait(dve, "a_o9", count(1))
                    v.reciprocal(rden[a][:, :].rearrange("p (k h) -> p k h", h=2), o9[a][:, :, 8:10]).then_inc(S["a_rden"], 1)
                    wait(dve, "a_rden", count(1))
                    for h in range(2):
                        last = v.tensor_tensor(on_buf[a][:, :].rearrange("p (k h w) -> p k h w", h=2, w=8)[:, :, h, :], o9[a][:, :, 10 * h:10 * h + 8],
                                               rden[a][:, :].rearrange("p (k h) -> p k h", h=2)[:, :, h:h + 1].to_broadcast([P, 8, 8]), ALU.mult)
                    last.then_inc(S["a_on"], 1)
                if has(-2):
                    wait(dve, "m_sq", n)
                    v.reduce_sum(s8[m][:, 2, :], by8(H[:, 2, :]), AX).then_inc(S["m_var"], 1)
                    wait(dve, "m_var", n)
                    v.tensor_scalar(s8[m][:, 3, :], s8[m][:, 2, :], 1.0 / 16, EPS_LN, ALU.mult, ALU.add).then_inc(S["m_veps"], 1)
                if has(-1):
                    y = lambda e: FB[:, 1 if e < 4 else 0, (e % 4) * P:(e % 4 + 1) * P]
                    wait(dve, "f_y0_mm", count(0))
                    for e in range(4):
                        add_expert(e, f, count, y)
                if has(-2):
                    wait(dve, "m_rstd", n)
                    v.tensor_tensor(by8(H[:, 3, :]), by8(H[:, 1, :]), wide(s8[m][:, 4, :]), ALU.mult).then_inc(S["m_hn"], 1)
                    wait(dve, "m_hn", n)
                    v.tensor_tensor(H[:, 4, :], H[:, 3, :], nw_g[:, :], ALU.mult).then_inc(S["m_hw"], 1)
                    wait(dve, "m_hw", n)
                    wait(dve, "m_kept", count(-3))
                    v.tensor_tensor(x3[m][:, :], H[:, 4, :], x2[m][:, :], ALU.add).then_inc(S["m_x3"], 1)
                    wait(dve, "m_x3", n)
                    norm(3, m, n, x3[m][:, :])
                if has(0):
                    wait(dve, "a_proj_mm", count(1))
                    wait(dve, "a_xb", count(1))
                    v.scalar_tensor_tensor(x1[a][:, :], TA[:, 0, P:2 * P], tg[:, 0:1], xb[a][:, :], ALU.mult, ALU.add).then_inc(S["a_x1"], 1)
                    wait(dve, "a_x1", count(1))
                    norm(1, a, count(1), x1[a][:, :])
                if has(-3):
                    state(1, count)
                if has(-2):
                    normed(3, m, n, x3[m][:, :])
                if has(0):
                    normed(1, a, count(1), x1[a][:, :])
                if has(-1):
                    wait(dve, "f_y1_mm", count(0))
                    for e in range(4, 8):
                        add_expert(e, f, count, y)
                    wait(dve, "f_acc7", count(0))
                    wait(dve, "f_acc8", count(0))
                    v.tensor_tensor(x2[f][:, :], acc[f][:, 7, :], acc[f][:, 8, :], ALU.add).then_inc(S["f_x2"], 1)
                    wait(dve, "f_x2", count(0))
                    norm(2, f, count(0), x2[f][:, :])
                if has(1):
                    k = f
                    if isinstance(i, int):
                        dve.wait_ge(S[f"ld_x{k}"], 32 * ((i + 1) // 2 + 1))
                    else:
                        dve.wait_ge(S[f"ld_x{k}"], dve.snap((i + 1 - k) * 16 + 32))
                    norm(0, k, count(2), x_in[k][:, :])
                if has(-1):
                    normed(2, f, count(0), x2[f][:, :])
                if has(1):
                    normed(0, f, count(2), x_in[f][:, :])

            def add_expert(e, f, count, y):
                if e == 0:
                    wait(dve, "f_comb", count(0))
                    v.tensor_scalar(acc[f][:, 1, :], y(0), rt[f][:, 9, 0:1], None, ALU.mult).then_inc(S["f_acc1"], 1)
                else:
                    before = e - 1
                    wait(dve, f"f_acc{before}", count(0))
                    v.scalar_tensor_tensor(acc[f][:, e + 1, :], y(e), rt[f][:, 9, e:e + 1], acc[f][:, before, :],
                                           ALU.mult, ALU.add).then_inc(S[f"f_acc{e + 1}"], 1)
            steps(dve, step)

            wait(dve, "l_c1", NP)
            for b in range(2):
                last = v.tensor_copy(cdup[:, b * SEQ:(b + 1) * SEQ], cst[0][:, 0:SEQ])
            last.then_inc(S["t_dup"], 1)
            wait(dve, "t_rr_mm", 1)
            v.tensor_tensor(rr[:, :], TA[:, 0, 0:P], C_("by"), ALU.add).then_inc(S["t_rr"], 1)
            wait(dve, "t_rr", 1)
            wait(dve, "l_po", NP)
            wait(dve, "m_kept", NP)
            for g in range(5):
                if g < 4:
                    if g >= 2:
                        wait(dve, "t_tanh", g - 1)
                    v.tensor_tensor(pre[g % 2][:, :, :], po_all[:, 4 * g:4 * g + 4, :], rr[:, :].unsqueeze(1).to_broadcast([P, 4, P]),
                                    ALU.add).then_inc(S["t_pre"], 1)
                if g >= 1:
                    h = g - 1
                    wait(dve, "t_tanh", h + 1)
                    if h >= 2:
                        dve.wait_ge(S[f"stored{h % 2}"], 16 * (h // 2))
                    v.scalar_tensor_tensor(res[h % 2][:, :, :], tt[h % 2][:, :, :], tg[:, 3:4], x3_all[:, 4 * h:4 * h + 4, :],
                                           ALU.mult, ALU.add).then_inc(S["t_out"], 1)

        @block.tensor
        def _(pe):
            pe.wait_ge(S["ld_a"], 32)
            nc.tensor.matmul(TA[:, 0, 0:P], C_("bv").to_broadcast([P, P]), A_("wo"), start=True, stop=True).then_inc(S["su_pe"], 1)
            pe.wait_ge(S["su_dve"], 3)
            pe.wait_ge(S["ld_w"], 48)
            mm = nc.tensor.matmul

            def transposed(out, src):
                return nc.tensor.transpose(out, src, ident)

            def buffered(name, i, d, k, n):
                if isinstance(i, int):
                    pe.wait_ge(S[f"{name}{k}"], 16 * n * ((i + d) // 2 + 1))
                else:
                    pe.wait_ge(S[f"{name}{k}"], pe.snap((i + (d - k)) * (8 * n) + 16 * n))

            def scan(k, count):
                if k == 0:
                    wait(pe, "l_c1", count(-3))
                    wait(pe, "l_po", count(-2))
                else:
                    wait(pe, "l_c0", count(-2))
                for g in range(3):
                    last = mm(RB[:, 0, g * P + k * SEQ:g * P + k * SEQ + 96], u_half[:, g * P:(g + 1) * P], cst[k][:, :],
                              start=False, stop=True, skip_group_check=True)
                last.then_inc(S[f"l_u{k}_mm"], 1)

            def step(i, j):
                a = j % 2
                f, m, r = (a + 1) % 2, a, (a + 1) % 2
                count = counter(pe, i)
                has = lambda d: not isinstance(i, int) or 0 <= i + d < NP
                if has(0):
                    wait(pe, "xn0", count(1))
                    wait(pe, "a_x1", count(0))
                    transposed(TA[:, 0, 0:P], xn[0][a][:, :]).then_inc(S["a_xT_mm"], 1)
                if has(-2):
                    wait(pe, "xn2", count(-1))
                    wait(pe, "m_clamp", count(-2))
                    transposed(MB[:, 0, 0:P], xn[2][m][:, :]).then_inc(S["m_xT_mm"], 1)
                if has(0):
                    wait(pe, "a_xT", count(1))
                    buffered("ld_x", i, 0, a, 2)
                    wait(pe, "a_o9", count(0))
                    mm(SS[:, 0, 0:P], A_("wq"), xT[0][a][:, :], start=True, stop=True)
                    mm(TA[:, 0, 2 * P:3 * P], A_("wk"), ctxT_a[a][:, :], start=True, stop=True)
                    mm(TA[:, 0, 3 * P:4 * P], ctxT_a[a][:, :], A_("wv"), start=True, stop=True).then_inc(S["a_qkv_mm"], 1)
                if has(-2):
                    wait(pe, "m_qs", count(-1))
                    buffered("ld_m", i, -2, m, 7)
                    mm(MB[0:40, 0, P:2 * P], wm[:, WM["gx"][0]:WM["gx"][1]], xT[2][m][:, :], start=True, stop=False)
                    mm(MB[0:40, 0, P:2 * P], gkv[:, :], ctxT_m[m][:, :], start=False, stop=True).then_inc(S["m_gate_mm"], 1)
                if has(0):
                    wait(pe, "a_kv", count(1))
                    for u in range(2):
                        wait(pe, f"a_qm{u}", count(1))
                        for k in range(4):
                            last = mm(SS[:, u, k * P:(k + 1) * P], qm[a][:, u, 2 * k:2 * k + 2, :].rearrange("p h t -> p (h t)"),
                                      kb[a][:, u, :], start=True, stop=True)
                        last.then_inc(S[f"a_s{u}_mm"], 1)
                if has(-1):
                    wait(pe, "xn1", count(0))
                    wait(pe, "f_acc8", count(-1))
                    transposed(FB[:, 0, 0:P], xn[1][f][:, :]).then_inc(S["f_xT_mm"], 1)
                    wait(pe, "f_xT", count(0))
                    mm(FB[:, 1, 0:96], xT[1][f][:, :], F_("router", w=96), start=True, stop=True).then_inc(S["f_logit_mm"], 1)
                    for n, w in enumerate(("sw1", "sw3")):
                        for c in range(2):
                            last = mm(FB[:, 0, (2 * n + c) * P:(2 * n + c + 1) * P], F_(w, c), xT[1][f][:, :], start=True, stop=True)
                    last.then_inc(S["f_hs_mm"], 1)
                if has(-2):
                    wait(pe, "m_qm", count(-1))
                    wait(pe, "m_h17", count(-2))
                    for u in range(2):
                        last = mm(MB[:, 1, u * 256:(u + 1) * 256], kb1[m][:, u, :], qm1[m][:, u, :, :].rearrange("p h t -> p (h t)"),
                                  start=True, stop=True)
                    last.then_inc(S["m_s_mm"], 1)
                if has(0):
                    for u in range(2):
                        wait(pe, f"a_exp{u}", count(1))
                        for k in range(4):
                            last = transposed(SS[:, u, k * P:(k + 1) * P], ex[a][:, u, k * P:(k + 1) * P])
                        last.then_inc(S[f"a_pT{u}_mm"], 1)
                if has(-1):
                    wait(pe, "f_logit", count(0))
                    for e in range(4):
                        last = mm(FB[:, 1, e * P:(e + 1) * P], F_("ew1", e), xT[1][f][:, :], start=True, stop=True)
                    last.then_inc(S["f_he0_mm"], 1)
                if has(-2):
                    buffered("rows", i, -2, m, 2)
                    wait(pe, "m_a", count(-1))
                    mm(MB[:, 0, :], ldl[m][0:98, :], ldr[m][0:98, :], start=True, stop=True).then_inc(S["m_ld_mm"], 1)
                if has(0):
                    for u in range(2):
                        wait(pe, f"a_pT{u}", count(1))
                        for k in range(4):
                            c = (4 * u + k) * W0
                            last = mm(SS[:, u, k * 96:(k + 1) * 96].rearrange("p (b w) -> p b w", b=2), pT[a][:, u, k * P:(k + 1) * P],
                                      v0[a][:, :, c:c + WIN], start=True, stop=True)
                    last.then_inc(S["a_pv_mm"], 1)
                if has(-3):
                    wait(pe, "xn3", count(-2))
                    wait(pe, "l_g1", count(-3))
                    transposed(RB[:, 0, 3 * P:4 * P], xn[3][r][:, :]).then_inc(S["l_xT_mm"], 1)
                    wait(pe, "l_xT", count(-2))
                    for g, w in enumerate(("wf", "wi", "wc")):
                        mm(RB[:, 0, g * P:(g + 1) * P], R_(w), xT[3][r][:, :], start=g == 0, stop=True, skip_group_check=True)
                    mm(RB[:, 0, 3 * P:4 * P], xT[3][r][:, :], R_("wy"), start=False, stop=True, skip_group_check=True).then_inc(S["l_xw_mm"], 1)
                if has(-2):
                    wait(pe, "m_c", count(-1))
                    for k in range(4):
                        last = mm(MB[:, 1, k * 96:(k + 1) * 96].rearrange("p (b w) -> p b w", b=2), cc[m][:, k * P:(k + 1) * P],
                                  v1[m][:, :, k * W1:k * W1 + WIN], start=True, stop=True)
                    last.then_inc(S["m_cv_mm"], 1)
                    wait(pe, "m_neg", count(-1))
                    transposed(MB[:, 0, 0:P], nsum[m][:, :]).then_inc(S["m_nT_mm"], 1)
                if has(-3):
                    scan(0, count)
                if has(-1):
                    wait(pe, "f_hs", count(0))
                    for c in range(2):
                        last = mm(FB[:, 0, 0:P], hs[f][:, c * P:(c + 1) * P], F_("sw2", c), start=c == 0, stop=c == 1)
                    last.then_inc(S["f_ys_mm"], 1)
                    wait(pe, "f_acc0", count(0))
                    for e in range(4):
                        last = mm(FB[:, 0, e * P:(e + 1) * P], F_("ew1", 4 + e), xT[1][f][:, :], start=True, stop=True)
                    last.then_inc(S["f_he1_mm"], 1)
                    wait(pe, "f_ge0", count(0))
                    for e in range(4):
                        last = mm(FB[:, 1, e * P:(e + 1) * P], he[f][:, e * P:(e + 1) * P], F_("ew2", e), start=True, stop=True)
                    last.then_inc(S["f_y0_mm"], 1)
                if has(0):
                    wait(pe, "a_on", count(1))
                    transposed(TA[:, 0, 0:P], on_buf[a][:, :]).then_inc(S["a_oT_mm"], 1)
                    wait(pe, "a_oT", count(1))
                    mm(TA[:, 0, P:2 * P], oT[a][:, :], A_("wo"), start=True, stop=True).then_inc(S["a_proj_mm"], 1)
                if has(-3):
                    scan(1, count)
                if has(-1):
                    wait(pe, "f_ge1", count(0))
                    for e in range(4):
                        last = mm(FB[:, 0, e * P:(e + 1) * P], he[f][:, (4 + e) * P:(5 + e) * P], F_("ew2", 4 + e), start=True, stop=True)
                    last.then_inc(S["f_y1_mm"], 1)
            steps(pe, step)
            pe.wait_ge(S["t_dup"], 1)
            mm(TA[:, 0, 0:P], cdup[:, :], u_half[:, 3 * P:4 * P], start=True, stop=True).then_inc(S["t_rr_mm"], 1)


def constants():
    ident = np.eye(P, dtype=np.float32)
    rows = np.arange(P)
    head0 = (rows[:, None] % SEQ // 8 == np.arange(8)).astype(np.float32)
    head1 = (rows[:, None] % SEQ // 16 == np.arange(4)).astype(np.float32)
    earlier = np.tile((np.arange(8)[None, :] < np.arange(8)[:, None]).astype(np.float32).reshape(1, 64), (P, 1))
    keep = np.ones((P, P), np.float32)
    keep[:, SEQ] = 0
    floor = np.zeros((P, P), np.float32)
    floor[:, SEQ] = LOWEST
    ldl = np.zeros((P, P), np.float32)
    ldl[0:SEQ] = np.tile(np.eye(SEQ, dtype=np.float32), (1, 2))
    ldl[96, 0:SEQ] = 1
    ldl[97, SEQ:P] = 1
    ldr = np.zeros((P, 8, SEQ), np.float32)
    t = np.arange(SEQ)
    ldr[0:SEQ] = np.where(t[:, None] > t[None, :], BIG, 0.0)[:, None, :]
    ldr[64 + np.arange(8), np.arange(8)] = 1
    return {"one": np.ones((P, 1), np.float32), "mhalf": np.full((P, 8), -0.5, np.float32), "head0": head0, "head1": head1,
            "earlier": earlier, "ident": ident, "keep": keep, "floor": floor, "ldl": ldl, "ldr": ldr.reshape(P, 512)}


def kernel(**inputs):
    import concourse.bacc as bacc
    from concourse.bass_utils import run_bass_kernel_spmd as run

    a = {k: np.asarray(v) for k, v in inputs.items()}
    col = lambda n: a[n].reshape(P, 1)
    row = lambda n: np.broadcast_to(a[n].reshape(1, -1), (P, a[n].size))

    def pack(parts, names):
        return np.ascontiguousarray(np.concatenate([parts[n] for n, _ in names], axis=1))

    def at_rows(v, *starts):
        out = np.zeros((P, 1), np.float32)
        for s in starts:
            out[s:s + 8, 0] = v
        return out

    router = np.zeros((P, 96), np.float32)
    router[:, 0:EXPERTS] = a["L0_ffn_router_w"].T
    flat = lambda n: a[n].transpose(1, 0, 2).reshape(P, EXPERTS * P)
    gates = {}
    for k, n in enumerate(("gx", "gk", "gv")):
        gates[n] = np.zeros((P, 40), np.float32)
        gates[n][:, 0:8] = a["L1_xattn_igate_w"][:, k * P:(k + 1) * P].T
        gates[n][:, 32:40] = a["L1_xattn_fgate_w"][:, k * P:(k + 1) * P].T
    x = np.ascontiguousarray(a["x"].reshape(NP * P, P))
    ctx = np.ascontiguousarray(a["ctx_1024"].reshape(NP * P, P))
    arrays = {
        "x": x, "ctxT": np.ascontiguousarray(ctx.T), "ctx": ctx,
        "wa": pack({k: a[f"L0_xattn_{k}"].T for k in ("wq", "wk", "wv", "wo")}, WEIGHTS_A),
        "wf": pack({"router": router, "sw1": a["L0_ffn_sw1"], "sw3": a["L0_ffn_sw3"],
                    "sw2": a["L0_ffn_sw2"].reshape(2, P, P).transpose(1, 0, 2).reshape(P, 2 * P),
                    "ew1": flat("L0_ffn_ew1"), "ew2": flat("L0_ffn_ew2")}, WEIGHTS_F),
        "wm": pack(gates, WEIGHTS_M),
        "wr": pack({"wf": a["L1_ffn_wf"].T, "wi": a["L1_ffn_wi"].T, "wc": a["L1_ffn_wc"].T, "wy": a["L1_ffn_wo"].T,
                    "uf": a["L1_ffn_uf"].T, "ui": a["L1_ffn_ui"].T, "uc": a["L1_ffn_uc"].T, "uy": a["L1_ffn_uo"].T}, WEIGHTS_R),
        "co": pack({"bq": col("L0_xattn_bq"), "bk": col("L0_xattn_bk"), "bv": col("L0_xattn_bv"),
                    "bf": col("L1_ffn_bf"), "bi": col("L1_ffn_bi"), "bc": col("L1_ffn_bc"), "c0": col("L1_ffn_in_c"),
                    "igb": at_rows(a["L1_xattn_igate_b"], 0), "fgb": at_rows(a["L1_xattn_fgate_b"], 0, 32),
                    "gates": np.concatenate([row("g_xattn"), row("g_ffn")], axis=1), "rb": row("L0_ffn_router_bias"),
                    "bo": row("L0_xattn_bo"), "nw": row("L1_xattn_norm_w"), "by": row("L1_ffn_bo"), **constants()}, COLUMNS),
    }
    nc = bacc.Bacc("TRN2", target_bir_lowering=False, num_devices=1)
    args = [nc.dram_tensor(f"in_{n}", v.shape, F32, kind="ExternalInput").ap() for n, v in arrays.items()]
    out = nc.dram_tensor("out", [NP * P, P], F32, kind="ExternalOutput").ap()
    build(nc, *args, out)
    r = run(nc, [{f"in_{n}": v for n, v in arrays.items()}], core_ids=[0])
    return r.results[0]["out"].reshape(NB, SEQ, P)
```

```python
from contextlib import ExitStack

import numpy as np

import concourse.bass as bass
from concourse import mybir

P = 128
SEQ = 64
NB = 32
NP = NB // 2
EXPERTS = 8
BIG = -1.0e30
LOWEST = -3.0e38
W0 = 17
W1 = 33
WIN = 48
V0W = 7 * W0 + WIN
V1W = 3 * W1 + WIN
EPS_LN = 1e-5
EPS_MLSTM = 1e-6

F32 = mybir.dt.float32
ALU = mybir.AluOpType
ACT = mybir.ActivationFunctionType
AX = mybir.AxisListType.X

WEIGHTS_A = [("wq", P), ("wk", P), ("wv", P), ("wo", P)]
WEIGHTS_F = [("router", 96), ("sw1", 2 * P), ("sw3", 2 * P), ("sw2", 2 * P), ("ew1", EXPERTS * P), ("ew2", EXPERTS * P)]
WEIGHTS_M = [("gx", 40), ("gk", 40), ("gv", 40)]
WEIGHTS_R = [("wf", P), ("wi", P), ("wc", P), ("wy", P), ("uf", P), ("ui", P), ("uc", P), ("uy", P)]
COLUMNS = [("bq", 1), ("bk", 1), ("bv", 1), ("bf", 1), ("bi", 1), ("bc", 1), ("c0", 1), ("igb", 1), ("fgb", 1),
           ("one", 1), ("gates", 4), ("mhalf", 8), ("head0", 8), ("head1", 4), ("rb", 8), ("earlier", 64),
           ("bo", P), ("nw", P), ("by", P), ("ident", P), ("keep", P), ("floor", P), ("ldl", P), ("ldr", 4 * P)]


def offsets(names):
    at, out = 0, {}
    for name, width in names:
        out[name] = (at, at + width)
        at += width
    return out, at


WA, WA_N = offsets(WEIGHTS_A)
WF, WF_N = offsets(WEIGHTS_F)
WM, WM_N = offsets(WEIGHTS_M)
WR, WR_N = offsets(WEIGHTS_R)
CO, CO_N = offsets(COLUMNS)

EVENTS = """
xn0_aggr xn0_eps xn0_rstd xn0 xn1_aggr xn1_eps xn1_rstd xn1 xn2_aggr xn2_eps xn2_rstd xn2 xn3_aggr xn3_eps xn3_rstd
xn3 a_xT_mm a_xT a_kv_mm a_q_mm a_qs0 a_qm0 a_qs1 a_qm1 a_k a_s0_mm a_max0 a_sub0 a_exp0 a_pT0_mm a_pT0 a_pv0_mm
a_s1_mm a_max1 a_sub1 a_exp1 a_pT1_mm a_pT1 a_o9 a_rden a_on a_oT_mm a_oT a_proj_mm a_xb a_x1 f_xT_mm f_xT f_logit_mm
f_logit f_hs_mm f_tanh f_silu_half f_hs f_ys_mm f_acc0 f_ge0 f_y0_mm f_ge1 f_y1_mm f_acc1 f_acc2 f_acc4 f_acc5 f_acc6
f_acc8 f_x2 r_plus r_sig r_sel r_cmp r_tie r_beat r_rank r_top r_best r_sum r_guard r_inv r_share f_comb m_xT_mm m_xT
m_qs m_qm m_gate_mm m_abs m_exp m_ln m_logf m_cum m_a m_run m_neg m_s_mm m_ld_mm m_d m_c m_cv_mm m_h17 m_nT_mm m_clamp
m_norm0 m_norm1 m_norm2 m_norm3 m_h m_sum m_cent m_sq m_var m_veps m_rstd m_hn m_hw m_x3 m_kept l_xT_mm l_xT l_xw_mm
l_po l_u0_mm l_g0 l_q0 l_c0 l_u1_mm l_g1 l_q1 l_c1
""".split()


def build(nc, x_d, ctxT_d, ctx_d, wa_d, wf_d, wm_d, wr_d, co_d, out_d):
    with ExitStack() as ctx:
        def sb(name, shape):
            return ctx.enter_context(nc.sbuf_tensor(name, shape, F32))

        S = {name: ctx.enter_context(nc.semaphore(name)) for name in EVENTS}
        for name in ("ld_a ld_w ld_x0 ld_x1 ld_k0 ld_k1 ld_v0 ld_v1 rows0 rows1 "
                     "su_zero su_dve su_act su_pe t_rr_mm t_rr t_dup t_pre t_tanh t_out stored0 stored1").split():
            S[name] = ctx.enter_context(nc.semaphore(name))

        wa, wf, wm, wr, co = (sb(n, [P, w]) for n, w in
                              (("wa", WA_N), ("wf", WF_N), ("wm", WM_N), ("wr", WR_N), ("co", CO_N)))

        def A_(n):
            return wa[:, WA[n][0]:WA[n][1]]

        def F_(n, i=0, w=None):
            a = WF[n][0]
            return wf[:, a + i * P:a + (i + 1) * P] if w is None else wf[:, a:a + w]

        def R_(n):
            return wr[:, WR[n][0]:WR[n][1]]

        def C_(n, rows=slice(0, P)):
            return co[rows, CO[n][0]:CO[n][1]]

        gkv = sb("gkv", [P, 40])
        tg = sb("tg", [P, 4])
        bo_g = sb("bo_g", [P, P])
        nw_g = sb("nw_g", [P, P])
        u_half = sb("u_half", [P, 4 * P])
        b_half = sb("b_half", [P, 2])
        ident = C_("ident")

        def two(name, shape):
            return [sb(f"{name}{k}", shape) for k in range(2)]

        x_in, ctxT_a, ctxT_m = two("x_in", [P, P]), two("ctxT_a", [P, P]), two("ctxT_m", [P, P])
        kb1, v1 = two("kb1", [P, 2, P]), two("v1", [P, 2, V1W])
        xn = [two(f"xn{k}", [P, P]) for k in range(4)]
        st = [two(f"st{k}", [P, 6]) for k in range(4)]
        mv = [two(f"mv{k}", [P, 2]) for k in range(4)]
        ve = [two(f"ve{k}", [P, 1]) for k in range(4)]
        rs = [two(f"rs{k}", [P, 1]) for k in range(4)]
        xT = [two(f"xT{k}", [P, P]) for k in range(4)]
        qs, qm = two("qs", [P, 2, SEQ]), two("qm", [P, 2, 8, SEQ])
        kb, v0 = two("kb", [P, 2, P]), two("v0", [P, 2, V0W])
        mx, ex = two("mx", [P, 2, 8]), two("ex", [P, 2, 4 * P])
        pT, o9 = two("pT", [P, 2, 4 * P]), two("o9", [P, 8, 18])
        rden, on_buf, oT, xb, x1 = two("rden", [P, 16]), two("on", [P, P]), two("oT", [P, P]), two("xb", [P, P]), two("x1", [P, P])
        th, uh, hs = two("th", [P, 2 * P]), two("uh", [P, 2 * P]), two("hs", [P, 2 * P])
        he, acc, x2 = two("he", [P, 8 * P]), two("acc", [P, 9, P]), two("x2", [P, P])
        rt = two("rt", [P, 12, 8])
        rc = two("rc", [P, 3, 64])
        r1c = two("r1c", [P, 4])
        qs1, qm1 = two("qs1", [P, 2, SEQ]), two("qm1", [P, 2, 4, SEQ])
        ga, nsum = two("ga", [8, 8, P]), two("nsum", [P, P])
        ldl, ldr = two("ldl", [P, P]), two("ldr", [P, 4 * P])
        dd, cc, h17 = two("dd", [P, 4 * P]), two("cc", [P, 4 * P]), two("h17", [P, 4, 34])
        n8 = two("n8", [P, 5, 8])
        hm = two("hm", [P, 5, P])
        s8 = two("s8", [P, 5, 8])
        tgate, pp = two("tgate", [P, 3, SEQ]), two("pp", [P, 2, SEQ])
        cst = two("cst", [P, 96])
        x3 = two("x3", [P, P])
        x3_all, po_all = sb("x3_all", [P, NP, P]), sb("po_all", [P, NP, P])
        rr, cdup = sb("rr", [P, P]), sb("cdup", [P, P])
        pre, tt, res = two("pre", [P, 4, P]), two("tt", [P, 4, P]), two("res", [P, 4, P])

        def bank(name, n=1):
            return ctx.enter_context(nc.psum_tensor(name, [P, n, 512], F32))

        TA, SS, FB, MB, RB = bank("TA"), bank("SS", 2), bank("FB", 2), bank("MB", 2), bank("RB")
        block = ctx.enter_context(nc.Block())

        def wait(eng, name, count):
            if not isinstance(count, int):
                eng.wait_ge(S[name], count)
            elif count > 0:
                eng.wait_ge(S[name], min(count, NP))

        def loaded(eng, name, i, d, k, n):
            if not isinstance(i, int):
                eng.wait_ge(S[f"{name}{k}"], eng.snap((i + (d - k)) * (8 * n) + 16 * n))
            elif i + d >= 0:
                eng.wait_ge(S[f"{name}{k}"], 16 * n * ((i + d) // 2 + 1))

        def steps(eng, step):
            for i in range(-1, 7):
                step(i, i)
            with eng.Fori(7, 14, 2) as r:
                for k in range(2):
                    step(r if k == 0 else eng.snap(r + 1), 7 + k)
            for i in range(15, NP + 6):
                step(i, i)

        def counter(eng, i):
            known = {}

            def count(d):
                if d not in known:
                    known[d] = i + d if isinstance(i, int) else eng.snap(i + d)
                return known[d]
            return count

        @block.sync
        def _(sp):
            sp.dma_start(co[:, :], co_d).then_inc(S["ld_a"], 16)
            sp.dma_start(wa[:, :], wa_d).then_inc(S["ld_a"], 16)

            sp.dma_start(wf[:, :], wf_d).then_inc(S["ld_w"], 16)
            sp.dma_start(wm[:, :], wm_d).then_inc(S["ld_w"], 16)
            sp.dma_start(wr[:, :], wr_d).then_inc(S["ld_w"], 16)
            sp.wait_ge(S["su_zero"], 4)

            def step(i, j):
                cur, oth = j % 2, (j + 1) % 2
                count = counter(sp, i)
                has = lambda d: not isinstance(i, int) or 0 <= i + d < NP
                fixed = isinstance(i, int)
                for d in range(-6 - 1, 2):
                    count(d)

                def tokens(d, b=None):
                    n = P if b is None else SEQ
                    at = (i + d) * P + (b or 0) * SEQ
                    return slice(at, at + n) if fixed else bass.ds(sp.snap(at), n)

                at = {d: (tokens(d), tokens(d, 0), tokens(d, 1)) for d in (-4, -3, 1) if has(d)}

                def load_x(d, k):
                    sp.dma_start(x_in[k][:, :], x_d[at[d][0], :]).then_inc(S[f"ld_x{k}"], 16)
                    sp.dma_start(ctxT_a[k][:, :], ctxT_d[:, at[d][0]]).then_inc(S[f"ld_x{k}"], 16)

                def load_keys(d, k):
                    sp.dma_start(ctxT_m[k][:, :], ctxT_d[:, at[d][0]]).then_inc(S[f"ld_k{k}"], 16)
                    for b in range(2):
                        q = slice(b * SEQ, (b + 1) * SEQ)
                        sp.dma_start(kb1[k][q, :, q], ctxT_d[:, at[d][1 + b]].rearrange("(u d) t -> d u t", u=2)).then_inc(S[f"ld_k{k}"], 16)

                def load_values(d, k):
                    for b in range(2):
                        for h in range(2):
                            sp.dma_start(v1[k][b * SEQ:(b + 1) * SEQ, b, 0:4 * W1].rearrange("t (h w) -> t h w", w=W1)[:, :, 17 * h:17 * h + 16],
                                         ctx_d[at[d][1 + b], :].rearrange("t (h w) -> t h w", w=32)[:, :, 16 * h:16 * h + 16])\
                              .then_inc(S[f"ld_v{k}"], 16)

                def copy_rows(d, k):
                    for b in range(2):
                        sp.dma_start(ldr[k][96 + b:97 + b, :].rearrange("o (h s) -> o h s", h=8),
                                     ga[k][:, 6, b * SEQ:(b + 1) * SEQ]).then_inc(S[f"rows{k}"], 16)

                if has(-4):
                    wait(sp, "m_neg", count(-3))
                    copy_rows(-4, cur)
                if has(-3):
                    load_keys(-3, oth)
                if has(-4):
                    load_values(-4, cur)
                if has(1):
                    wait(sp, "a_xb", count(0))
                    load_x(1, oth)
            steps(sp, step)
            sp.wait_ge(S["stored0"], 2 * 16)
            sp.wait_ge(S["stored1"], 2 * 16)

        @block.gpsimd
        def _(pool):
            for k in range(2):
                nc.gpsimd.memset(kb[k][:, :, :], 0.0)
                nc.gpsimd.memset(v0[k][:, :, :], 0.0)
                nc.gpsimd.memset(kb1[k][:, :, :], 0.0)
                nc.gpsimd.memset(cst[k][:, :], 0.0)
                nc.gpsimd.memset(nsum[k][:, :], 0.0)
                nc.gpsimd.memset(v1[k][:, :, :], 0.0).then_inc(S["su_zero"], 1)
            pool.wait_ge(S["su_zero"], 2)
            for k in range(2):
                for b in range(2):
                    q = slice(b * SEQ, (b + 1) * SEQ)
                    nc.gpsimd.memset(v0[k][q, b, 0:8 * W0].rearrange("t (h w) -> t h w", w=W0)[:, :, 8:9], 1.0)
                    last = nc.gpsimd.memset(v1[k][q, b, 0:4 * W1].rearrange("t (h w) -> t h w", w=W1)[:, :, 16:17], 1.0)
                last.then_inc(S["su_zero"], 1)
            pool.wait_ge(S["su_dve"], 3)

            heads = lambda t: t.rearrange("p (h w) -> p h w", w=16)
            each = lambda t: t.unsqueeze(2).to_broadcast([P, 8, 16])

            def step(i, j):
                cur, oth = j % 2, (j + 1) % 2
                count = counter(pool, i)
                has = lambda d: not isinstance(i, int) or 0 <= i + d < NP
                if has(-3):
                    wait(pool, "xn1_eps", count(-2))
                    nc.gpsimd.tensor_tensor(rs[1][oth][:, :], ve[1][oth][:, :], C_("mhalf")[:, 0:1], ALU.pow).then_inc(S["xn1_rstd"], 1)
                if has(-2):
                    nc.gpsimd.tensor_tensor(xb[cur][:, :], x_in[cur][:, :], bo_g[:, :], ALU.add).then_inc(S["a_xb"], 1)
                if has(-4):
                    wait(pool, "xn2_eps", count(-3))
                    nc.gpsimd.tensor_tensor(rs[2][cur][:, :], ve[2][cur][:, :], C_("mhalf")[:, 0:1], ALU.pow).then_inc(S["xn2_rstd"], 1)
                if has(-1):
                    wait(pool, "xn0_eps", count(0))
                    nc.gpsimd.tensor_tensor(rs[0][oth][:, :], ve[0][oth][:, :], C_("mhalf")[:, 0:1], ALU.pow).then_inc(S["xn0_rstd"], 1)
                if has(-6):
                    wait(pool, "xn3_eps", count(-5))
                    nc.gpsimd.tensor_tensor(rs[3][cur][:, :], ve[3][cur][:, :], C_("mhalf")[:, 0:1], ALU.pow).then_inc(S["xn3_rstd"], 1)
                if has(-5):
                    wait(pool, "m_cent", count(-4))
                    nc.gpsimd.tensor_tensor(hm[oth][:, 2, :], hm[oth][:, 1, :], hm[oth][:, 1, :], ALU.mult).then_inc(S["m_sq"], 1)
                if has(-4):
                    wait(pool, "m_qs", count(-3))
                    nc.gpsimd.tensor_tensor(qm1[cur][:, :, :, :], qs1[cur][:, :, :].unsqueeze(2).to_broadcast([P, 2, 4, SEQ]),
                                            C_("head1").unsqueeze(1).unsqueeze(3).to_broadcast([P, 2, 4, SEQ]), ALU.mult).then_inc(S["m_qm"], 1)
                if has(-5):
                    wait(pool, "m_veps", count(-4))
                    nc.gpsimd.tensor_tensor(s8[oth][:, 4, :], s8[oth][:, 3, :], C_("mhalf"), ALU.pow).then_inc(S["m_rstd"], 1)
                    wait(pool, "m_rstd", count(-4))
                    nc.gpsimd.tensor_tensor(heads(hm[oth][:, 3, :]), heads(hm[oth][:, 1, :]), each(s8[oth][:, 4, :]), ALU.mult).then_inc(S["m_hn"], 1)
                    wait(pool, "m_hn", count(-4))
                    nc.gpsimd.tensor_tensor(hm[oth][:, 4, :], hm[oth][:, 3, :], nw_g[:, :], ALU.mult).then_inc(S["m_hw"], 1)
                if has(-1):
                    wait(pool, "a_qs1", count(0))
                    nc.gpsimd.tensor_tensor(qm[oth][:, 1, :, :], qs[oth][:, 1, :].unsqueeze(1).to_broadcast([P, 8, SEQ]),
                                            C_("head0").unsqueeze(2).to_broadcast([P, 8, SEQ]), ALU.mult).then_inc(S["a_qm1"], 1)
                    wait(pool, "a_qs0", count(0))
                    nc.gpsimd.tensor_tensor(qm[oth][:, 0, :, :], qs[oth][:, 0, :].unsqueeze(1).to_broadcast([P, 8, SEQ]),
                                            C_("head0").unsqueeze(2).to_broadcast([P, 8, SEQ]), ALU.mult).then_inc(S["a_qm0"], 1)
                if has(-3):
                    wait(pool, "f_acc8", count(-2))
                    nc.gpsimd.tensor_tensor(x2[oth][:, :], acc[oth][:, 7, :], acc[oth][:, 8, :], ALU.add).then_inc(S["f_x2"], 1)
            steps(pool, step)

        @block.scalar
        def _(act):
            act.wait_ge(S["ld_a"], 32)
            nc.scalar.activation(tg[:, :], C_("gates"), ACT.Tanh).then_inc(S["su_act"], 1)

            def step(i, j):
                cur, oth = j % 2, (j + 1) % 2
                count = counter(act, i)
                has = lambda d: not isinstance(i, int) or 0 <= i + d < NP
                if has(-2):
                    wait(act, "f_logit_mm", count(-1))
                    nc.scalar.activation(rt[cur][:, 0, :], FB[:, 1, 0:EXPERTS], ACT.Exp, scale=-1.0).then_inc(S["f_logit"], 1)
                if has(-4):
                    wait(act, "m_cv_mm", count(-3))
                    cv = MB[:, 1, 0:4 * 96].rearrange("p (k b w) -> p k b w", k=4, b=2)
                    for h in range(2):
                        for b in range(2):
                            last = nc.scalar.copy(h17[cur][b * SEQ:(b + 1) * SEQ, :, 17 * h:17 * h + 17],
                                                  cv[h * SEQ:(h + 1) * SEQ, :, b, 16 * h:16 * h + 17])
                    last.then_inc(S["m_h17"], 1)
                if has(-1):
                    wait(act, "a_sub0", count(0))
                    nc.scalar.activation(ex[oth][:, 0, :], ex[oth][:, 0, :], ACT.Exp, scale=8.0 ** -0.5).then_inc(S["a_exp0"], 1)
                if has(-3):
                    wait(act, "m_gate_mm", count(-2))
                    nc.scalar.activation(ga[oth][:, 0, :], MB[32:40, 0, 0:P], ACT.Abs, bias=C_("fgb", slice(32, 40))).then_inc(S["m_abs"], 1)
                if has(-1):
                    wait(act, "a_pT1_mm", count(0))
                    nc.scalar.copy(pT[oth][:, 1, :], SS[:, 1, :]).then_inc(S["a_pT1"], 1)
                if has(-3):
                    wait(act, "m_abs", count(-2))
                    nc.scalar.activation(ga[oth][:, 1, :], ga[oth][:, 0, :], ACT.Exp, scale=-1.0).then_inc(S["m_exp"], 1)
                if has(-5):
                    wait(act, "l_xT_mm", count(-4))
                    nc.scalar.copy(xT[3][oth][:, :], RB[:, 0, 3 * P:4 * P]).then_inc(S["l_xT"], 1)
                if has(-1):
                    wait(act, "a_pT0_mm", count(0))
                    nc.scalar.copy(pT[oth][:, 0, :], SS[:, 0, :]).then_inc(S["a_pT0"], 1)
                if has(-3):
                    wait(act, "m_exp", count(-2))
                    nc.scalar.activation(ga[oth][:, 2, :], ga[oth][:, 1, :], ACT.Ln, bias=C_("one", slice(0, 8))).then_inc(S["m_ln"], 1)
                act.preload_act_table(ACT.Gelu)
                if has(-2):
                    nc.scalar.activation(he[cur][:, 4 * P:8 * P], FB[:, 0, :], ACT.Gelu).then_inc(S["f_ge1"], 1)
                if has(-1):
                    wait(act, "a_pv0_mm", count(0))
                    pv = SS[:, :, 0:4 * 96].rearrange("p u (k b w) -> p u k b w", k=4, b=2)
                    o = o9[oth][:, :, :].rearrange("p (u k) w -> p u k w", u=2)
                    for h in range(2):
                        for b in range(2):
                            last = nc.scalar.copy(o[b * SEQ:(b + 1) * SEQ, :, :, 9 * h:9 * h + 9],
                                                  pv[h * SEQ:(h + 1) * SEQ, :, :, b, 8 * h:8 * h + 9])
                    last.then_inc(S["a_o9"], 1)
                if has(-5):
                    wait(act, "l_xw_mm", count(-4))
                    dst = po_all[:, i - 5, :] if isinstance(i, int) else po_all[:, bass.ds(count(-5), 1), :].rearrange("p o d -> p (o d)")
                    nc.scalar.copy(dst, RB[:, 0, 3 * P:4 * P]).then_inc(S["l_po"], 1)
                if has(-2):
                    nc.scalar.activation(he[cur][:, 0 * P:4 * P], FB[:, 1, :], ACT.Gelu).then_inc(S["f_ge0"], 1)
                if has(-5):
                    dst = x3_all[:, i - 5, :] if isinstance(i, int) else x3_all[:, bass.ds(count(-5), 1), :].rearrange("p o d -> p (o d)")
                    nc.scalar.copy(dst, x3[oth][:, :]).then_inc(S["m_kept"], 1)
                if has(0):
                    wait(act, "a_xT_mm", count(1))
                    nc.scalar.copy(xT[0][cur][:, :], TA[:, 0, 0:P]).then_inc(S["a_xT"], 1)
                if has(-2):
                    wait(act, "f_hs_mm", count(-1))
                    nc.scalar.activation(th[cur][:, :], FB[:, 0, 0:2 * P], ACT.Tanh, scale=0.5).then_inc(S["f_tanh"], 1)
                if has(-5):
                    wait(act, "l_u0_mm", count(-4))
                    for g in range(3):
                        last = nc.scalar.activation(tgate[0][:, g, :], RB[:, 0, g * P + 0:g * P + SEQ], ACT.Tanh,
                                                    bias=b_half[:, g:g + 1] if g < 2 else C_("bc"), scale=0.5 if g < 2 else 1.0)
                    last.then_inc(S["l_g0"], 1)
                if has(0):
                    wait(act, "a_kv_mm", count(1))
                    for b in range(2):
                        q = slice(b * SEQ, (b + 1) * SEQ)
                        v = v0[cur][q, b, 0:8 * W0].rearrange("t (h w) -> t h w", w=W0)
                        s = SS[q, 1, P:2 * P].rearrange("t (h w) -> t h w", w=16)
                        nc.scalar.copy(v[:, :, 0:8], s[:, :, 0:8])
                        last = nc.scalar.copy(v[:, :, 9:17], s[:, :, 8:16])
                if has(-1):
                    wait(act, "a_oT_mm", count(0))
                    nc.scalar.copy(oT[oth][:, :], TA[:, 0, 0:P]).then_inc(S["a_oT"], 1)
                if has(0):
                    wait(act, "a_q_mm", count(1))
                    for b in range(2):
                        w, q = slice(SEQ, 2 * SEQ), slice(b * SEQ, (b + 1) * SEQ)
                        last = nc.scalar.activation(qs[cur][q, 1, :], SS[w, 0, q], ACT.Identity, bias=C_("bq", w))
                    last.then_inc(S["a_qs1"], 1)
                    for u in range(2):
                        for b in range(2):
                            q, w = slice(b * SEQ, (b + 1) * SEQ), slice(u * SEQ, (u + 1) * SEQ)
                            last = nc.scalar.activation(kb[cur][q, u, q], SS[w, 1, q], ACT.Identity, bias=C_("bk", w))
                    last.then_inc(S["a_k"], 1)
                    for b in range(2):
                        w, q = slice(0, SEQ), slice(b * SEQ, (b + 1) * SEQ)
                        last = nc.scalar.activation(qs[cur][q, 0, :], SS[w, 0, q], ACT.Identity, bias=C_("bq", w))
                    last.then_inc(S["a_qs0"], 1)
                if has(-5):
                    wait(act, "l_u1_mm", count(-4))
                    for g in range(3):
                        last = nc.scalar.activation(tgate[1][:, g, :], RB[:, 0, g * P + SEQ:g * P + 2 * SEQ], ACT.Tanh,
                                                    bias=b_half[:, g:g + 1] if g < 2 else C_("bc"), scale=0.5 if g < 2 else 1.0)
                    last.then_inc(S["l_g1"], 1)
                act.preload_act_table_set("natural_log_exp_and_others")
                if has(-3):
                    wait(act, "m_ld_mm", count(-2))
                    nc.scalar.activation(dd[oth][:, :], MB[:, 0, :], ACT.Exp).then_inc(S["m_d"], 1)
                if has(0):
                    wait(act, "a_sub1", count(1))
                    nc.scalar.activation(ex[cur][:, 1, :], ex[cur][:, 1, :], ACT.Exp, scale=8.0 ** -0.5).then_inc(S["a_exp1"], 1)
                if has(-1):
                    wait(act, "f_xT_mm", count(0))
                    nc.scalar.copy(xT[1][oth][:, :], FB[:, 0, 0:P]).then_inc(S["f_xT"], 1)
                if has(-3):
                    wait(act, "m_clamp", count(-2))
                    nc.scalar.activation(n8[oth][:, 1, :], n8[oth][:, 0, :], ACT.Exp)
                if has(-2):
                    wait(act, "m_xT_mm", count(-1))
                    for u in range(2):
                        for b in range(2):
                            last = nc.scalar.copy(qs1[cur][b * SEQ:(b + 1) * SEQ, u, :], MB[u * SEQ:(u + 1) * SEQ, 0, b * SEQ:(b + 1) * SEQ])
                    last.then_inc(S["m_qs"], 1)
                    nc.scalar.copy(xT[2][cur][:, :], MB[:, 0, 0:P]).then_inc(S["m_xT"], 1)
            steps(act, step)

            for g in range(4):
                wait(act, "t_pre", g + 1)
                if g >= 2:
                    wait(act, "t_out", g - 1)
                nc.scalar.activation(tt[g % 2][:, :, :], pre[g % 2][:, :, :], ACT.Tanh).then_inc(S["t_tanh"], 1)
                wait(act, "t_out", g + 1)
                act.dma_start(out_d.rearrange("(n p) d -> p n d", p=P)[:, 4 * g:4 * g + 4, :], res[g % 2][:, :, :]).then_inc(S[f"stored{g % 2}"], 16)

        @block.vector
        def _(dve):
            dve.wait_ge(S["ld_a"], 32)
            dve.wait_ge(S["ld_w"], 48)
            dve.wait_ge(S["su_act"], 1)
            dve.wait_ge(S["su_zero"], 4)
            v = nc.vector
            v.tensor_tensor(gkv[:, :], wm[:, WM["gk"][0]:WM["gk"][1]], wm[:, WM["gv"][0]:WM["gv"][1]], ALU.add)
            v.tensor_scalar(nw_g[:, :], C_("nw"), tg[:, 1:2], None, ALU.mult)
            v.tensor_scalar(u_half[:, :], wr[:, WR["uf"][0]:WR["uy"][1]], 0.5, None, ALU.mult)
            v.tensor_scalar(b_half[:, :], co[:, CO["bf"][0]:CO["bi"][1]], 0.5, None, ALU.mult)
            v.tensor_scalar(cst[0][:, 0:SEQ], C_("c0").to_broadcast([P, SEQ]), 2.0, None, ALU.mult)
            for k in range(2):
                v.tensor_copy(ldl[k][:, :], C_("ldl"))
                last = v.tensor_copy(ldr[k][:, :], C_("ldr"))
            last.then_inc(S["su_dve"], 1)
            dve.wait_ge(S["su_pe"], 1)
            v.tensor_tensor(pre[0][:, 0, :], TA[:, 0, 0:P], C_("bo"), ALU.add).then_inc(S["su_dve"], 1)
            dve.wait_ge(S["su_dve"], 2)
            v.tensor_scalar(bo_g[:, :], pre[0][:, 0, :], tg[:, 0:1], None, ALU.mult).then_inc(S["su_dve"], 1)

            def statistics(n, k, src):
                v.bn_stats(st[n][k][:, :], src)
                dve.drain()
                return v.bn_aggr(mv[n][k][:, :], st[n][k][:, :])

            square = lambda k, n: rc[k][:, n, :].rearrange("p (e o) -> p e o", o=8)
            eight = lambda k, n: n8[k][:, n, :].rearrange("p (k h) -> p k h", h=2)
            heads = lambda t: t.rearrange("p (h w) -> p h w", w=16)
            each = lambda t: t.unsqueeze(2).to_broadcast([P, 8, 16])

            def step(i, j):
                cur, oth = j % 2, (j + 1) % 2
                count = counter(dve, i)
                has = lambda d: not isinstance(i, int) or 0 <= i + d < NP
                if has(0):
                    wait(dve, "xn0_rstd", count(1))
                    v.tensor_scalar(xn[0][cur][:, :], x_in[cur][:, :], mv[0][cur][:, 0:1], rs[0][cur][:, 0:1], ALU.subtract, ALU.mult).then_inc(S["xn0"], 1)
                if has(-2):
                    wait(dve, "r_plus", count(-1))
                    v.reciprocal(rt[cur][:, 2, :], rt[cur][:, 1, :]).then_inc(S["r_sig"], 1)
                if has(-6):
                    wait(dve, "l_g1", count(-5))
                    v.scalar_tensor_tensor(pp[1][:, 0, :], tgate[1][:, 0, :], 1.0, cst[1][:, 0:SEQ], ALU.add, ALU.mult)
                    v.scalar_tensor_tensor(pp[1][:, 1, :], tgate[1][:, 1, :], 1.0, tgate[1][:, 2, :], ALU.add, ALU.mult).then_inc(S["l_q1"], 1)
                if has(-2):
                    wait(dve, "r_sig", count(-1))
                    v.tensor_tensor(rt[cur][:, 3, :], rt[cur][:, 2, :], C_("rb"), ALU.add).then_inc(S["r_sel"], 1)
                if has(-5):
                    wait(dve, "xn3_rstd", count(-4))
                    v.tensor_scalar(xn[3][oth][:, :], x3[oth][:, :], mv[3][oth][:, 0:1], rs[3][oth][:, 0:1], ALU.subtract, ALU.mult).then_inc(S["xn3"], 1)
                if has(-4):
                    wait(dve, "m_h17", count(-3))
                    v.scalar_tensor_tensor(eight(cur, 2), h17[cur][:, :, 16:18], -1.0, h17[cur][:, :, 16:18], ALU.mult, ALU.max).then_inc(S["m_norm0"], 1)
                if has(-2):
                    wait(dve, "r_sel", count(-1))
                    mine = rt[cur][:, 3, :].unsqueeze(2).to_broadcast([P, 8, 8])
                    other = rt[cur][:, 3, :].unsqueeze(1).to_broadcast([P, 8, 8])
                    v.tensor_tensor(square(cur, 0), other, mine, ALU.is_gt)
                    v.tensor_tensor(square(cur, 1), other, mine, ALU.is_ge).then_inc(S["r_cmp"], 1)
                if has(-4):
                    wait(dve, "m_norm0", count(-3))
                    v.tensor_tensor(n8[cur][:, 3, :], n8[cur][:, 2, :], n8[cur][:, 1, :], ALU.max).then_inc(S["m_norm1"], 1)
                if has(-6):
                    wait(dve, "l_q1", count(-5))
                    v.scalar_tensor_tensor(cst[0][:, 0:SEQ], pp[1][:, 0, :], 0.5, pp[1][:, 1, :], ALU.mult, ALU.add).then_inc(S["l_c1"], 1)
                if has(1):
                    loaded(dve, "ld_x", i, 1, oth, 2)
                    statistics(0, oth, x_in[oth][:, :]).then_inc(S["xn0_aggr"], 1)
                if has(-2):
                    wait(dve, "r_cmp", count(-1))
                    v.tensor_tensor(rc[cur][:, 2, :], rc[cur][:, 1, :], C_("earlier"), ALU.mult).then_inc(S["r_tie"], 1)
                if has(1):
                    wait(dve, "xn0_aggr", count(2))
                    v.tensor_scalar(ve[0][oth][:, :], mv[0][oth][:, 1:2], EPS_LN, None, ALU.add).then_inc(S["xn0_eps"], 1)
                if has(-4):
                    wait(dve, "m_norm1", count(-3))
                    v.tensor_scalar(n8[cur][:, 2, :], n8[cur][:, 3, :], EPS_MLSTM, None, ALU.add).then_inc(S["m_norm2"], 1)
                if has(-3):
                    wait(dve, "m_abs", count(-2))
                    v.tensor_scalar(ga[oth][:, 3, :], MB[32:40, 0, 0:P], C_("fgb", slice(32, 40)), 0.0, ALU.add, ALU.min)
                if has(-4):
                    wait(dve, "m_norm2", count(-3))
                    v.reciprocal(n8[cur][:, 4, :], n8[cur][:, 2, :]).then_inc(S["m_norm3"], 1)
                if has(-2):
                    wait(dve, "r_tie", count(-1))
                    v.tensor_tensor(rc[cur][:, 1, :], rc[cur][:, 0, :], rc[cur][:, 2, :], ALU.max).then_inc(S["r_beat"], 1)
                if has(-4):
                    wait(dve, "m_norm3", count(-3))
                    for h in range(2):
                        last = v.tensor_tensor(hm[cur][:, 0, :].rearrange("p (k h w) -> p k h w", h=2, w=16)[:, :, h, :], h17[cur][:, :, 18 * h:18 * h + 16],
                                               eight(cur, 4)[:, :, h:h + 1].to_broadcast([P, 4, 16]), ALU.mult)
                    last.then_inc(S["m_h"], 1)
                if has(-2):
                    wait(dve, "r_beat", count(-1))
                    v.reduce_sum(rt[cur][:, 4, :], square(cur, 1), AX).then_inc(S["r_rank"], 1)
                if has(-3):
                    wait(dve, "m_ln", count(-2))
                    v.tensor_tensor(ga[oth][:, 3, :], ga[oth][:, 3, :], ga[oth][:, 2, :], ALU.subtract).then_inc(S["m_logf"], 1)
                if has(-4):
                    wait(dve, "m_h", count(-3))
                    v.reduce_sum(s8[cur][:, 0, :], heads(hm[cur][:, 0, :]), AX).then_inc(S["m_sum"], 1)
                if has(-2):
                    wait(dve, "r_rank", count(-1))
                    v.tensor_scalar(rt[cur][:, 5, :], rt[cur][:, 4, :], 2.0, None, ALU.is_lt).then_inc(S["r_top"], 1)
                if has(-3):
                    wait(dve, "m_logf", count(-2))
                    v.tensor_tensor_scan(ga[oth][:, 4, :], C_("keep", slice(0, 8)), ga[oth][:, 3, :], 0.0, ALU.mult, ALU.add).then_inc(S["m_cum"], 1)
                if has(-4):
                    wait(dve, "m_sum", count(-3))
                    v.scalar_tensor_tensor(heads(hm[cur][:, 1, :]), each(s8[cur][:, 0, :]), -1.0 / 16, heads(hm[cur][:, 0, :]), ALU.mult, ALU.add).then_inc(S["m_cent"], 1)
                if has(-2):
                    wait(dve, "r_top", count(-1))
                    v.tensor_tensor(rt[cur][:, 6, :], rt[cur][:, 5, :], rt[cur][:, 2, :], ALU.mult).then_inc(S["r_best"], 1)
                if has(-3):
                    wait(dve, "m_cum", count(-2))
                    v.scalar_tensor_tensor(ldl[oth][64:72, :], MB[0:8, 0, 0:P], C_("igb", slice(0, 8)), ga[oth][:, 4, :], ALU.add, ALU.subtract)
                    v.scalar_tensor_tensor(ga[oth][:, 5, :], MB[0:8, 0, 0:P], C_("igb", slice(0, 8)), ga[oth][:, 4, :], ALU.add, ALU.subtract).then_inc(S["m_a"], 1)
                if has(-2):
                    wait(dve, "r_best", count(-1))
                    v.reduce_sum(r1c[cur][:, 0:1], rt[cur][:, 6, :], AX).then_inc(S["r_sum"], 1)
                if has(-4):
                    wait(dve, "m_sq", count(-3))
                    v.reduce_sum(s8[cur][:, 2, :], heads(hm[cur][:, 2, :]), AX).then_inc(S["m_var"], 1)
                if has(-2):
                    wait(dve, "r_sum", count(-1))
                    v.tensor_scalar(r1c[cur][:, 2:3], r1c[cur][:, 0:1], 1e-9, 0.5, ALU.is_le, ALU.mult)
                    v.tensor_scalar(r1c[cur][:, 1:2], r1c[cur][:, 0:1], 1e-9, None, ALU.add).then_inc(S["r_guard"], 1)
                if has(-3):
                    wait(dve, "m_a", count(-2))
                    v.tensor_tensor_scan(ga[oth][:, 7, :], C_("floor", slice(0, 8)), ga[oth][:, 5, :], LOWEST, ALU.add, ALU.max).then_inc(S["m_run"], 1)
                if has(-4):
                    wait(dve, "m_var", count(-3))
                    v.tensor_scalar(s8[cur][:, 3, :], s8[cur][:, 2, :], 1.0 / 16, EPS_LN, ALU.mult, ALU.add).then_inc(S["m_veps"], 1)
                if has(-1):
                    wait(dve, "a_o9", count(0))
                    v.reciprocal(rden[oth][:, :].rearrange("p (k h) -> p k h", h=2), o9[oth][:, :, 8:10]).then_inc(S["a_rden"], 1)
                if has(-2):
                    wait(dve, "r_guard", count(-1))
                    v.reciprocal(r1c[cur][:, 3:4], r1c[cur][:, 1:2]).then_inc(S["r_inv"], 1)
                if has(-3):
                    wait(dve, "m_run", count(-2))
                    v.scalar_tensor_tensor(nsum[oth][0:8, :], ga[oth][:, 4, :], -1.0, ga[oth][:, 7, :], ALU.mult, ALU.subtract)
                    v.tensor_scalar(ga[oth][:, 6, :], ga[oth][:, 7, :], -1.0, None, ALU.mult).then_inc(S["m_neg"], 1)
                if has(-2):
                    wait(dve, "r_inv", count(-1))
                    v.tensor_scalar(rt[cur][:, 7, :], rt[cur][:, 6, :], r1c[cur][:, 3:4], r1c[cur][:, 2:3], ALU.mult, ALU.max).then_inc(S["r_share"], 1)
                if has(-1):
                    wait(dve, "a_rden", count(0))
                    for h in range(2):
                        last = v.tensor_tensor(on_buf[oth][:, :].rearrange("p (k h w) -> p k h w", h=2, w=8)[:, :, h, :], o9[oth][:, :, 10 * h:10 * h + 8],
                                               rden[oth][:, :].rearrange("p (k h) -> p k h", h=2)[:, :, h:h + 1].to_broadcast([P, 8, 8]), ALU.mult)
                    last.then_inc(S["a_on"], 1)
                if has(-2):
                    wait(dve, "f_tanh", count(-1))
                    v.scalar_tensor_tensor(uh[cur][:, :], th[cur][:, :], 1.0, FB[:, 0, 0:2 * P], ALU.add, ALU.mult).then_inc(S["f_silu_half"], 1)
                    wait(dve, "r_share", count(-1))
                    v.scalar_tensor_tensor(rt[cur][:, 9, :], rt[cur][:, 7, :], tg[:, 2:3], rt[cur][:, 5, :], ALU.mult, ALU.mult).then_inc(S["f_comb"], 1)
                    wait(dve, "f_silu_half", count(-1))
                    v.scalar_tensor_tensor(hs[cur][:, :], uh[cur][:, :], 0.5, FB[:, 0, 2 * P:4 * P], ALU.mult, ALU.mult).then_inc(S["f_hs"], 1)
                if has(-5):
                    wait(dve, "l_g0", count(-4))
                    v.scalar_tensor_tensor(pp[0][:, 0, :], tgate[0][:, 0, :], 1.0, cst[0][:, 0:SEQ], ALU.add, ALU.mult)
                    v.scalar_tensor_tensor(pp[0][:, 1, :], tgate[0][:, 1, :], 1.0, tgate[0][:, 2, :], ALU.add, ALU.mult).then_inc(S["l_q0"], 1)
                if has(-2):
                    wait(dve, "f_comb", count(-1))
                    wait(dve, "f_y0_mm", count(-1))
                    v.tensor_scalar(acc[cur][:, 1, :], FB[:, 1, 0:P], rt[cur][:, 9, 0:1], None, ALU.mult).then_inc(S["f_acc1"], 1)
                if has(-5):
                    wait(dve, "l_q0", count(-4))
                    v.scalar_tensor_tensor(cst[1][:, 0:SEQ], pp[0][:, 0, :], 0.5, pp[0][:, 1, :], ALU.mult, ALU.add).then_inc(S["l_c0"], 1)
                if has(-2):
                    wait(dve, "f_acc1", count(-1))
                    v.scalar_tensor_tensor(acc[cur][:, 3, :], FB[:, 1, 2 * P:3 * P], rt[cur][:, 9, 2:3], acc[cur][:, 1, :], ALU.mult, ALU.add)
                    wait(dve, "f_ys_mm", count(-1))
                    v.scalar_tensor_tensor(acc[cur][:, 0, :], FB[:, 0, 0:P], tg[:, 2:3], x1[cur][:, :], ALU.mult, ALU.add).then_inc(S["f_acc0"], 1)
                if has(-1):
                    wait(dve, "a_proj_mm", count(0))
                    v.scalar_tensor_tensor(x1[oth][:, :], TA[:, 0, 0:P], tg[:, 0:1], xb[oth][:, :], ALU.mult, ALU.add).then_inc(S["a_x1"], 1)
                if has(-2):
                    wait(dve, "f_acc0", count(-1))
                    v.scalar_tensor_tensor(acc[cur][:, 2, :], FB[:, 1, 1 * P:2 * P], rt[cur][:, 9, 1:2], acc[cur][:, 0, :], ALU.mult, ALU.add).then_inc(S["f_acc2"], 1)
                if has(-1):
                    wait(dve, "a_x1", count(0))
                    statistics(1, oth, x1[oth][:, :]).then_inc(S["xn1_aggr"], 1)
                if has(-2):
                    wait(dve, "f_acc2", count(-1))
                    v.scalar_tensor_tensor(acc[cur][:, 4, :], FB[:, 1, 3 * P:4 * P], rt[cur][:, 9, 3:4], acc[cur][:, 2, :], ALU.mult, ALU.add).then_inc(S["f_acc4"], 1)
                if has(-4):
                    wait(dve, "m_hw", count(-3))
                    v.tensor_tensor(x3[cur][:, :], hm[cur][:, 4, :], x2[cur][:, :], ALU.add).then_inc(S["m_x3"], 1)
                if has(-2):
                    wait(dve, "f_y1_mm", count(-1))
                    v.scalar_tensor_tensor(acc[cur][:, 5, :], FB[:, 0, 0 * P:1 * P], rt[cur][:, 9, 4:5], acc[cur][:, 3, :], ALU.mult, ALU.add).then_inc(S["f_acc5"], 1)
                    wait(dve, "f_acc4", count(-1))
                    v.scalar_tensor_tensor(acc[cur][:, 6, :], FB[:, 0, 1 * P:2 * P], rt[cur][:, 9, 5:6], acc[cur][:, 4, :], ALU.mult, ALU.add).then_inc(S["f_acc6"], 1)
                    wait(dve, "f_acc5", count(-1))
                    v.scalar_tensor_tensor(acc[cur][:, 7, :], FB[:, 0, 2 * P:3 * P], rt[cur][:, 9, 6:7], acc[cur][:, 5, :], ALU.mult, ALU.add)
                    wait(dve, "f_acc6", count(-1))
                    v.scalar_tensor_tensor(acc[cur][:, 8, :], FB[:, 0, 3 * P:4 * P], rt[cur][:, 9, 7:8], acc[cur][:, 6, :], ALU.mult, ALU.add).then_inc(S["f_acc8"], 1)
                if has(-1):
                    wait(dve, "xn1_aggr", count(0))
                    v.tensor_scalar(ve[1][oth][:, :], mv[1][oth][:, 1:2], EPS_LN, None, ALU.add).then_inc(S["xn1_eps"], 1)
                if has(0):
                    wait(dve, "a_s1_mm", count(1))
                    v.tensor_reduce(mx[cur][:, 1, :], SS[:, 1, :].rearrange("p (g t) -> p g t", t=SEQ), AX, ALU.max).then_inc(S["a_max1"], 1)
                if has(-2):
                    wait(dve, "f_x2", count(-1))
                    statistics(2, cur, x2[cur][:, :]).then_inc(S["xn2_aggr"], 1)
                if has(0):
                    wait(dve, "a_max1", count(1))
                    v.tensor_tensor(ex[cur][:, 1, :].rearrange("p (g t) -> p g t", t=SEQ), SS[:, 1, :].rearrange("p (g t) -> p g t", t=SEQ),
                                    mx[cur][:, 1, :].unsqueeze(2).to_broadcast([P, 8, SEQ]), ALU.subtract).then_inc(S["a_sub1"], 1)
                if has(-2):
                    wait(dve, "xn2_aggr", count(-1))
                    v.tensor_scalar(ve[2][cur][:, :], mv[2][cur][:, 1:2], EPS_LN, None, ALU.add).then_inc(S["xn2_eps"], 1)
                if has(-1):
                    wait(dve, "xn1_rstd", count(0))
                    v.tensor_scalar(xn[1][oth][:, :], x1[oth][:, :], mv[1][oth][:, 0:1], rs[1][oth][:, 0:1], ALU.subtract, ALU.mult).then_inc(S["xn1"], 1)
                if has(-3):
                    wait(dve, "m_d", count(-2))
                    wait(dve, "m_s_mm", count(-2))
                    v.scalar_tensor_tensor(cc[oth][:, :], MB[:, 1, :], 0.25, dd[oth][:, :], ALU.mult, ALU.mult).then_inc(S["m_c"], 1)
                    wait(dve, "m_nT_mm", count(-2))
                    v.tensor_scalar(n8[oth][:, 0, :], MB[:, 0, 0:8], 88.0, None, ALU.min).then_inc(S["m_clamp"], 1)
                if has(-2):
                    wait(dve, "xn2_rstd", count(-1))
                    v.tensor_scalar(xn[2][cur][:, :], x2[cur][:, :], mv[2][cur][:, 0:1], rs[2][cur][:, 0:1], ALU.subtract, ALU.mult).then_inc(S["xn2"], 1)
                if has(0):
                    wait(dve, "a_s0_mm", count(1))
                    v.tensor_reduce(mx[cur][:, 0, :], SS[:, 0, :].rearrange("p (g t) -> p g t", t=SEQ), AX, ALU.max).then_inc(S["a_max0"], 1)
                if has(-4):
                    wait(dve, "m_x3", count(-3))
                    statistics(3, cur, x3[cur][:, :]).then_inc(S["xn3_aggr"], 1)
                if has(0):
                    wait(dve, "a_max0", count(1))
                    v.tensor_tensor(ex[cur][:, 0, :].rearrange("p (g t) -> p g t", t=SEQ), SS[:, 0, :].rearrange("p (g t) -> p g t", t=SEQ),
                                    mx[cur][:, 0, :].unsqueeze(2).to_broadcast([P, 8, SEQ]), ALU.subtract).then_inc(S["a_sub0"], 1)
                if has(-4):
                    wait(dve, "xn3_aggr", count(-3))
                    v.tensor_scalar(ve[3][cur][:, :], mv[3][cur][:, 1:2], EPS_LN, None, ALU.add).then_inc(S["xn3_eps"], 1)
                if has(-1):
                    wait(dve, "f_logit", count(0))
                    v.tensor_scalar(rt[oth][:, 1, :], rt[oth][:, 0, :], 1.0, None, ALU.add).then_inc(S["r_plus"], 1)
            steps(dve, step)

            wait(dve, "l_c1", NP)
            for b in range(2):
                last = v.tensor_copy(cdup[:, b * SEQ:(b + 1) * SEQ], cst[0][:, 0:SEQ])
            last.then_inc(S["t_dup"], 1)
            wait(dve, "t_rr_mm", 1)
            v.tensor_tensor(rr[:, :], TA[:, 0, 0:P], C_("by"), ALU.add).then_inc(S["t_rr"], 1)
            wait(dve, "t_rr", 1)
            wait(dve, "l_po", NP)
            wait(dve, "m_kept", NP)
            for g in range(5):
                if g < 4:
                    if g >= 2:
                        wait(dve, "t_tanh", g - 1)
                    v.tensor_tensor(pre[g % 2][:, :, :], po_all[:, 4 * g:4 * g + 4, :], rr[:, :].unsqueeze(1).to_broadcast([P, 4, P]),
                                    ALU.add).then_inc(S["t_pre"], 1)
                if g >= 1:
                    h = g - 1
                    wait(dve, "t_tanh", h + 1)
                    if h >= 2:
                        dve.wait_ge(S[f"stored{h % 2}"], 16 * (h // 2))
                    v.scalar_tensor_tensor(res[h % 2][:, :, :], tt[h % 2][:, :, :], tg[:, 3:4], x3_all[:, 4 * h:4 * h + 4, :],
                                           ALU.mult, ALU.add).then_inc(S["t_out"], 1)

        @block.tensor
        def _(pe):
            pe.wait_ge(S["ld_a"], 32)
            nc.tensor.matmul(TA[:, 0, 0:P], C_("bv").to_broadcast([P, P]), A_("wo"), start=True, stop=True).then_inc(S["su_pe"], 1)
            pe.wait_ge(S["su_dve"], 3)
            pe.wait_ge(S["ld_w"], 48)
            mm = nc.tensor.matmul

            def transposed(out, src):
                return nc.tensor.transpose(out, src, ident)

            def step(i, j):
                cur, oth = j % 2, (j + 1) % 2
                count = counter(pe, i)
                has = lambda d: not isinstance(i, int) or 0 <= i + d < NP
                if has(-4):
                    wait(pe, "m_d", count(-3))
                    transposed(MB[:, 0, 0:P], nsum[cur][:, :]).then_inc(S["m_nT_mm"], 1)
                if has(-1):
                    wait(pe, "a_qm0", count(0))
                    for k in range(4):
                        last = mm(SS[:, 0, k * P:(k + 1) * P], qm[oth][:, 0, 2 * k:2 * k + 2, :].rearrange("p h t -> p (h t)"),
                                  kb[oth][:, 0, :], start=True, stop=True)
                    last.then_inc(S["a_s0_mm"], 1)
                if has(-2):
                    wait(pe, "xn1", count(-1))
                    transposed(FB[:, 0, 0:P], xn[1][cur][:, :]).then_inc(S["f_xT_mm"], 1)
                if has(-1):
                    wait(pe, "a_exp1", count(0))
                    for k in range(4):
                        last = transposed(SS[:, 1, k * P:(k + 1) * P], ex[oth][:, 1, k * P:(k + 1) * P])
                    last.then_inc(S["a_pT1_mm"], 1)
                if has(-3):
                    wait(pe, "xn2", count(-2))
                    transposed(MB[:, 0, 0:P], xn[2][oth][:, :]).then_inc(S["m_xT_mm"], 1)
                if has(-2):
                    wait(pe, "f_xT", count(-1))
                    mm(FB[:, 1, 0:96], xT[1][cur][:, :], F_("router", w=96), start=True, stop=True).then_inc(S["f_logit_mm"], 1)
                if has(-4):
                    loaded(pe, "ld_v", i, -4, cur, 4)
                    wait(pe, "m_c", count(-3))
                    for k in range(4):
                        last = mm(MB[:, 1, k * 96:(k + 1) * 96].rearrange("p (b w) -> p b w", b=2), cc[cur][:, k * P:(k + 1) * P],
                                  v1[cur][:, :, k * W1:k * W1 + WIN], start=True, stop=True)
                    last.then_inc(S["m_cv_mm"], 1)
                if has(-3):
                    loaded(pe, "ld_k", i, -3, oth, 3)
                    wait(pe, "m_xT", count(-2))
                    mm(MB[0:40, 0, 0:P], wm[:, WM["gx"][0]:WM["gx"][1]], xT[2][oth][:, :], start=True, stop=False)
                    mm(MB[0:40, 0, 0:P], gkv[:, :], ctxT_m[oth][:, :], start=False, stop=True).then_inc(S["m_gate_mm"], 1)
                if has(-2):
                    for e in range(4):
                        last = mm(FB[:, 0, e * P:(e + 1) * P], F_("ew1", 4 + e), xT[1][cur][:, :], start=True, stop=True)
                if has(-1):
                    wait(pe, "a_exp0", count(0))
                    for k in range(4):
                        last = transposed(SS[:, 0, k * P:(k + 1) * P], ex[oth][:, 0, k * P:(k + 1) * P])
                    last.then_inc(S["a_pT0_mm"], 1)
                if has(-5):
                    wait(pe, "xn3", count(-4))
                    transposed(RB[:, 0, 3 * P:4 * P], xn[3][oth][:, :]).then_inc(S["l_xT_mm"], 1)
                if has(-2):
                    for e in range(4):
                        last = mm(FB[:, 1, e * P:(e + 1) * P], F_("ew1", e), xT[1][cur][:, :], start=True, stop=True)
                if has(-1):
                    wait(pe, "a_pT1", count(0))
                    for k in range(4):
                        c = (4 + k) * W0
                        last = mm(SS[:, 1, k * 96:(k + 1) * 96].rearrange("p (b w) -> p b w", b=2), pT[oth][:, 1, k * P:(k + 1) * P],
                                  v0[oth][:, :, c:c + WIN], start=True, stop=True)
                if has(0):
                    wait(pe, "xn0", count(1))
                    transposed(TA[:, 0, 0:P], xn[0][cur][:, :]).then_inc(S["a_xT_mm"], 1)
                if has(-1):
                    wait(pe, "a_pT0", count(0))
                    for k in range(4):
                        c = k * W0
                        last = mm(SS[:, 0, k * 96:(k + 1) * 96].rearrange("p (b w) -> p b w", b=2), pT[oth][:, 0, k * P:(k + 1) * P],
                                  v0[oth][:, :, c:c + WIN], start=True, stop=True)
                    last.then_inc(S["a_pv0_mm"], 1)
                if has(-5):
                    wait(pe, "l_xT", count(-4))
                    for g, w in enumerate(("wf", "wi", "wc")):
                        mm(RB[:, 0, g * P:(g + 1) * P], R_(w), xT[3][oth][:, :], start=g == 0, stop=True, skip_group_check=True)
                    mm(RB[:, 0, 3 * P:4 * P], xT[3][oth][:, :], R_("wy"), start=False, stop=True, skip_group_check=True).then_inc(S["l_xw_mm"], 1)
                if has(-2):
                    wait(pe, "f_ge1", count(-1))
                    for n, w in enumerate(("sw1", "sw3")):
                        for c in range(2):
                            last = mm(FB[:, 0, (2 * n + c) * P:(2 * n + c + 1) * P], F_(w, c), xT[1][cur][:, :], start=True, stop=True)
                    last.then_inc(S["f_hs_mm"], 1)
                if has(-5):
                    wait(pe, "l_c1", count(-5))
                    wait(pe, "l_po", count(-4))
                    for g in range(3):
                        last = mm(RB[:, 0, g * P + 0:g * P + 0 + 96], u_half[:, g * P:(g + 1) * P], cst[0][:, :],
                                  start=False, stop=True, skip_group_check=True)
                    last.then_inc(S["l_u0_mm"], 1)
                if has(0):
                    wait(pe, "a_o9", count(0))
                    mm(SS[:, 1, 0:P], A_("wk"), ctxT_a[cur][:, :], start=True, stop=True)
                    mm(SS[:, 1, P:2 * P], ctxT_a[cur][:, :], A_("wv"), start=True, stop=True).then_inc(S["a_kv_mm"], 1)
                if has(-2):
                    wait(pe, "f_ge0", count(-1))
                    for e in range(0, 4):
                        last = mm(FB[:, 1, (e % 4) * P:(e % 4 + 1) * P], he[cur][:, e * P:(e + 1) * P], F_("ew2", e), start=True, stop=True)
                    last.then_inc(S["f_y0_mm"], 1)
                if has(-1):
                    wait(pe, "a_on", count(0))
                    wait(pe, "a_xT", count(1))
                    transposed(TA[:, 0, 0:P], on_buf[oth][:, :]).then_inc(S["a_oT_mm"], 1)
                if has(0):
                    wait(pe, "a_xT", count(1))
                    mm(SS[:, 0, 0:P], A_("wq"), xT[0][cur][:, :], start=True, stop=True).then_inc(S["a_q_mm"], 1)
                if has(-2):
                    wait(pe, "f_hs", count(-1))
                    for c in range(2):
                        last = mm(FB[:, 0, 0:P], hs[cur][:, c * P:(c + 1) * P], F_("sw2", c), start=c == 0, stop=c == 1)
                    last.then_inc(S["f_ys_mm"], 1)
                if has(-1):
                    wait(pe, "a_oT", count(0))
                    mm(TA[:, 0, 0:P], oT[oth][:, :], A_("wo"), start=True, stop=True).then_inc(S["a_proj_mm"], 1)
                if has(-5):
                    wait(pe, "l_c0", count(-4))
                    for g in range(3):
                        last = mm(RB[:, 0, g * P + SEQ:g * P + SEQ + 96], u_half[:, g * P:(g + 1) * P], cst[1][:, :],
                                  start=False, stop=True, skip_group_check=True)
                    last.then_inc(S["l_u1_mm"], 1)
                if has(-2):
                    wait(pe, "f_acc0", count(-1))
                    for e in range(4, 8):
                        last = mm(FB[:, 0, (e % 4) * P:(e % 4 + 1) * P], he[cur][:, e * P:(e + 1) * P], F_("ew2", e), start=True, stop=True)
                    last.then_inc(S["f_y1_mm"], 1)
                if has(0):
                    wait(pe, "a_k", count(1))
                    wait(pe, "a_qm1", count(1))
                    for k in range(4):
                        last = mm(SS[:, 1, k * P:(k + 1) * P], qm[cur][:, 1, 2 * k:2 * k + 2, :].rearrange("p h t -> p (h t)"),
                                  kb[cur][:, 1, :], start=True, stop=True)
                    last.then_inc(S["a_s1_mm"], 1)
                if has(-3):
                    loaded(pe, "rows", i, -3, oth, 2)
                    mm(MB[:, 0, :], ldl[oth][0:98, :], ldr[oth][0:98, :], start=True, stop=True).then_inc(S["m_ld_mm"], 1)
                    wait(pe, "m_qm", count(-2))
                    for u in range(2):
                        last = mm(MB[:, 1, u * 256:(u + 1) * 256], kb1[oth][:, u, :], qm1[oth][:, u, :, :].rearrange("p h t -> p (h t)"), start=True, stop=True)
                    last.then_inc(S["m_s_mm"], 1)
            steps(pe, step)
            pe.wait_ge(S["t_dup"], 1)
            mm(TA[:, 0, 0:P], cdup[:, :], u_half[:, 3 * P:4 * P], start=True, stop=True).then_inc(S["t_rr_mm"], 1)


def constants():
    ident = np.eye(P, dtype=np.float32)
    rows = np.arange(P)
    head0 = (rows[:, None] % SEQ // 8 == np.arange(8)).astype(np.float32)
    head1 = (rows[:, None] % SEQ // 16 == np.arange(4)).astype(np.float32)
    earlier = np.tile((np.arange(8)[None, :] < np.arange(8)[:, None]).astype(np.float32).reshape(1, 64), (P, 1))
    keep = np.ones((P, P), np.float32)
    keep[:, SEQ] = 0
    floor = np.zeros((P, P), np.float32)
    floor[:, SEQ] = LOWEST
    ldl = np.zeros((P, P), np.float32)
    ldl[0:SEQ] = np.tile(np.eye(SEQ, dtype=np.float32), (1, 2))
    ldl[96, 0:SEQ] = 1
    ldl[97, SEQ:P] = 1
    ldr = np.zeros((P, 8, SEQ), np.float32)
    t = np.arange(SEQ)
    ldr[0:SEQ] = np.where(t[:, None] > t[None, :], BIG, 0.0)[:, None, :]
    ldr[64 + np.arange(8), np.arange(8)] = 1
    return {"one": np.ones((P, 1), np.float32), "mhalf": np.full((P, 8), -0.5, np.float32), "head0": head0, "head1": head1,
            "earlier": earlier, "ident": ident, "keep": keep, "floor": floor, "ldl": ldl, "ldr": ldr.reshape(P, 512)}


def kernel(**inputs):
    import concourse.bacc as bacc
    from concourse.bass_utils import run_bass_kernel_spmd as run

    a = {k: np.asarray(v) for k, v in inputs.items()}
    col = lambda n: a[n].reshape(P, 1)
    row = lambda n: np.broadcast_to(a[n].reshape(1, -1), (P, a[n].size))

    def pack(parts, names):
        return np.ascontiguousarray(np.concatenate([parts[n] for n, _ in names], axis=1))

    def at_rows(v, *starts):
        out = np.zeros((P, 1), np.float32)
        for s in starts:
            out[s:s + 8, 0] = v
        return out

    router = np.zeros((P, 96), np.float32)
    router[:, 0:EXPERTS] = a["L0_ffn_router_w"].T
    flat = lambda n: a[n].transpose(1, 0, 2).reshape(P, EXPERTS * P)
    gates = {}
    for k, n in enumerate(("gx", "gk", "gv")):
        gates[n] = np.zeros((P, 40), np.float32)
        gates[n][:, 0:8] = a["L1_xattn_igate_w"][:, k * P:(k + 1) * P].T
        gates[n][:, 32:40] = a["L1_xattn_fgate_w"][:, k * P:(k + 1) * P].T
    x = np.ascontiguousarray(a["x"].reshape(NP * P, P))
    ctx = np.ascontiguousarray(a["ctx_1024"].reshape(NP * P, P))
    arrays = {
        "x": x, "ctxT": np.ascontiguousarray(ctx.T), "ctx": ctx,
        "wa": pack({k: a[f"L0_xattn_{k}"].T for k in ("wq", "wk", "wv", "wo")}, WEIGHTS_A),
        "wf": pack({"router": router, "sw1": a["L0_ffn_sw1"], "sw3": a["L0_ffn_sw3"],
                    "sw2": a["L0_ffn_sw2"].reshape(2, P, P).transpose(1, 0, 2).reshape(P, 2 * P),
                    "ew1": flat("L0_ffn_ew1"), "ew2": flat("L0_ffn_ew2")}, WEIGHTS_F),
        "wm": pack(gates, WEIGHTS_M),
        "wr": pack({"wf": a["L1_ffn_wf"].T, "wi": a["L1_ffn_wi"].T, "wc": a["L1_ffn_wc"].T, "wy": a["L1_ffn_wo"].T,
                    "uf": a["L1_ffn_uf"].T, "ui": a["L1_ffn_ui"].T, "uc": a["L1_ffn_uc"].T, "uy": a["L1_ffn_uo"].T}, WEIGHTS_R),
        "co": pack({"bq": col("L0_xattn_bq"), "bk": col("L0_xattn_bk"), "bv": col("L0_xattn_bv"),
                    "bf": col("L1_ffn_bf"), "bi": col("L1_ffn_bi"), "bc": col("L1_ffn_bc"), "c0": col("L1_ffn_in_c"),
                    "igb": at_rows(a["L1_xattn_igate_b"], 0), "fgb": at_rows(a["L1_xattn_fgate_b"], 0, 32),
                    "gates": np.concatenate([row("g_xattn"), row("g_ffn")], axis=1), "rb": row("L0_ffn_router_bias"),
                    "bo": row("L0_xattn_bo"), "nw": row("L1_xattn_norm_w"), "by": row("L1_ffn_bo"), **constants()}, COLUMNS),
    }
    nc = bacc.Bacc("TRN2", target_bir_lowering=False, num_devices=1)
    args = [nc.dram_tensor(f"in_{n}", v.shape, F32, kind="ExternalInput").ap() for n, v in arrays.items()]
    out = nc.dram_tensor("out", [NP * P, P], F32, kind="ExternalOutput").ap()
    build(nc, *args, out)
    r = run(nc, [{f"in_{n}": v for n, v in arrays.items()}], core_ids=[0])
    return r.results[0]["out"].reshape(NB, SEQ, P)
```

```python
from contextlib import ExitStack

import numpy as np

import concourse.bass as bass
from concourse import mybir

P = 128
SEQ = 64
NB = 32
NP = NB // 2
EXPERTS = 8
BIG = -1.0e30
LOWEST = -3.0e38
W0 = 17
W1 = 33
WIN = 48
V0W = 7 * W0 + WIN
V1W = 3 * W1 + WIN
EPS_LN = 1e-5
EPS_MLSTM = 1e-6

F32 = mybir.dt.float32
ALU = mybir.AluOpType
ACT = mybir.ActivationFunctionType
AX = mybir.AxisListType.X

EXP_LN, GELU_TANH = "natural_log_exp_and_others", "gelu_and_others"

WEIGHTS_A = [("wq", P), ("wk", P), ("wv", P), ("wo", P)]
WEIGHTS_F = [("router", 96), ("sw1", 2 * P), ("sw3", 2 * P), ("sw2", 2 * P), ("ew1", EXPERTS * P), ("ew2", EXPERTS * P)]
WEIGHTS_M = [("gx", 40), ("gk", 40), ("gv", 40)]
WEIGHTS_R = [("wf", P), ("wi", P), ("wc", P), ("wy", P), ("uf", P), ("ui", P), ("uc", P), ("uy", P)]
COLUMNS = [("ident", P), ("bq", 1), ("bk", 1), ("bv", 1), ("bf", 1), ("bi", 1), ("bc", 1), ("c0", 1), ("igb", 1), ("fgb", 1),
           ("one", 1), ("eps", 1), ("gates", 4), ("mhalf", 8), ("head0", 8), ("head1", 4), ("rb", 8), ("earlier", 64),
           ("bo", P), ("nw", P), ("by", P), ("keep", P), ("floor", P), ("ldl", P), ("ldr", 4 * P)]


def offsets(names):
    at, out = 0, {}
    for name, width in names:
        out[name] = (at, at + width)
        at += width
    return out, at


WA, WA_N = offsets(WEIGHTS_A)
WF, WF_N = offsets(WEIGHTS_F)
WM, WM_N = offsets(WEIGHTS_M)
WR, WR_N = offsets(WEIGHTS_R)
CO, CO_N = offsets(COLUMNS)
SOON = CO["rb"][0]

EVENTS = """
xn0_aggr xn0_eps xn0_rstd xn0 xn1_aggr xn1_eps xn1_rstd xn1 xn2_aggr xn2_eps xn2_rstd xn2 xn3_aggr xn3_eps xn3_rstd
xn3 a_xT_mm a_xT a_kv_mm a_q_mm a_qs0 a_qm0 a_qs1 a_qm1 a_k a_v a_s0_mm a_max0 a_sub0 a_exp0 a_pT0_mm a_pT0 a_s1_mm
a_max1 a_sub1 a_exp1 a_pT1_mm a_pT1 a_pv1_mm a_o9 a_rden a_on a_oT_mm a_oT a_proj_mm a_xb a_x1 f_xT_mm f_xT f_logit_mm
f_logit f_hs_mm f_tanh f_hs f_ys_mm f_acc0 f_he0_mm f_ge0 f_he1_mm f_ge1 f_y1_mm f_acc1 f_acc2 f_acc3 f_acc4 f_acc5
f_acc6 f_acc8 f_x2 r_plus r_sig r_sel r_cmp r_tie r_beat r_rank r_top r_best r_sum r_guard r_inv r_share f_comb
m_xT_mm m_xT m_qs m_qm m_gate_mm m_abs m_exp m_ln m_min m_logf m_cum m_a m_run m_neg m_ld_mm m_d m_c m_cv_mm m_h17
m_nT_mm m_clamp m_norm0 m_norm1 m_norm2 m_norm3 m_h m_sum m_cent m_sq m_var m_veps m_rstd m_hn m_hw m_x3 m_kept
l_xT_mm l_xT l_xw_mm l_po l_u0_mm l_g0 l_q0 l_c0 l_u1_mm l_g1 l_q1 l_c1
""".split()


def build(nc, x_d, ctxT_d, ctxv_d, wa_d, wf_d, wm_d, wr_d, co_d, out_d):
    with ExitStack() as ctx:
        def sb(name, shape):
            return ctx.enter_context(nc.sbuf_tensor(name, shape, F32))

        S = {name: ctx.enter_context(nc.semaphore(name)) for name in EVENTS}
        for name in ("ld_c ld_a ld_w ld_x0 ld_x1 ld_k0 ld_k1 ld_v0 ld_v1 rows0 rows1 "
                     "su_zero su_dve su_act su_pe su_bias t_rr_mm t_rr t_dup t_pre t_pre_pool t_tanh t_out stored").split():
            S[name] = ctx.enter_context(nc.semaphore(name))

        wa, wf, wm, wr, co = (sb(n, [P, w]) for n, w in
                              (("wa", WA_N), ("wf", WF_N), ("wm", WM_N), ("wr", WR_N), ("co", CO_N)))

        def A_(n):
            return wa[:, WA[n][0]:WA[n][1]]

        def F_(n, i=0, w=None):
            a = WF[n][0]
            return wf[:, a + i * P:a + (i + 1) * P] if w is None else wf[:, a:a + w]

        def R_(n):
            return wr[:, WR[n][0]:WR[n][1]]

        def C_(n, rows=slice(0, P)):
            return co[rows, CO[n][0]:CO[n][1]]

        gkv = sb("gkv", [P, 40])
        tg = sb("tg", [P, 4])
        bo_g = sb("bo_g", [P, P])
        nw_g = sb("nw_g", [P, P])
        u_half = sb("u_half", [P, 4 * P])
        b_half = sb("b_half", [P, 2])
        ident = C_("ident")

        def two(name, shape):
            return [sb(f"{name}{k}", shape) for k in range(2)]

        x_in, ctxT_a, ctxT_m = two("x_in", [P, P]), two("ctxT_a", [P, P]), two("ctxT_m", [P, P])
        kb1, v1 = two("kb1", [P, 2, P]), two("v1", [P, 2, V1W])
        xn = [two(f"xn{k}", [P, P]) for k in range(4)]
        st = [two(f"st{k}", [P, 6]) for k in range(4)]
        mv = [two(f"mv{k}", [P, 2]) for k in range(4)]
        ve = [two(f"ve{k}", [P, 1]) for k in range(4)]
        rs = [two(f"rs{k}", [P, 1]) for k in range(4)]
        xT = [two(f"xT{k}", [P, P]) for k in range(4)]
        qs, qm = two("qs", [P, 2, SEQ]), two("qm", [P, 2, 8, SEQ])
        kb, v0 = two("kb", [P, 2, P]), two("v0", [P, 2, V0W])
        mx, ex = two("mx", [P, 2, 8]), two("ex", [P, 2, 4 * P])
        pT, o9 = two("pT", [P, 2, 4 * P]), two("o9", [P, 8, 20])
        rden, on_buf, oT, xb, x1 = two("rden", [P, 16]), two("on", [P, P]), two("oT", [P, P]), two("xb", [P, P]), two("x1", [P, P])
        th, uh, hs = two("th", [P, 2 * P]), two("uh", [P, 2 * P]), two("hs", [P, 2 * P])
        he, acc, x2 = two("he", [P, 8 * P]), two("acc", [P, 9, P]), two("x2", [P, P])
        rt = two("rt", [P, 12, 8])
        rc = two("rc", [P, 3, 64])
        r1c = two("r1c", [P, 4])
        qs1, qm1 = two("qs1", [P, 2, SEQ]), two("qm1", [P, 2, 4, SEQ])
        ga, nsum = two("ga", [8, 6, P]), two("nsum", [P, P])
        ldl, ldr = two("ldl", [P, P]), two("ldr", [P, 4 * P])
        dd, cc, h17 = two("dd", [P, 4 * P]), two("cc", [P, 4 * P]), two("h17", [P, 4, 36])
        n8 = two("n8", [P, 5, 8])
        hm = two("hm", [P, 5, P])
        s8 = two("s8", [P, 5, 8])
        tgate, pp = two("tgate", [P, 3, SEQ]), two("pp", [P, 2, SEQ])
        cst = two("cst", [P, 96])
        x3 = two("x3", [P, P])
        x3_all, po_all = sb("x3_all", [P, NP, P]), sb("po_all", [P, NP, P])
        rr, cdup = sb("rr", [P, P]), sb("cdup", [P, P])
        pre, res = ([sb(f"{n}{g}", [P, 4, P]) for g in range(4)] for n in ("pre", "res"))

        def bank(name, n=1):
            return ctx.enter_context(nc.psum_tensor(name, [P, n, 512], F32))

        TA, SS, FB, MB, RB = bank("TA"), bank("SS", 2), bank("FB", 2), bank("MB", 2), bank("RB")
        block = ctx.enter_context(nc.Block())

        def wait(eng, name, count):
            if not isinstance(count, int):
                eng.wait_ge(S[name], count)
            elif count > 0:
                eng.wait_ge(S[name], min(count, NP))

        def loaded(eng, name, i, d, k, n):
            if not isinstance(i, int):
                eng.wait_ge(S[f"{name}{k}"], eng.snap((i + (d - k)) * (8 * n) + 16 * n))
            elif i + d >= 0:
                eng.wait_ge(S[f"{name}{k}"], 16 * n * ((i + d) // 2 + 1))

        def steps(eng, step):
            for i in range(-1, 9):
                step(i, i)
            with eng.Fori(9, 14, 2) as r:
                for k in range(2):
                    step(r if k == 0 else eng.snap(r + 1), 9 + k)
            for i in range(15, NP + 7):
                step(i, i)

        def counter(eng, i):
            known = {}

            def count(d):
                if d not in known:
                    known[d] = i + d if isinstance(i, int) else eng.snap(i + d)
                return known[d]
            return count

        @block.sync
        def _(sp):

            def step(i, j):
                cur, oth = j % 2, (j + 1) % 2
                count = counter(sp, i)
                has = lambda d: not isinstance(i, int) or 0 <= i + d < NP
                fixed = isinstance(i, int)
                for d in range(-8, 2):
                    count(d)

                def tokens(d, b=None):
                    n = P if b is None else SEQ
                    at = (i + d) * P + (b or 0) * SEQ
                    return slice(at, at + n) if fixed else bass.ds(sp.snap(at), n)

                at = {d: (tokens(d), tokens(d, 0), tokens(d, 1)) for d in (-4, -3, 1) if has(d)}

                def load_x(d, k):
                    sp.dma_start(x_in[k][:, :], x_d[at[d][0], :]).then_inc(S[f"ld_x{k}"], 16)
                    sp.dma_start(ctxT_a[k][:, :], ctxT_d[:, at[d][0]]).then_inc(S[f"ld_x{k}"], 16)
                    if fixed and i + d == 0:
                        sp.dma_start(wa[:, :], wa_d).then_inc(S["ld_a"], 16)
                        sp.dma_start(co[:, SOON:CO_N], co_d[:, SOON:CO_N]).then_inc(S["ld_a"], 16)
                    if fixed and i + d == 1:
                        sp.dma_start(wf[:, :], wf_d).then_inc(S["ld_w"], 16)
                        sp.dma_start(wm[:, :], wm_d).then_inc(S["ld_w"], 16)
                        sp.dma_start(wr[:, :], wr_d).then_inc(S["ld_w"], 16)
                        sp.wait_ge(S["su_zero"], 3)

                def load_keys(d, k):
                    sp.dma_start(ctxT_m[k][:, :], ctxT_d[:, at[d][0]]).then_inc(S[f"ld_k{k}"], 16)
                    for b in range(2):
                        q = slice(b * SEQ, (b + 1) * SEQ)
                        sp.dma_start(kb1[k][q, :, q], ctxT_d[:, at[d][1 + b]].rearrange("(u d) t -> d u t", u=2)).then_inc(S[f"ld_k{k}"], 16)

                def load_values(d, k):
                    for b in range(2):
                        sp.dma_start(v1[k][b * SEQ:(b + 1) * SEQ, b, 0:4 * W1], ctxv_d[at[d][1 + b], :]).then_inc(S[f"ld_v{k}"], 16)

                def copy_rows(d, k):
                    for b in range(2):
                        sp.dma_start(ldr[k][96 + b:97 + b, :].rearrange("o (h s) -> o h s", h=8),
                                     ga[k][:, 4, b * SEQ:(b + 1) * SEQ]).then_inc(S[f"rows{k}"], 16)

                if has(-5):
                    wait(sp, "m_run", count(-4))
                    copy_rows(-5, oth)
                if has(-4):
                    load_keys(-4, cur)
                if has(1):
                    wait(sp, "a_kv_mm", count(0))
                    wait(sp, "a_xb", count(0))
                    load_x(1, oth)
                if has(-3):
                    wait(sp, "m_cv_mm", count(-4))
                    load_values(-3, oth)
            steps(sp, step)
            for g in range(4):
                wait(sp, "t_out", g + 1)
                sp.dma_start(out_d.rearrange("(n p) d -> p n d", p=P)[:, 4 * g:4 * g + 4, :], res[g][:, :, :]).then_inc(S["stored"], 16)
            sp.wait_ge(S["stored"], 4 * 16)

        @block.gpsimd
        def _(pool):
            for k in range(2):
                nc.gpsimd.memset(kb[k][:, :, :], 0.0)
                last = nc.gpsimd.memset(v0[k][:, :, :], 0.0)
            last.then_inc(S["su_zero"], 1)
            pool.wait_ge(S["su_zero"], 1)
            for k in range(2):
                for b in range(2):
                    q = slice(b * SEQ, (b + 1) * SEQ)
                    last = nc.gpsimd.memset(v0[k][q, b, 0:8 * W0].rearrange("t (h w) -> t h w", w=W0)[:, :, 8:9], 1.0)
            last.then_inc(S["su_zero"], 1)
            pool.wait_ge(S["su_zero"], 2)
            for k in range(2):
                nc.gpsimd.memset(kb1[k][:, :, :], 0.0)
                nc.gpsimd.memset(cst[k][:, :], 0.0)
                nc.gpsimd.memset(nsum[k][:, :], 0.0)
                last = nc.gpsimd.memset(v1[k][:, :, :], 0.0)
            last.then_inc(S["su_zero"], 1)
            pool.wait_ge(S["su_zero"], 3)

            heads = lambda t: t.rearrange("p (h w) -> p h w", w=16)
            each = lambda t: t.unsqueeze(2).to_broadcast([P, 8, 16])

            def step(i, j):
                cur, oth = j % 2, (j + 1) % 2
                count = counter(pool, i)
                has = lambda d: not isinstance(i, int) or 0 <= i + d < NP
                if has(-5):
                    wait(pool, "m_veps", count(-4))
                    nc.gpsimd.tensor_tensor(s8[oth][:, 4, :], s8[oth][:, 3, :], C_("mhalf"), ALU.pow).then_inc(S["m_rstd"], 1)
                if has(1):
                    if isinstance(i, int) and i == -1:
                        pool.wait_ge(S["ld_c"], 16)
                    wait(pool, "xn0_aggr", count(2))
                    nc.gpsimd.tensor_tensor(ve[0][oth][:, :], mv[0][oth][:, 1:2], C_("eps"), ALU.add).then_inc(S["xn0_eps"], 1)
                if has(-5):
                    wait(pool, "m_rstd", count(-4))
                    nc.gpsimd.tensor_tensor(heads(hm[oth][:, 3, :]), heads(hm[oth][:, 1, :]), each(s8[oth][:, 4, :]), ALU.mult).then_inc(S["m_hn"], 1)
                if has(-1):
                    wait(pool, "a_rden", count(0))
                    nc.gpsimd.tensor_tensor(on_buf[oth][:, :].rearrange("p (k h w) -> p k h w", h=2, w=8),
                                            o9[oth][:, :, :].rearrange("p k (h w) -> p k h w", h=2)[:, :, :, 0:8],
                                            rden[oth][:, :].rearrange("p (k h) -> p k h", h=2).unsqueeze(3).to_broadcast([P, 8, 2, 8]), ALU.mult).then_inc(S["a_on"], 1)
                if has(-5):
                    wait(pool, "m_hn", count(-4))
                    nc.gpsimd.tensor_tensor(hm[oth][:, 4, :], hm[oth][:, 3, :], nw_g[:, :], ALU.mult).then_inc(S["m_hw"], 1)
                    wait(pool, "m_hw", count(-4))
                    nc.gpsimd.tensor_tensor(x3[oth][:, :], hm[oth][:, 4, :], x2[oth][:, :], ALU.add).then_inc(S["m_x3"], 1)
                if has(0):
                    if isinstance(i, int) and i == 0:
                        pool.wait_ge(S["su_dve"], 1)
                    nc.gpsimd.tensor_tensor(xb[cur][:, :], x_in[cur][:, :], bo_g[:, :], ALU.add).then_inc(S["a_xb"], 1)
                if has(-3):
                    wait(pool, "m_x3", count(-4))
                    wait(pool, "f_acc8", count(-2))
                    nc.gpsimd.tensor_tensor(x2[oth][:, :], acc[oth][:, 7, :], acc[oth][:, 8, :], ALU.add).then_inc(S["f_x2"], 1)
                if has(0):
                    wait(pool, "a_qs0", count(1))
                    nc.gpsimd.tensor_tensor(qm[cur][:, 0, :, :], qs[cur][:, 0, :].unsqueeze(1).to_broadcast([P, 8, SEQ]),
                                            C_("head0").unsqueeze(2).to_broadcast([P, 8, SEQ]), ALU.mult).then_inc(S["a_qm0"], 1)
                if has(-3):
                    wait(pool, "xn2_aggr", count(-2))
                    nc.gpsimd.tensor_tensor(ve[2][oth][:, :], mv[2][oth][:, 1:2], C_("eps"), ALU.add).then_inc(S["xn2_eps"], 1)
                if has(-5):
                    wait(pool, "xn3_aggr", count(-4))
                    nc.gpsimd.tensor_tensor(ve[3][oth][:, :], mv[3][oth][:, 1:2], C_("eps"), ALU.add).then_inc(S["xn3_eps"], 1)
                if has(-3):
                    wait(pool, "xn2_eps", count(-2))
                    nc.gpsimd.tensor_tensor(rs[2][oth][:, :], ve[2][oth][:, :], C_("mhalf")[:, 0:1], ALU.pow).then_inc(S["xn2_rstd"], 1)
                if has(1):
                    wait(pool, "xn0_eps", count(2))
                    nc.gpsimd.tensor_tensor(rs[0][oth][:, :], ve[0][oth][:, :], C_("mhalf")[:, 0:1], ALU.pow).then_inc(S["xn0_rstd"], 1)
                if has(-5):
                    wait(pool, "xn3_eps", count(-4))
                    nc.gpsimd.tensor_tensor(rs[3][oth][:, :], ve[3][oth][:, :], C_("mhalf")[:, 0:1], ALU.pow).then_inc(S["xn3_rstd"], 1)
                if has(0):
                    wait(pool, "a_qs1", count(1))
                    nc.gpsimd.tensor_tensor(qm[cur][:, 1, :, :], qs[cur][:, 1, :].unsqueeze(1).to_broadcast([P, 8, SEQ]),
                                            C_("head0").unsqueeze(2).to_broadcast([P, 8, SEQ]), ALU.mult).then_inc(S["a_qm1"], 1)
                if has(-1):
                    wait(pool, "xn1_aggr", count(0))
                    nc.gpsimd.tensor_tensor(ve[1][oth][:, :], mv[1][oth][:, 1:2], C_("eps"), ALU.add).then_inc(S["xn1_eps"], 1)
                    wait(pool, "xn1_eps", count(0))
                    nc.gpsimd.tensor_tensor(rs[1][oth][:, :], ve[1][oth][:, :], C_("mhalf")[:, 0:1], ALU.pow).then_inc(S["xn1_rstd"], 1)
                if has(-3):
                    wait(pool, "m_qs", count(-2))
                    nc.gpsimd.tensor_tensor(qm1[oth][:, :, :, :], qs1[oth][:, :, :].unsqueeze(2).to_broadcast([P, 2, 4, SEQ]),
                                            C_("head1").unsqueeze(1).unsqueeze(3).to_broadcast([P, 2, 4, SEQ]), ALU.mult).then_inc(S["m_qm"], 1)
                if has(-4):
                    wait(pool, "m_norm3", count(-3))
                    nc.gpsimd.tensor_tensor(hm[cur][:, 0, :].rearrange("p (k h w) -> p k h w", h=2, w=16),
                                            h17[cur][:, :, :].rearrange("p k (h w) -> p k h w", h=2)[:, :, :, 0:16],
                                            n8[cur][:, 4, :].rearrange("p (k h) -> p k h", h=2).unsqueeze(3).to_broadcast([P, 4, 2, 16]), ALU.mult).then_inc(S["m_h"], 1)
                    wait(pool, "m_cent", count(-3))
                    nc.gpsimd.tensor_tensor(hm[cur][:, 2, :], hm[cur][:, 1, :], hm[cur][:, 1, :], ALU.mult).then_inc(S["m_sq"], 1)
            steps(pool, step)
            wait(pool, "t_rr", 1)
            wait(pool, "l_po", NP)
            for g in range(2, 4):
                nc.gpsimd.tensor_tensor(pre[g][:, :, :], po_all[:, 4 * g:4 * g + 4, :], rr[:, :].unsqueeze(1).to_broadcast([P, 4, P]),
                                        ALU.add).then_inc(S["t_pre_pool"], 1)

        @block.scalar
        def _(act):
            act.dma_start(co[:, 0:SOON], co_d[:, 0:SOON]).then_inc(S["ld_c"], 16)
            act.wait_ge(S["ld_c"], 16)
            nc.scalar.activation(tg[:, :], C_("gates"), ACT.Tanh).then_inc(S["su_act"], 1)

            held = [None]

            def table(name):
                if held[0] != name:
                    if name == GELU_TANH:
                        act.preload_act_table(ACT.Gelu)
                    else:
                        act.preload_act_table_set(name)
                    held[0] = name

            def step(i, j):
                cur, oth = j % 2, (j + 1) % 2
                count = counter(act, i)
                has = lambda d: not isinstance(i, int) or 0 <= i + d < NP
                if has(-2):
                    table(EXP_LN)
                    wait(act, "f_logit_mm", count(-1))
                    nc.scalar.activation(rt[cur][:, 0, :], FB[:, 1, 0:EXPERTS], ACT.Exp, scale=-1.0).then_inc(S["f_logit"], 1)
                if has(-1):
                    wait(act, "a_oT_mm", count(0))
                    nc.scalar.copy(oT[oth][:, :], TA[:, 0, 0:P]).then_inc(S["a_oT"], 1)
                if has(0):
                    if isinstance(i, int) and i == 0:
                        act.wait_ge(S["su_zero"], 2)
                    wait(act, "a_kv_mm", count(1))
                    for u in range(2):
                        for b in range(2):
                            q, w = slice(b * SEQ, (b + 1) * SEQ), slice(u * SEQ, (u + 1) * SEQ)
                            last = nc.scalar.activation(kb[cur][q, u, q], SS[w, 1, q], ACT.Identity, bias=C_("bk", w))
                    last.then_inc(S["a_k"], 1)
                if has(-4):
                    table(EXP_LN)
                    wait(act, "m_ld_mm", count(-3))
                    nc.scalar.activation(dd[cur][:, :], MB[:, 0, :], ACT.Exp).then_inc(S["m_d"], 1)
                if has(-2):
                    table(GELU_TANH)
                    wait(act, "f_he1_mm", count(-1))
                    nc.scalar.activation(he[cur][:, 4 * P:8 * P], FB[:, 0, :], ACT.Gelu).then_inc(S["f_ge1"], 1)
                if has(0):
                    for b in range(2):
                        q = slice(b * SEQ, (b + 1) * SEQ)
                        v = v0[cur][q, b, 0:8 * W0].rearrange("t (h w) -> t h w", w=W0)
                        s = SS[q, 1, P:2 * P].rearrange("t (h w) -> t h w", w=16)
                        nc.scalar.copy(v[:, :, 0:8], s[:, :, 0:8])
                        last = nc.scalar.copy(v[:, :, 9:17], s[:, :, 8:16])
                    last.then_inc(S["a_v"], 1)
                if has(-2):
                    table(GELU_TANH)
                    wait(act, "f_he0_mm", count(-1))
                    nc.scalar.activation(he[cur][:, 0 * P:4 * P], FB[:, 1, :], ACT.Gelu).then_inc(S["f_ge0"], 1)
                if has(-6):
                    table(GELU_TANH)
                    wait(act, "l_u1_mm", count(-5))
                    for g in range(3):
                        last = nc.scalar.activation(tgate[1][:, g, :], RB[:, 0, g * P + SEQ:g * P + 2 * SEQ], ACT.Tanh,
                                                    bias=b_half[:, g:g + 1] if g < 2 else C_("bc"), scale=0.5 if g < 2 else 1.0)
                    last.then_inc(S["l_g1"], 1)
                if has(-4):
                    wait(act, "m_cv_mm", count(-3))
                    cv = MB[:, 1, 0:4 * 96].rearrange("p (k b w) -> p k b w", k=4, b=2)
                    for h in range(2):
                        for b in range(2):
                            last = nc.scalar.copy(h17[cur][b * SEQ:(b + 1) * SEQ, :, 17 * h:17 * h + 17],
                                                  cv[h * SEQ:(h + 1) * SEQ, :, b, 16 * h:16 * h + 17])
                    last.then_inc(S["m_h17"], 1)
                if has(-3):
                    wait(act, "m_xT_mm", count(-2))
                    for u in range(2):
                        for b in range(2):
                            last = nc.scalar.copy(qs1[oth][b * SEQ:(b + 1) * SEQ, u, :], MB[u * SEQ:(u + 1) * SEQ, 0, b * SEQ:(b + 1) * SEQ])
                    last.then_inc(S["m_qs"], 1)
                    nc.scalar.copy(xT[2][oth][:, :], MB[:, 0, 0:P]).then_inc(S["m_xT"], 1)
                if has(-2):
                    table(GELU_TANH)
                    wait(act, "f_hs_mm", count(-1))
                    nc.scalar.activation(th[cur][:, :], FB[:, 0, 0:2 * P], ACT.Tanh, scale=0.5).then_inc(S["f_tanh"], 1)
                if has(-3):
                    table(EXP_LN)
                    wait(act, "m_gate_mm", count(-2))
                    nc.scalar.activation(ga[oth][:, 0, :], MB[32:40, 0, 0:P], ACT.Abs, bias=C_("fgb", slice(32, 40))).then_inc(S["m_abs"], 1)
                if has(-5):
                    wait(act, "l_xT_mm", count(-4))
                    nc.scalar.copy(xT[3][oth][:, :], RB[:, 0, 3 * P:4 * P]).then_inc(S["l_xT"], 1)
                if has(-3):
                    table(EXP_LN)
                    wait(act, "m_abs", count(-2))
                    nc.scalar.activation(ga[oth][:, 1, :], ga[oth][:, 0, :], ACT.Exp, scale=-1.0).then_inc(S["m_exp"], 1)
                if has(0):
                    table(EXP_LN)
                    wait(act, "a_sub0", count(1))
                    nc.scalar.activation(ex[cur][:, 0, :], ex[cur][:, 0, :], ACT.Exp, scale=8.0 ** -0.5).then_inc(S["a_exp0"], 1)
                if has(-3):
                    table(EXP_LN)
                    wait(act, "m_exp", count(-2))
                    nc.scalar.activation(ga[oth][:, 2, :], ga[oth][:, 1, :], ACT.Ln, bias=C_("one", slice(0, 8))).then_inc(S["m_ln"], 1)
                if has(0):
                    table(EXP_LN)
                    wait(act, "a_sub1", count(1))
                    nc.scalar.activation(ex[cur][:, 1, :], ex[cur][:, 1, :], ACT.Exp, scale=8.0 ** -0.5).then_inc(S["a_exp1"], 1)
                if has(-5):
                    dst = x3_all[:, i - 5, :] if isinstance(i, int) else x3_all[:, bass.ds(count(-5), 1), :].rearrange("p o d -> p (o d)")
                    nc.scalar.copy(dst, x3[oth][:, :]).then_inc(S["m_kept"], 1)
                    wait(act, "l_xw_mm", count(-4))
                    dst = po_all[:, i - 5, :] if isinstance(i, int) else po_all[:, bass.ds(count(-5), 1), :].rearrange("p o d -> p (o d)")
                    nc.scalar.copy(dst, RB[:, 0, 3 * P:4 * P]).then_inc(S["l_po"], 1)
                if has(0):
                    wait(act, "a_pT0_mm", count(1))
                    nc.scalar.copy(pT[cur][:, 0, :], SS[:, 0, :]).then_inc(S["a_pT0"], 1)
                    wait(act, "a_pT1_mm", count(1))
                    nc.scalar.copy(pT[cur][:, 1, :], SS[:, 1, :]).then_inc(S["a_pT1"], 1)
                if has(-5):
                    table(GELU_TANH)
                    wait(act, "l_u0_mm", count(-4))
                    for g in range(3):
                        last = nc.scalar.activation(tgate[0][:, g, :], RB[:, 0, g * P + 0:g * P + SEQ], ACT.Tanh,
                                                    bias=b_half[:, g:g + 1] if g < 2 else C_("bc"), scale=0.5 if g < 2 else 1.0)
                    last.then_inc(S["l_g0"], 1)
                if has(-1):
                    wait(act, "f_xT_mm", count(0))
                    nc.scalar.copy(xT[1][oth][:, :], FB[:, 0, 0:P]).then_inc(S["f_xT"], 1)
                if has(-2):
                    wait(act, "f_comb", count(-1))
                    nc.scalar.activation(acc[cur][:, 1, :], FB[:, 1, 0:P], ACT.Copy, scale=rt[cur][:, 9, 0:1]).then_inc(S["f_acc1"], 1)
                if has(1):
                    wait(act, "a_xT_mm", count(2))
                    nc.scalar.copy(xT[0][oth][:, :], TA[:, 0, 0:P]).then_inc(S["a_xT"], 1)
                if has(0):
                    wait(act, "a_pv1_mm", count(1))
                    pv = SS[:, :, 0:4 * 96].rearrange("p u (k b w) -> p u k b w", k=4, b=2)
                    o = o9[cur][:, :, :].rearrange("p (u k) w -> p u k w", u=2)
                    for h in range(2):
                        for b in range(2):
                            last = nc.scalar.copy(o[b * SEQ:(b + 1) * SEQ, :, :, 9 * h:9 * h + 9],
                                                  pv[h * SEQ:(h + 1) * SEQ, :, :, b, 8 * h:8 * h + 9])
                    last.then_inc(S["a_o9"], 1)
                if has(-3):
                    table(EXP_LN)
                    wait(act, "m_clamp", count(-2))
                    nc.scalar.activation(n8[oth][:, 1, :], n8[oth][:, 0, :], ACT.Exp)
                if has(1):
                    wait(act, "a_q_mm", count(2))
                    for b in range(2):
                        w, q = slice(0, SEQ), slice(b * SEQ, (b + 1) * SEQ)
                        last = nc.scalar.activation(qs[oth][q, 0, :], SS[w, 0, q], ACT.Identity, bias=C_("bq", w))
                    last.then_inc(S["a_qs0"], 1)
                    for b in range(2):
                        w, q = slice(SEQ, 2 * SEQ), slice(b * SEQ, (b + 1) * SEQ)
                        last = nc.scalar.activation(qs[oth][q, 1, :], SS[w, 0, q], ACT.Identity, bias=C_("bq", w))
                    last.then_inc(S["a_qs1"], 1)
            steps(act, step)

            for g in range(4):
                if g < 2:
                    wait(act, "t_pre", g + 1)
                else:
                    wait(act, "t_pre_pool", g - 1)
                nc.scalar.activation(pre[g][:, :, :], pre[g][:, :, :], ACT.Tanh).then_inc(S["t_tanh"], 1)

        @block.vector
        def _(dve):
            v = nc.vector

            def statistics(n, k, src):
                v.bn_stats(st[n][k][:, :], src)
                dve.drain()
                return v.bn_aggr(mv[n][k][:, :], st[n][k][:, :])

            square = lambda k, n: rc[k][:, n, :].rearrange("p (e o) -> p e o", o=8)
            eight = lambda k, n: n8[k][:, n, :].rearrange("p (k h) -> p k h", h=2)
            heads = lambda t: t.rearrange("p (h w) -> p h w", w=16)
            each = lambda t: t.unsqueeze(2).to_broadcast([P, 8, 16])

            def step(i, j):
                cur, oth = j % 2, (j + 1) % 2
                count = counter(dve, i)
                has = lambda d: not isinstance(i, int) or 0 <= i + d < NP
                if has(-6):
                    wait(dve, "m_sq", count(-5))
                    v.reduce_sum(s8[cur][:, 2, :], heads(hm[cur][:, 2, :]), AX).then_inc(S["m_var"], 1)
                if has(-4):
                    wait(dve, "f_ys_mm", count(-3))
                    v.scalar_tensor_tensor(acc[cur][:, 0, :], FB[:, 0, 0:P], tg[:, 2:3], x1[cur][:, :], ALU.mult, ALU.add).then_inc(S["f_acc0"], 1)
                if has(-6):
                    wait(dve, "m_var", count(-5))
                    v.tensor_scalar(s8[cur][:, 3, :], s8[cur][:, 2, :], 1.0 / 16, EPS_LN, ALU.mult, ALU.add).then_inc(S["m_veps"], 1)
                if has(-4):
                    wait(dve, "r_inv", count(-3))
                    v.tensor_scalar(rt[cur][:, 7, :], rt[cur][:, 6, :], r1c[cur][:, 3:4], r1c[cur][:, 2:3], ALU.mult, ALU.max).then_inc(S["r_share"], 1)
                if has(-5):
                    wait(dve, "m_run", count(-4))
                    v.scalar_tensor_tensor(nsum[oth][0:8, :], ga[oth][:, 3, :], -1.0, ga[oth][:, 4, :], ALU.mult, ALU.subtract).then_inc(S["m_neg"], 1)
                if has(-4):
                    wait(dve, "r_share", count(-3))
                    v.scalar_tensor_tensor(rt[cur][:, 9, :], rt[cur][:, 7, :], tg[:, 2:3], rt[cur][:, 5, :], ALU.mult, ALU.mult).then_inc(S["f_comb"], 1)
                if has(0):
                    loaded(dve, "ld_x", i, 0, cur, 2)
                    statistics(0, cur, x_in[cur][:, :]).then_inc(S["xn0_aggr"], 1)
                if has(-7):
                    wait(dve, "l_g0", count(-6))
                    v.scalar_tensor_tensor(pp[0][:, 0, :], tgate[0][:, 0, :], 1.0, cst[0][:, 0:SEQ], ALU.add, ALU.mult)
                    v.scalar_tensor_tensor(pp[0][:, 1, :], tgate[0][:, 1, :], 1.0, tgate[0][:, 2, :], ALU.add, ALU.mult).then_inc(S["l_q0"], 1)
                if has(-4):
                    wait(dve, "f_acc1", count(-3))
                    v.scalar_tensor_tensor(acc[cur][:, 2, :], FB[:, 1, 1 * P:2 * P], rt[cur][:, 9, 1:2], acc[cur][:, 0, :], ALU.mult, ALU.add).then_inc(S["f_acc2"], 1)
                    v.scalar_tensor_tensor(acc[cur][:, 3, :], FB[:, 1, 2 * P:3 * P], rt[cur][:, 9, 2:3], acc[cur][:, 1, :], ALU.mult, ALU.add).then_inc(S["f_acc3"], 1)
                if has(-2):
                    wait(dve, "a_o9", count(-1))
                    v.reciprocal(rden[cur][:, :].rearrange("p (k h) -> p k h", h=2), o9[cur][:, :, 8:10]).then_inc(S["a_rden"], 1)
                if has(-4):
                    wait(dve, "f_acc2", count(-3))
                    v.scalar_tensor_tensor(acc[cur][:, 4, :], FB[:, 1, 3 * P:4 * P], rt[cur][:, 9, 3:4], acc[cur][:, 2, :], ALU.mult, ALU.add).then_inc(S["f_acc4"], 1)
                if has(-5):
                    wait(dve, "m_nT_mm", count(-4))
                    v.tensor_scalar(n8[oth][:, 0, :], MB[:, 0, 0:8], 88.0, None, ALU.min).then_inc(S["m_clamp"], 1)
                if has(-4):
                    wait(dve, "f_acc3", count(-3))
                    wait(dve, "f_y1_mm", count(-3))
                    v.scalar_tensor_tensor(acc[cur][:, 5, :], FB[:, 0, 0 * P:1 * P], rt[cur][:, 9, 4:5], acc[cur][:, 3, :], ALU.mult, ALU.add).then_inc(S["f_acc5"], 1)
                    wait(dve, "f_acc4", count(-3))
                    v.scalar_tensor_tensor(acc[cur][:, 6, :], FB[:, 0, 1 * P:2 * P], rt[cur][:, 9, 5:6], acc[cur][:, 4, :], ALU.mult, ALU.add).then_inc(S["f_acc6"], 1)
                    wait(dve, "f_acc5", count(-3))
                    v.scalar_tensor_tensor(acc[cur][:, 7, :], FB[:, 0, 2 * P:3 * P], rt[cur][:, 9, 6:7], acc[cur][:, 5, :], ALU.mult, ALU.add)
                    wait(dve, "f_acc6", count(-3))
                    v.scalar_tensor_tensor(acc[cur][:, 8, :], FB[:, 0, 3 * P:4 * P], rt[cur][:, 9, 7:8], acc[cur][:, 6, :], ALU.mult, ALU.add).then_inc(S["f_acc8"], 1)
                if has(-3):
                    wait(dve, "f_logit", count(-2))
                    v.tensor_scalar(rt[oth][:, 1, :], rt[oth][:, 0, :], 1.0, None, ALU.add).then_inc(S["r_plus"], 1)
                if has(-7):
                    wait(dve, "l_q0", count(-6))
                    v.scalar_tensor_tensor(cst[1][:, 0:SEQ], pp[0][:, 0, :], 0.5, pp[0][:, 1, :], ALU.mult, ALU.add).then_inc(S["l_c0"], 1)
                if has(-6):
                    wait(dve, "m_x3", count(-5))
                    statistics(3, cur, x3[cur][:, :]).then_inc(S["xn3_aggr"], 1)
                if has(-3):
                    wait(dve, "r_plus", count(-2))
                    v.reciprocal(rt[oth][:, 2, :], rt[oth][:, 1, :]).then_inc(S["r_sig"], 1)
                    wait(dve, "r_sig", count(-2))
                    v.tensor_tensor(rt[oth][:, 3, :], rt[oth][:, 2, :], C_("rb"), ALU.add).then_inc(S["r_sel"], 1)
                if has(-4):
                    wait(dve, "f_x2", count(-3))
                    statistics(2, cur, x2[cur][:, :]).then_inc(S["xn2_aggr"], 1)
                if has(-2):
                    wait(dve, "a_proj_mm", count(-1))
                    v.scalar_tensor_tensor(x1[cur][:, :], TA[:, 0, 0:P], tg[:, 0:1], xb[cur][:, :], ALU.mult, ALU.add).then_inc(S["a_x1"], 1)
                if has(-5):
                    wait(dve, "m_d", count(-4))
                    v.scalar_tensor_tensor(cc[oth][:, :], MB[:, 1, :], 0.25, dd[oth][:, :], ALU.mult, ALU.mult).then_inc(S["m_c"], 1)
                if has(-3):
                    wait(dve, "r_sel", count(-2))
                    mine = rt[oth][:, 3, :].unsqueeze(2).to_broadcast([P, 8, 8])
                    other = rt[oth][:, 3, :].unsqueeze(1).to_broadcast([P, 8, 8])
                    v.tensor_tensor(square(oth, 0), other, mine, ALU.is_gt)
                    v.tensor_tensor(square(oth, 1), other, mine, ALU.is_ge).then_inc(S["r_cmp"], 1)
                if has(-4):
                    wait(dve, "xn2_rstd", count(-3))
                    v.tensor_scalar(xn[2][cur][:, :], x2[cur][:, :], mv[2][cur][:, 0:1], rs[2][cur][:, 0:1], ALU.subtract, ALU.mult).then_inc(S["xn2"], 1)
                if has(-3):
                    wait(dve, "r_cmp", count(-2))
                    v.tensor_tensor(rc[oth][:, 2, :], rc[oth][:, 1, :], C_("earlier"), ALU.mult).then_inc(S["r_tie"], 1)
                if has(-6):
                    wait(dve, "xn3_rstd", count(-5))
                    v.tensor_scalar(xn[3][cur][:, :], x3[cur][:, :], mv[3][cur][:, 0:1], rs[3][cur][:, 0:1], ALU.subtract, ALU.mult).then_inc(S["xn3"], 1)
                if has(0):
                    wait(dve, "xn0_rstd", count(1))
                    v.tensor_scalar(xn[0][cur][:, :], x_in[cur][:, :], mv[0][cur][:, 0:1], rs[0][cur][:, 0:1], ALU.subtract, ALU.mult).then_inc(S["xn0"], 1)
                    if isinstance(i, int) and i == 0:
                        dve.wait_ge(S["ld_a"], 32)
                        dve.wait_ge(S["su_act"], 1)
                        dve.wait_ge(S["su_pe"], 1)
                        v.tensor_tensor(pre[0][:, 0, :], RB[:, 0, 0:P], C_("bo"), ALU.add).then_inc(S["su_bias"], 1)
                        v.tensor_scalar(nw_g[:, :], C_("nw"), tg[:, 1:2], None, ALU.mult)
                        v.tensor_scalar(b_half[:, :], co[:, CO["bf"][0]:CO["bi"][1]], 0.5, None, ALU.mult)
                        dve.wait_ge(S["su_zero"], 3)
                        v.tensor_scalar(cst[0][:, 0:SEQ], C_("c0").to_broadcast([P, SEQ]), 2.0, None, ALU.mult)
                        dve.wait_ge(S["su_bias"], 1)
                        v.tensor_scalar(bo_g[:, :], pre[0][:, 0, :], tg[:, 0:1], None, ALU.mult).then_inc(S["su_dve"], 1)
                if has(-2):
                    wait(dve, "a_x1", count(-1))
                    statistics(1, cur, x1[cur][:, :]).then_inc(S["xn1_aggr"], 1)
                if has(-1):
                    wait(dve, "a_s0_mm", count(0))
                    v.tensor_reduce(mx[oth][:, 0, :], SS[:, 0, :].rearrange("p (g t) -> p g t", t=SEQ), AX, ALU.max).then_inc(S["a_max0"], 1)
                    wait(dve, "a_max0", count(0))
                    v.tensor_tensor(ex[oth][:, 0, :].rearrange("p (g t) -> p g t", t=SEQ), SS[:, 0, :].rearrange("p (g t) -> p g t", t=SEQ),
                                    mx[oth][:, 0, :].unsqueeze(2).to_broadcast([P, 8, SEQ]), ALU.subtract).then_inc(S["a_sub0"], 1)
                if has(-7):
                    wait(dve, "l_g1", count(-6))
                    v.scalar_tensor_tensor(pp[1][:, 0, :], tgate[1][:, 0, :], 1.0, cst[1][:, 0:SEQ], ALU.add, ALU.mult)
                    v.scalar_tensor_tensor(pp[1][:, 1, :], tgate[1][:, 1, :], 1.0, tgate[1][:, 2, :], ALU.add, ALU.mult).then_inc(S["l_q1"], 1)
                if has(-5):
                    wait(dve, "m_h17", count(-4))
                    v.scalar_tensor_tensor(eight(oth, 2), h17[oth][:, :, 16:18], -1.0, h17[oth][:, :, 16:18], ALU.mult, ALU.max).then_inc(S["m_norm0"], 1)
                if has(-3):
                    wait(dve, "r_tie", count(-2))
                    v.tensor_tensor(rc[oth][:, 1, :], rc[oth][:, 0, :], rc[oth][:, 2, :], ALU.max).then_inc(S["r_beat"], 1)
                if has(-5):
                    wait(dve, "m_norm0", count(-4))
                    v.tensor_tensor(n8[oth][:, 3, :], n8[oth][:, 2, :], n8[oth][:, 1, :], ALU.max).then_inc(S["m_norm1"], 1)
                if has(-3):
                    wait(dve, "r_beat", count(-2))
                    v.reduce_sum(rt[oth][:, 4, :], square(oth, 1), AX).then_inc(S["r_rank"], 1)
                if has(-5):
                    wait(dve, "m_norm1", count(-4))
                    v.tensor_scalar(n8[oth][:, 2, :], n8[oth][:, 3, :], EPS_MLSTM, None, ALU.add).then_inc(S["m_norm2"], 1)
                if has(-3):
                    if isinstance(i, int) and i == 3:
                        dve.wait_ge(S["ld_w"], 48)
                        v.tensor_tensor(gkv[:, :], wm[:, WM["gk"][0]:WM["gk"][1]], wm[:, WM["gv"][0]:WM["gv"][1]], ALU.add)
                        v.tensor_scalar(u_half[:, :], wr[:, WR["uf"][0]:WR["uy"][1]], 0.5, None, ALU.mult)
                        for k in range(2):
                            v.tensor_copy(ldl[k][:, :], C_("ldl"))
                            last = v.tensor_copy(ldr[k][:, :], C_("ldr"))
                        last.then_inc(S["su_dve"], 1)
                    wait(dve, "f_tanh", count(-2))
                    v.scalar_tensor_tensor(uh[oth][:, :], th[oth][:, :], 1.0, FB[:, 0, 0:2 * P], ALU.add, ALU.mult)
                if has(-5):
                    wait(dve, "m_norm2", count(-4))
                    v.reciprocal(n8[oth][:, 4, :], n8[oth][:, 2, :]).then_inc(S["m_norm3"], 1)
                if has(-7):
                    wait(dve, "l_q1", count(-6))
                    v.scalar_tensor_tensor(cst[0][:, 0:SEQ], pp[1][:, 0, :], 0.5, pp[1][:, 1, :], ALU.mult, ALU.add).then_inc(S["l_c1"], 1)
                if has(-1):
                    wait(dve, "a_s1_mm", count(0))
                    v.tensor_reduce(mx[oth][:, 1, :], SS[:, 1, :].rearrange("p (g t) -> p g t", t=SEQ), AX, ALU.max).then_inc(S["a_max1"], 1)
                if has(-3):
                    wait(dve, "r_rank", count(-2))
                    v.tensor_scalar(rt[oth][:, 5, :], rt[oth][:, 4, :], 2.0, None, ALU.is_lt).then_inc(S["r_top"], 1)
                if has(-5):
                    wait(dve, "m_h", count(-4))
                    v.reduce_sum(s8[oth][:, 0, :], heads(hm[oth][:, 0, :]), AX).then_inc(S["m_sum"], 1)
                if has(-1):
                    wait(dve, "a_max1", count(0))
                    v.tensor_tensor(ex[oth][:, 1, :].rearrange("p (g t) -> p g t", t=SEQ), SS[:, 1, :].rearrange("p (g t) -> p g t", t=SEQ),
                                    mx[oth][:, 1, :].unsqueeze(2).to_broadcast([P, 8, SEQ]), ALU.subtract).then_inc(S["a_sub1"], 1)
                if has(-3):
                    v.scalar_tensor_tensor(hs[oth][:, :], uh[oth][:, :], 0.5, FB[:, 0, 2 * P:4 * P], ALU.mult, ALU.mult).then_inc(S["f_hs"], 1)
                if has(-5):
                    wait(dve, "m_sum", count(-4))
                    v.scalar_tensor_tensor(heads(hm[oth][:, 1, :]), each(s8[oth][:, 0, :]), -1.0 / 16, heads(hm[oth][:, 0, :]), ALU.mult, ALU.add).then_inc(S["m_cent"], 1)
                if has(-4):
                    wait(dve, "m_abs", count(-3))
                    v.tensor_scalar(ga[cur][:, 5, :], MB[32:40, 0, 0:P], C_("fgb", slice(32, 40)), 0.0, ALU.add, ALU.min).then_inc(S["m_min"], 1)
                if has(-3):
                    wait(dve, "r_top", count(-2))
                    v.tensor_tensor(rt[oth][:, 6, :], rt[oth][:, 5, :], rt[oth][:, 2, :], ALU.mult).then_inc(S["r_best"], 1)
                if has(-2):
                    wait(dve, "xn1_rstd", count(-1))
                    v.tensor_scalar(xn[1][cur][:, :], x1[cur][:, :], mv[1][cur][:, 0:1], rs[1][cur][:, 0:1], ALU.subtract, ALU.mult).then_inc(S["xn1"], 1)
                if has(-4):
                    wait(dve, "m_ln", count(-3))
                    wait(dve, "m_min", count(-3))
                    v.tensor_tensor(ga[cur][:, 5, :], ga[cur][:, 5, :], ga[cur][:, 2, :], ALU.subtract).then_inc(S["m_logf"], 1)
                if has(-3):
                    wait(dve, "r_best", count(-2))
                    v.reduce_sum(r1c[oth][:, 0:1], rt[oth][:, 6, :], AX).then_inc(S["r_sum"], 1)
                if has(-4):
                    wait(dve, "m_logf", count(-3))
                    v.tensor_tensor_scan(ga[cur][:, 3, :], C_("keep", slice(0, 8)), ga[cur][:, 5, :], 0.0, ALU.mult, ALU.add).then_inc(S["m_cum"], 1)
                if has(-3):
                    wait(dve, "r_sum", count(-2))
                    v.tensor_scalar(r1c[oth][:, 2:3], r1c[oth][:, 0:1], 1e-9, 0.5, ALU.is_le, ALU.mult)
                    v.tensor_scalar(r1c[oth][:, 1:2], r1c[oth][:, 0:1], 1e-9, None, ALU.add).then_inc(S["r_guard"], 1)
                if has(-4):
                    wait(dve, "m_cum", count(-3))
                    v.scalar_tensor_tensor(ldl[cur][64:72, :], MB[0:8, 0, 0:P], C_("igb", slice(0, 8)), ga[cur][:, 3, :], ALU.add, ALU.subtract).then_inc(S["m_a"], 1)
                if has(-3):
                    wait(dve, "r_guard", count(-2))
                    v.reciprocal(r1c[oth][:, 3:4], r1c[oth][:, 1:2]).then_inc(S["r_inv"], 1)
                if has(-4):
                    wait(dve, "m_a", count(-3))
                    v.tensor_tensor_scan(ga[cur][:, 4, :], C_("floor", slice(64, 72)), ldl[cur][64:72, :], LOWEST, ALU.add, ALU.max).then_inc(S["m_run"], 1)
            steps(dve, step)

            wait(dve, "l_c1", NP)
            for b in range(2):
                last = v.tensor_copy(cdup[:, b * SEQ:(b + 1) * SEQ], cst[0][:, 0:SEQ])
            last.then_inc(S["t_dup"], 1)
            wait(dve, "t_rr_mm", 1)
            v.tensor_tensor(rr[:, :], TA[:, 0, 0:P], C_("by"), ALU.add).then_inc(S["t_rr"], 1)
            wait(dve, "t_rr", 1)
            wait(dve, "l_po", NP)
            wait(dve, "m_kept", NP)
            for g in range(2):
                v.tensor_tensor(pre[g][:, :, :], po_all[:, 4 * g:4 * g + 4, :], rr[:, :].unsqueeze(1).to_broadcast([P, 4, P]),
                                ALU.add).then_inc(S["t_pre"], 1)
            for g in range(4):
                wait(dve, "t_tanh", g + 1)
                v.scalar_tensor_tensor(res[g][:, :, :], pre[g][:, :, :], tg[:, 3:4], x3_all[:, 4 * g:4 * g + 4, :],
                                       ALU.mult, ALU.add).then_inc(S["t_out"], 1)

        @block.tensor
        def _(pe):
            pe.wait_ge(S["ld_c"], 16)
            pe.wait_ge(S["ld_a"], 32)
            nc.tensor.matmul(RB[:, 0, 0:P], C_("bv").to_broadcast([P, P]), A_("wo"), start=True, stop=True).then_inc(S["su_pe"], 1)
            mm = nc.tensor.matmul

            def transposed(out, src):
                return nc.tensor.transpose(out, src, ident)

            def step(i, j):
                cur, oth = j % 2, (j + 1) % 2
                count = counter(pe, i)
                has = lambda d: not isinstance(i, int) or 0 <= i + d < NP
                if has(-4):
                    wait(pe, "f_ge1", count(-3))
                    for n, w in enumerate(("sw1", "sw3")):
                        for c in range(2):
                            last = mm(FB[:, 0, (2 * n + c) * P:(2 * n + c + 1) * P], F_(w, c), xT[1][cur][:, :], start=True, stop=True)
                    last.then_inc(S["f_hs_mm"], 1)
                if has(-2):
                    wait(pe, "a_qm1", count(-1))
                    wait(pe, "a_v", count(-1))
                    for k in range(4):
                        last = mm(SS[:, 1, k * P:(k + 1) * P], qm[cur][:, 1, 2 * k:2 * k + 2, :].rearrange("p h t -> p (h t)"),
                                  kb[cur][:, 1, :], start=True, stop=True)
                    last.then_inc(S["a_s1_mm"], 1)
                if has(-7):
                    wait(pe, "l_g1", count(-7))
                    wait(pe, "xn3", count(-6))
                    transposed(RB[:, 0, 3 * P:4 * P], xn[3][oth][:, :]).then_inc(S["l_xT_mm"], 1)
                if has(-5):
                    if isinstance(i, int) and i == 5:
                        pe.wait_ge(S["su_dve"], 2)
                    loaded(pe, "ld_k", i, -5, oth, 3)
                    wait(pe, "m_xT", count(-4))
                    mm(MB[0:40, 0, 0:P], wm[:, WM["gx"][0]:WM["gx"][1]], xT[2][oth][:, :], start=True, stop=False)
                    mm(MB[0:40, 0, 0:P], gkv[:, :], ctxT_m[oth][:, :], start=False, stop=True).then_inc(S["m_gate_mm"], 1)
                if has(-4):
                    wait(pe, "f_ge0", count(-3))
                    for e in range(0, 4):
                        last = mm(FB[:, 1, (e % 4) * P:(e % 4 + 1) * P], he[cur][:, e * P:(e + 1) * P], F_("ew2", e), start=True, stop=True)
                if has(-5):
                    wait(pe, "m_qm", count(-4))
                    for u in range(2):
                        last = mm(MB[:, 1, u * 256:(u + 1) * 256], kb1[oth][:, u, :], qm1[oth][:, u, :, :].rearrange("p h t -> p (h t)"), start=True, stop=True)
                if has(-7):
                    wait(pe, "l_xT", count(-6))
                    for g, w in enumerate(("wf", "wi", "wc")):
                        mm(RB[:, 0, g * P:(g + 1) * P], R_(w), xT[3][oth][:, :], start=g == 0, stop=True, skip_group_check=True)
                    mm(RB[:, 0, 3 * P:4 * P], xT[3][oth][:, :], R_("wy"), start=False, stop=True, skip_group_check=True).then_inc(S["l_xw_mm"], 1)
                if has(-1):
                    wait(pe, "xn0", count(0))
                    transposed(TA[:, 0, 0:P], xn[0][oth][:, :]).then_inc(S["a_xT_mm"], 1)
                if has(-2):
                    wait(pe, "a_exp0", count(-1))
                    for k in range(4):
                        last = transposed(SS[:, 0, k * P:(k + 1) * P], ex[cur][:, 0, k * P:(k + 1) * P])
                    last.then_inc(S["a_pT0_mm"], 1)
                    wait(pe, "a_exp1", count(-1))
                    for k in range(4):
                        last = transposed(SS[:, 1, k * P:(k + 1) * P], ex[cur][:, 1, k * P:(k + 1) * P])
                    last.then_inc(S["a_pT1_mm"], 1)
                if has(-4):
                    wait(pe, "f_hs", count(-3))
                    for c in range(2):
                        last = mm(FB[:, 0, 0:P], hs[cur][:, c * P:(c + 1) * P], F_("sw2", c), start=c == 0, stop=c == 1)
                    last.then_inc(S["f_ys_mm"], 1)
                if has(-7):
                    wait(pe, "l_c1", count(-7))
                    wait(pe, "l_po", count(-6))
                    for g in range(3):
                        last = mm(RB[:, 0, g * P + 0:g * P + 0 + 96], u_half[:, g * P:(g + 1) * P], cst[0][:, :],
                                  start=False, stop=True, skip_group_check=True)
                    last.then_inc(S["l_u0_mm"], 1)
                if has(-2):
                    wait(pe, "a_pT0", count(-1))
                    for k in range(4):
                        c = k * W0
                        last = mm(SS[:, 0, k * 96:(k + 1) * 96].rearrange("p (b w) -> p b w", b=2), pT[cur][:, 0, k * P:(k + 1) * P],
                                  v0[cur][:, :, c:c + WIN], start=True, stop=True)
                if has(-3):
                    if isinstance(i, int) and i == 3:
                        pe.wait_ge(S["ld_w"], 48)
                    wait(pe, "f_acc0", count(-3))
                    wait(pe, "xn1", count(-2))
                    transposed(FB[:, 0, 0:P], xn[1][oth][:, :]).then_inc(S["f_xT_mm"], 1)
                if has(-2):
                    wait(pe, "a_pT1", count(-1))
                    for k in range(4):
                        c = (4 + k) * W0
                        last = mm(SS[:, 1, k * 96:(k + 1) * 96].rearrange("p (b w) -> p b w", b=2), pT[cur][:, 1, k * P:(k + 1) * P],
                                  v0[cur][:, :, c:c + WIN], start=True, stop=True)
                    last.then_inc(S["a_pv1_mm"], 1)
                if has(-5):
                    wait(pe, "m_neg", count(-4))
                    transposed(MB[:, 0, 0:P], nsum[oth][:, :]).then_inc(S["m_nT_mm"], 1)
                if has(-4):
                    wait(pe, "f_xT", count(-2))
                    for e in range(4, 8):
                        last = mm(FB[:, 0, (e % 4) * P:(e % 4 + 1) * P], he[cur][:, e * P:(e + 1) * P], F_("ew2", e), start=True, stop=True)
                    last.then_inc(S["f_y1_mm"], 1)
                if has(-1):
                    wait(pe, "a_o9", count(-1))
                    wait(pe, "a_xT", count(0))
                    mm(SS[:, 0, 0:P], A_("wq"), xT[0][oth][:, :], start=True, stop=True).then_inc(S["a_q_mm"], 1)
                    mm(SS[:, 1, 0:P], A_("wk"), ctxT_a[oth][:, :], start=True, stop=True)
                    mm(SS[:, 1, P:2 * P], ctxT_a[oth][:, :], A_("wv"), start=True, stop=True).then_inc(S["a_kv_mm"], 1)
                if has(-3):
                    wait(pe, "f_acc4", count(-3))
                    mm(FB[:, 1, 0:96], xT[1][oth][:, :], F_("router", w=96), start=True, stop=True).then_inc(S["f_logit_mm"], 1)
                if has(-2):
                    wait(pe, "a_on", count(-1))
                    transposed(TA[:, 0, 0:P], on_buf[cur][:, :]).then_inc(S["a_oT_mm"], 1)
                if has(-5):
                    wait(pe, "m_clamp", count(-4))
                    loaded(pe, "rows", i, -5, oth, 2)
                    mm(MB[:, 0, :], ldl[oth][0:98, :], ldr[oth][0:98, :], start=True, stop=True).then_inc(S["m_ld_mm"], 1)
                if has(-3):
                    wait(pe, "f_acc8", count(-3))
                    for e in range(4):
                        last = mm(FB[:, 0, e * P:(e + 1) * P], F_("ew1", 4 + e), xT[1][oth][:, :], start=True, stop=True)
                    last.then_inc(S["f_he1_mm"], 1)
                if has(-2):
                    wait(pe, "a_oT", count(-1))
                    mm(TA[:, 0, 0:P], oT[cur][:, :], A_("wo"), start=True, stop=True).then_inc(S["a_proj_mm"], 1)
                if has(-3):
                    wait(pe, "f_logit", count(-2))
                    for e in range(4):
                        last = mm(FB[:, 1, e * P:(e + 1) * P], F_("ew1", e), xT[1][oth][:, :], start=True, stop=True)
                    last.then_inc(S["f_he0_mm"], 1)
                if has(-1):
                    wait(pe, "a_k", count(0))
                    wait(pe, "a_qm0", count(0))
                    for k in range(4):
                        last = mm(SS[:, 0, k * P:(k + 1) * P], qm[oth][:, 0, 2 * k:2 * k + 2, :].rearrange("p h t -> p (h t)"),
                                  kb[oth][:, 0, :], start=True, stop=True)
                    last.then_inc(S["a_s0_mm"], 1)
                if has(-7):
                    wait(pe, "l_c0", count(-6))
                    for g in range(3):
                        last = mm(RB[:, 0, g * P + SEQ:g * P + SEQ + 96], u_half[:, g * P:(g + 1) * P], cst[1][:, :],
                                  start=False, stop=True, skip_group_check=True)
                    last.then_inc(S["l_u1_mm"], 1)
                if has(-5):
                    loaded(pe, "ld_v", i, -5, oth, 2)
                    wait(pe, "m_c", count(-4))
                    for k in range(4):
                        last = mm(MB[:, 1, k * 96:(k + 1) * 96].rearrange("p (b w) -> p b w", b=2), cc[oth][:, k * P:(k + 1) * P],
                                  v1[oth][:, :, k * W1:k * W1 + WIN], start=True, stop=True)
                    last.then_inc(S["m_cv_mm"], 1)
                if has(-4):
                    wait(pe, "xn2", count(-3))
                    transposed(MB[:, 0, 0:P], xn[2][cur][:, :]).then_inc(S["m_xT_mm"], 1)
            steps(pe, step)
            pe.wait_ge(S["t_dup"], 1)
            mm(TA[:, 0, 0:P], cdup[:, :], u_half[:, 3 * P:4 * P], start=True, stop=True).then_inc(S["t_rr_mm"], 1)


def constants():
    ident = np.eye(P, dtype=np.float32)
    rows = np.arange(P)
    head0 = (rows[:, None] % SEQ // 8 == np.arange(8)).astype(np.float32)
    head1 = (rows[:, None] % SEQ // 16 == np.arange(4)).astype(np.float32)
    earlier = np.tile((np.arange(8)[None, :] < np.arange(8)[:, None]).astype(np.float32).reshape(1, 64), (P, 1))
    keep = np.ones((P, P), np.float32)
    keep[:, SEQ] = 0
    floor = np.zeros((P, P), np.float32)
    floor[:, SEQ] = LOWEST
    ldl = np.zeros((P, P), np.float32)
    ldl[0:SEQ] = np.tile(np.eye(SEQ, dtype=np.float32), (1, 2))
    ldl[96, 0:SEQ] = -1
    ldl[97, SEQ:P] = -1
    ldr = np.zeros((P, 8, SEQ), np.float32)
    t = np.arange(SEQ)
    ldr[0:SEQ] = np.where(t[:, None] > t[None, :], BIG, 0.0)[:, None, :]
    ldr[64 + np.arange(8), np.arange(8)] = 1
    return {"one": np.ones((P, 1), np.float32), "eps": np.full((P, 1), EPS_LN, np.float32), "mhalf": np.full((P, 8), -0.5, np.float32), "head0": head0, "head1": head1,
            "earlier": earlier, "ident": ident, "keep": keep, "floor": floor, "ldl": ldl, "ldr": ldr.reshape(P, 512)}


def kernel(**inputs):
    import concourse.bacc as bacc
    from concourse.bass_utils import run_bass_kernel_spmd as run

    a = {k: np.asarray(v) for k, v in inputs.items()}
    col = lambda n: a[n].reshape(P, 1)
    row = lambda n: np.broadcast_to(a[n].reshape(1, -1), (P, a[n].size))

    def pack(parts, names):
        return np.ascontiguousarray(np.concatenate([parts[n] for n, _ in names], axis=1))

    def at_rows(v, *starts):
        out = np.zeros((P, 1), np.float32)
        for s in starts:
            out[s:s + 8, 0] = v
        return out

    router = np.zeros((P, 96), np.float32)
    router[:, 0:EXPERTS] = a["L0_ffn_router_w"].T
    flat = lambda n: a[n].transpose(1, 0, 2).reshape(P, EXPERTS * P)
    gates = {}
    for k, n in enumerate(("gx", "gk", "gv")):
        gates[n] = np.zeros((P, 40), np.float32)
        gates[n][:, 0:8] = a["L1_xattn_igate_w"][:, k * P:(k + 1) * P].T
        gates[n][:, 32:40] = a["L1_xattn_fgate_w"][:, k * P:(k + 1) * P].T
    x = np.ascontiguousarray(a["x"].reshape(NP * P, P))
    ctx = np.ascontiguousarray(a["ctx_1024"].reshape(NP * P, P))
    values = np.ones((NP * P, 4, W1), np.float32)
    values[:, :, 0:16], values[:, :, 17:W1] = ctx.reshape(NP * P, 4, 32)[:, :, 0:16], ctx.reshape(NP * P, 4, 32)[:, :, 16:32]
    values = values.reshape(NP * P, 4 * W1)
    arrays = {
        "x": x, "ctxT": np.ascontiguousarray(ctx.T), "ctxv": values,
        "wa": pack({k: a[f"L0_xattn_{k}"].T for k in ("wq", "wk", "wv", "wo")}, WEIGHTS_A),
        "wf": pack({"router": router, "sw1": a["L0_ffn_sw1"], "sw3": a["L0_ffn_sw3"],
                    "sw2": a["L0_ffn_sw2"].reshape(2, P, P).transpose(1, 0, 2).reshape(P, 2 * P),
                    "ew1": flat("L0_ffn_ew1"), "ew2": flat("L0_ffn_ew2")}, WEIGHTS_F),
        "wm": pack(gates, WEIGHTS_M),
        "wr": pack({"wf": a["L1_ffn_wf"].T, "wi": a["L1_ffn_wi"].T, "wc": a["L1_ffn_wc"].T, "wy": a["L1_ffn_wo"].T,
                    "uf": a["L1_ffn_uf"].T, "ui": a["L1_ffn_ui"].T, "uc": a["L1_ffn_uc"].T, "uy": a["L1_ffn_uo"].T}, WEIGHTS_R),
        "co": pack({"bq": col("L0_xattn_bq"), "bk": col("L0_xattn_bk"), "bv": col("L0_xattn_bv"),
                    "bf": col("L1_ffn_bf"), "bi": col("L1_ffn_bi"), "bc": col("L1_ffn_bc"), "c0": col("L1_ffn_in_c"),
                    "igb": at_rows(a["L1_xattn_igate_b"], 0), "fgb": at_rows(a["L1_xattn_fgate_b"], 0, 32),
                    "gates": np.concatenate([row("g_xattn"), row("g_ffn")], axis=1), "rb": row("L0_ffn_router_bias"),
                    "bo": row("L0_xattn_bo"), "nw": row("L1_xattn_norm_w"), "by": row("L1_ffn_bo"), **constants()}, COLUMNS),
    }
    nc = bacc.Bacc("TRN2", target_bir_lowering=False, num_devices=1)
    args = [nc.dram_tensor(f"in_{n}", v.shape, F32, kind="ExternalInput").ap() for n, v in arrays.items()]
    out = nc.dram_tensor("out", [NP * P, P], F32, kind="ExternalOutput").ap()
    build(nc, *args, out)
    r = run(nc, [{f"in_{n}": v for n, v in arrays.items()}], core_ids=[0])
    return r.results[0]["out"].reshape(NB, SEQ, P)
```
